# Optimizing a Trainium2 kernel written in Bass

```python
import numpy as np
import jax
import jax.numpy as jnp

def _softmax(x, axis=-1):
    return jax.nn.softmax(x, axis=axis)

def _gelu(x):
    return jax.nn.gelu(x, approximate=True)

def _silu(x):
    return jax.nn.silu(x)

def _sigmoid(x):
    return jax.nn.sigmoid(x)

def _layernorm(x, axis=-1, eps=1e-05):
    m = jnp.mean(x, axis=axis, keepdims=True)
    v = jnp.var(x, axis=axis, keepdims=True)
    return (x - m) / jnp.sqrt(v + eps)

def _scatter_add(tgt, idx, src, axis=0):
    return tgt.at[idx].add(src)

def _segment_sum(src, seg, n):
    return jax.ops.segment_sum(src, seg, n)
kernel_name = 'mk_cond_resid_d2_seqx_r2_b2dd2d'

def setup_inputs(seed: int=0):
    np.random.seed(seed)
    _w = jnp.asarray

    def _rec_inputs():
        import jax
        import jax.numpy as jnp
        _rk = jax.random.key(seed)
        x = -0.0002928 + 1 * jax.random.normal(jax.random.fold_in(_rk, 1), (2, 2048, 512), jnp.float32)
        _lenS = 2048 - jax.random.randint(jax.random.fold_in(_rk, 7), (2,), 0, max(1, 2048 // 4) + 1, jnp.int32)
        _lenS2 = 2048 - jax.random.randint(jax.random.fold_in(_rk, 8), (2,), 0, max(1, 2048 // 4) + 1, jnp.int32)
        cond_1024 = 0.000887014 + 1.03683 * jax.random.normal(jax.random.fold_in(_rk, 11), (2, 512), jnp.float32)
        return (x, cond_1024)
    x, cond_1024 = _rec_inputs()

    def _L0_cond_setup():
        import jax, jax.numpy as jnp
        import numpy as np
        TOP_K = 2
        N_EXPERTS = 8
        N_SHARED = 1
        EPS = 1e-09
        key = jax.random.key(seed)
        ks = jax.random.split(key, 10)
        B, T, d = (2, 1024, 512)
        h_s, h_r, E = (1024, 256, N_EXPERTS)
        return {'x': jax.random.normal(ks[0], (B, T, d), jnp.float32), 't_emb': jax.random.normal(ks[1], (B, d), jnp.float32), 'router_w': jax.random.normal(ks[2], (E, d), jnp.float32) * 0.01, 'router_t_w': jax.random.normal(ks[3], (E, d), jnp.float32) * 0.01, 'router_bias': jnp.zeros((E,), jnp.float32), 'sw1': jax.random.normal(ks[4], (h_s, d), jnp.float32) * 0.02, 'sw3': jax.random.normal(ks[5], (h_s, d), jnp.float32) * 0.02, 'sw2': jax.random.normal(ks[6], (d, h_s), jnp.float32) * 0.02, 'rw1': jax.random.normal(ks[7], (E, h_r, d), jnp.float32) * 0.02, 'rw2': jax.random.normal(ks[8], (E, d, h_r), jnp.float32) * 0.02}
    _L0_cond_all = _L0_cond_setup()
    _L0_cond_in = {k: v for k, v in _L0_cond_all.items() if k in ('router_w', 'router_t_w', 'router_bias', 'sw1', 'sw3', 'sw2', 'rw1', 'rw2')}
    del _L0_cond_all

    def _L1_cond_setup():
        import jax, jax.numpy as jnp
        import numpy as np
        B, T, D_IN, V_IN, E = (64, 128, 512, 512, 512)
        key = jax.random.key(seed)
        ks = jax.random.split(key, 16)
        s = 0.01
        return {'video': jax.random.normal(ks[0], (B, V_IN), jnp.float32), 'seq': jax.random.normal(ks[1], (B, T, D_IN), jnp.float32), 'W_z': jax.random.normal(ks[2], (D_IN, E), jnp.float32) * s, 'U_z': jax.random.normal(ks[3], (E, E), jnp.float32) * s, 'C_z': jax.random.normal(ks[4], (V_IN, E), jnp.float32) * s, 'b_z': jnp.zeros((E,), jnp.float32), 'W_r': jax.random.normal(ks[5], (D_IN, E), jnp.float32) * s, 'U_r': jax.random.normal(ks[6], (E, E), jnp.float32) * s, 'C_r': jax.random.normal(ks[7], (V_IN, E), jnp.float32) * s, 'b_r': jnp.zeros((E,), jnp.float32), 'W': jax.random.normal(ks[8], (D_IN, E), jnp.float32) * s, 'U': jax.random.normal(ks[9], (E, E), jnp.float32) * s, 'C': jax.random.normal(ks[10], (V_IN, E), jnp.float32) * s, 'b': jnp.zeros((E,), jnp.float32)}
    _L1_cond_all = _L1_cond_setup()
    _L1_cond_in = {k: v for k, v in _L1_cond_all.items() if k in ('W_z', 'U_z', 'C_z', 'b_z', 'W_r', 'U_r', 'C_r', 'b_r', 'W', 'U', 'C', 'b')}
    del _L1_cond_all
    return {'x': x, 'cond_1024': cond_1024, 'L0_cond_router_w': _L0_cond_in['router_w'], 'L0_cond_router_t_w': _L0_cond_in['router_t_w'], 'L0_cond_router_bias': _L0_cond_in['router_bias'], 'L0_cond_sw1': _L0_cond_in['sw1'], 'L0_cond_sw3': _L0_cond_in['sw3'], 'L0_cond_sw2': _L0_cond_in['sw2'], 'L0_cond_rw1': _L0_cond_in['rw1'], 'L0_cond_rw2': _L0_cond_in['rw2'], 'L1_cond_W_z': _L1_cond_in['W_z'], 'L1_cond_U_z': _L1_cond_in['U_z'], 'L1_cond_C_z': _L1_cond_in['C_z'], 'L1_cond_b_z': _L1_cond_in['b_z'], 'L1_cond_W_r': _L1_cond_in['W_r'], 'L1_cond_U_r': _L1_cond_in['U_r'], 'L1_cond_C_r': _L1_cond_in['C_r'], 'L1_cond_b_r': _L1_cond_in['b_r'], 'L1_cond_W': _L1_cond_in['W'], 'L1_cond_U': _L1_cond_in['U'], 'L1_cond_C': _L1_cond_in['C'], 'L1_cond_b': _L1_cond_in['b']}

def reference(x, cond_1024, L0_cond_router_w, L0_cond_router_t_w, L0_cond_router_bias, L0_cond_sw1, L0_cond_sw3, L0_cond_sw2, L0_cond_rw1, L0_cond_rw2, L1_cond_W_z, L1_cond_U_z, L1_cond_C_z, L1_cond_b_z, L1_cond_W_r, L1_cond_U_r, L1_cond_C_r, L1_cond_b_r, L1_cond_W, L1_cond_U, L1_cond_C, L1_cond_b):
    import jax
    import jax.numpy as jnp

    def _L0_cond_ref(x, t_emb, router_w, router_t_w, router_bias, sw1, sw3, sw2, rw1, rw2):
        import jax, jax.numpy as jnp
        import numpy as np
        TOP_K = 2
        N_EXPERTS = 8
        N_SHARED = 1
        EPS = 1e-09
        B, T, C = x.shape
        N = B * T
        x_flat = x.reshape(N, C)
        shared_out = jnp.einsum('nh,dh->nd', jax.nn.silu(x_flat @ sw1.T) * (x_flat @ sw3.T), sw2)
        t_bias = t_emb @ router_t_w.T
        t_bias_flat = jnp.broadcast_to(t_bias[:, None, :], (B, T, N_EXPERTS)).reshape(N, N_EXPERTS)
        s = jax.nn.sigmoid((x_flat @ router_w.T + t_bias_flat).astype(jnp.float32))
        sel_scores = s + router_bias
        _, topk_idx = jax.lax.top_k(sel_scores, TOP_K)
        s_sel = jnp.take_along_axis(s, topk_idx, axis=1)
        denom = jnp.sum(s_sel, axis=1, keepdims=True)
        gates = jnp.where(denom > EPS, s_sel / (denom + EPS), 1.0 / TOP_K).astype(x.dtype)
        combine = jnp.sum(gates[:, :, None] * jax.nn.one_hot(topk_idx, N_EXPERTS, dtype=x.dtype), axis=1)
        H = jax.nn.gelu(jnp.einsum('nd,ehd->enh', x_flat, rw1), approximate=False)
        O = jnp.einsum('enh,edh->end', H, rw2)
        routed_out = jnp.einsum('end,ne->nd', O, combine)
        out = (shared_out + routed_out) / (N_SHARED + TOP_K)
        return out.reshape(B, T, C)

    def _L1_cond_ref(video, seq, W_z, U_z, C_z, b_z, W_r, U_r, C_r, b_r, W, U, C, b):
        import jax, jax.numpy as jnp
        import numpy as np
        B, T, D_IN, V_IN, E = (64, 128, 512, 512, 512)
        vz = video @ C_z + b_z
        vr = video @ C_r + b_r
        vh = video @ C + b
        xz = jnp.einsum('btd,de->bte', seq, W_z)
        xr = jnp.einsum('btd,de->bte', seq, W_r)
        xh = jnp.einsum('btd,de->bte', seq, W)

        def step(h, xs):
            xzt, xrt, xht = xs
            z = jax.nn.sigmoid(xzt + h @ U_z + vz)
            r = jax.nn.sigmoid(xrt + h @ U_r + vr)
            hh = jnp.tanh(xht + r * h @ U + vh)
            h_new = (1.0 - z) * h + z * hh
            return (h_new, h_new)
        h0 = jnp.zeros((seq.shape[0], U.shape[0]), seq.dtype)
        xs = (jnp.swapaxes(xz, 0, 1), jnp.swapaxes(xr, 0, 1), jnp.swapaxes(xh, 0, 1))
        _, out_t = jax.lax.scan(step, h0, xs)
        return jnp.swapaxes(out_t, 0, 1)
    x = x + _L0_cond_ref(x, cond_1024, L0_cond_router_w, L0_cond_router_t_w, L0_cond_router_bias, L0_cond_sw1, L0_cond_sw3, L0_cond_sw2, L0_cond_rw1, L0_cond_rw2)
    x = x + _L1_cond_ref(cond_1024, x, L1_cond_W_z, L1_cond_U_z, L1_cond_C_z, L1_cond_b_z, L1_cond_W_r, L1_cond_U_r, L1_cond_C_r, L1_cond_b_r, L1_cond_W, L1_cond_U, L1_cond_C, L1_cond_b)
    return x

_drawn_inputs = setup_inputs


def setup_inputs(seed=0):
    import zlib

    import numpy as np

    out = dict(_drawn_inputs(seed))
    spreads = {'L0_cond_router_bias': (0.0, 0.429),
     'L1_cond_b_z': (0.0, 0.8),
     'L1_cond_b_r': (0.0, 0.8),
     'L1_cond_b': (0.0, 0.1)}
    factors = {'L0_cond_router_w': 5.766,
     'L0_cond_router_t_w': 6.301,
     'L0_cond_rw1': 3.116,
     'L0_cond_rw2': 2.973,
     'L1_cond_W_z': 3.81,
     'L1_cond_U_z': 8.0,
     'L1_cond_C_z': 4.733,
     'L1_cond_W_r': 8.0,
     'L1_cond_U_r': 8.0,
     'L1_cond_C_r': 8.0}
    for name, (base, spread) in spreads.items():
        noise = np.random.default_rng([zlib.crc32(name.encode()), seed]).standard_normal(out[name].shape)
        drawn = base * np.exp(spread * noise) if base else spread * noise
        out[name] = jnp.asarray(drawn.astype(out[name].dtype))
    for name, factor in factors.items():
        out[name] = (out[name] * factor).astype(out[name].dtype)
    return out
```

```python
from contextlib import ExitStack

import concourse.bass as bass
from concourse import mybir

ALU = mybir.AluOpType
ACT = mybir.ActivationFunctionType
AX = mybir.AxisListType
F32 = mybir.dt.float32
F32R = mybir.dt.float32r
F16 = mybir.dt.float16
BF16 = mybir.dt.bfloat16
I32 = mybir.dt.int32

P = 128
D = 512
KD = D // P
B = 2
T = 2048
TILE = 512
TILES = B * T // TILE
TT = TILE // P
BLOCKS = B * T // P
E = 8
HS = 1024
HR = 256
TOP_K = 2
EPS = 1e-9
SCALE = 1.0 / 3.0
PARTS = 3
NONE = -3.0e38

CH = 128
CHUNKS = T // CH
PER_TILE = TILE // CH
TURNS = 8
FINE = 5
LOW = 2048.0
R, Z, C = range(3)
CHECKS = 4
BOUNDS = [KD * CH * x * x for x in (1e-6, 1e-3, 1e-3, 1e-3)]


class Shared:
    pass


def constants(nc, ctx, g):
    sb = lambda n, s, d: ctx.enter_context(nc.sbuf_tensor(n, s, d))
    g.ident = sb("ident", [P, P], F32)
    g.ident_b = sb("ident_b", [P, P], BF16)
    g.ones = sb("ones", [P, P], F32)
    g.select = sb("select", [PARTS * E, E, P], BF16)
    g.gates_t = sb("gates_t", [PARTS * E, B * T], BF16)
    g.cond_t = sb("cond_t", [P, KD, B], F32)
    g.pick_f = sb("pick_f", [B, B, P], F32)
    g.made = ctx.enter_context(nc.semaphore("constants_made"))
    with nc.Block() as block:
        @block.gpsimd
        def _(pool):
            nc.gpsimd.memset(g.ident[:], 0.0).then_inc(g.made, 1)
            nc.gpsimd.memset(g.ident_b[:], 0.0).then_inc(g.made, 1)
            nc.gpsimd.memset(g.select[:], 0.0).then_inc(g.made, 1)
            nc.gpsimd.memset(g.ones[:], 1.0).then_inc(g.made, 1)
            nc.gpsimd.memset(g.pick_f[:], 0.0).then_inc(g.made, 1)
            pool.wait_ge(g.made, 5)
            nc.gpsimd.affine_select(out=g.pick_f[:], in_=g.pick_f[:], compare_op=ALU.not_equal, fill=1.0, base=0,
                                    pattern=[[-1, B], [0, P]], channel_multiplier=1).then_inc(g.made, 1)
            for t in (g.ident, g.ident_b):
                nc.gpsimd.affine_select(out=t[:], in_=t[:], compare_op=ALU.not_equal, fill=1.0, base=0,
                                        pattern=[[-1, P]], channel_multiplier=1).then_inc(g.made, 1)
            for q in range(PARTS):
                nc.gpsimd.affine_select(out=g.select[:], in_=g.select[:], compare_op=ALU.not_equal, fill=1.0,
                                        base=-q * E, pattern=[[-1, E], [0, P]], channel_multiplier=1
                                        ).then_inc(g.made, 1)
                pool.wait_ge(g.made, 9 + q)


def tokens(nc, g, x, cond, router_w, router_t_w, router_bias):
    with ExitStack() as ctx:
        sb = lambda n, s, d=F32: ctx.enter_context(nc.sbuf_tensor(n, s, d))
        ps = lambda n, s, d=F32: ctx.enter_context(nc.psum_tensor(n, s, d))
        sem = lambda n: ctx.enter_context(nc.semaphore(n))
        x_rows = [sb(f"x_rows{q}", [P, TT, D]) for q in range(2)]
        x_cols = [sb(f"x_cols{q}", [P, KD, TILE]) for q in range(2)]
        small = sb("small_rows", [E, 3, D])
        router_t = sb("router_t", [P, KD, 2, E])
        t_bias = sb("t_bias", [1, B * E])
        bias = sb("bias_all", [P, 1, E])
        score, chosen, replaced, mask, kept, gate, rest, top, find = [sb(n, [P, BLOCKS, E]) for n in (
            "score", "chosen", "replaced", "mask", "kept", "gate", "rest", "top", "find")]
        total, good, inverse, half = [sb(n, [P, BLOCKS, 1]) for n in ("total", "good", "inverse", "half")]
        parts = sb("parts", [P, BLOCKS, PARTS, E], BF16)
        turned = [ps(f"turned{a}", [P, KD, P]) for a in range(TT)]
        logits = ps("logits", [P, BLOCKS * E])
        small_t = ps("small_t", [P, 3, KD, E])
        gates_p = [ps(f"gates_p{q}", [PARTS * E, 8 * P], BF16) for q in range(2)]

        x_loaded = [sem(f"x_loaded{q}") for q in range(2)]
        x_stored = [sem(f"x_stored{q}") for q in range(2)]
        small_loaded, x_turned = sem("small_loaded"), sem("x_turned")
        cols_v, cols_a = sem("cols_v"), sem("cols_a")
        small_turned, small_kept = sem("small_turned"), sem("small_kept")
        t_bias_done, t_bias_kept = sem("t_bias_done"), sem("t_bias_kept")
        logits_done, scored, routed = sem("logits_done"), sem("scored"), sem("routed")
        gates_turned, gates_kept, step = sem("gates_turned"), sem("gates_kept"), sem("route_step")
        x_v = x.rearrange("b (i a p) d -> (b i) p a d", a=TT, p=P)
        half_tiles = TILES // 2

        with nc.Block() as block:
            @block.sync
            def _(sp):
                sp.dma_start(small[0:E, 0, :], router_w).then_inc(small_loaded, 16)
                sp.dma_start(small[0:E, 1, :], router_t_w).then_inc(small_loaded, 16)
                sp.dma_start(small[0:B, 2, :], cond).then_inc(small_loaded, 16)
                sp.dma_start(bias[:, 0, :], router_bias.partition_broadcast(P)).then_inc(small_loaded, 16)
                for q in range(2):
                    sp.dma_start(x_rows[q][:], x_v[q]).then_inc(x_loaded[q], 16)
                    sp.sem_inc(x_stored[q], 16)
                with sp.Fori(0, half_tiles) as pair:
                    for q in range(2):
                        sp.wait_ge(cols_v, 2 * (2 * pair + q) + 4)
                        sp.wait_ge(cols_a, 2 * (2 * pair + q) + 4)
                        sp.dma_start(g.x_t[2 * pair + q], x_cols[q][:]).then_inc(x_stored[q], 16)
                        sp.dma_start(x_rows[q][:], x_v[(2 * pair + (2 + q)) % TILES]).then_inc(x_loaded[q], 16)
                for q in range(2):
                    sp.wait_ge(x_stored[q], 16 * (half_tiles + 1))
                    sp.wait_ge(x_loaded[q], 16 * (half_tiles + 1))

            @block.tensor
            def _(pe):
                pe.wait_ge(small_loaded, 64)
                for w, n in ((0, E), (1, E), (2, B)):
                    for k in range(KD):
                        last = nc.tensor.transpose(small_t[:, w, k, 0:n], small[0:n, w, k * P:(k + 1) * P],
                                                   g.ident[0:n, 0:n])
                last.then_inc(small_turned, 1)
                pe.wait_ge(small_kept, 3)
                for b in range(B):
                    for k in range(KD):
                        last = nc.tensor.matmul(logits[0:1, b * E:(b + 1) * E], g.cond_t[:, k, b:b + 1],
                                                router_t[:, k, 1, :], start=k == 0, stop=k == KD - 1)
                last.then_inc(t_bias_done, 1)
                pe.wait_ge(t_bias_kept, 1)
                with pe.Fori(0, B) as b:
                    with pe.Fori(0, half_tiles // B) as pair:
                        for q in range(2):
                            tile = b * (TILES // B) + 2 * pair + q
                            pe.wait_ge(x_loaded[q], 16 * (b * (half_tiles // B) + pair + 1))
                            for a in range(TT):
                                if a == 0:
                                    pe.wait_ge(cols_v, 2 * tile + 2)
                                if a == 2:
                                    pe.wait_ge(cols_a, 2 * tile + 2)
                                for k in range(KD):
                                    last = nc.tensor.transpose(turned[a][:, k, :], x_rows[q][:, a, k * P:(k + 1) * P],
                                                               g.ident[:])
                                last.then_inc(x_turned, 1)
                            pe.wait_ge(cols_v, 2 * tile + 4)
                            pe.wait_ge(cols_a, 2 * tile + 4)
                            for a in range(TT):
                                to = logits[:, bass.ds((tile * TT + a) * E, E)]
                                for k in range(KD):
                                    nc.tensor.matmul(to, x_cols[q][:, k, a * P:(a + 1) * P], router_t[:, k, 0, :],
                                                     start=k == 0, stop=False)
                                nc.tensor.matmul(to, g.ones[0:1, :], t_bias[0:1, bass.ds(b * E, E)],
                                                 start=False, stop=True).then_inc(logits_done, 1)
                pe.wait_ge(routed, 1)
                for i in range(BLOCKS // 8):
                    if i >= 2:
                        pe.wait_ge(gates_kept, i - 1)
                    for a in range(8):
                        last = nc.tensor.transpose(
                            gates_p[i % 2][:, a * P:(a + 1) * P],
                            parts[:, 8 * i + a, :, :].rearrange("p q e -> p (q e)"), g.ident_b[:])
                    last.then_inc(gates_turned, 1)

            @block.scalar
            def _(act):
                act.sem_inc(cols_a, 2)
                with act.Fori(0, half_tiles) as pair:
                    for q in range(2):
                        act.wait_ge(x_stored[q], 16 * (pair + 1))
                        for a in (2, 3):
                            act.wait_ge(x_turned, TT * (2 * pair + q) + a + 1)
                            nc.scalar.activation(x_cols[q][:, :, a * P:(a + 1) * P], turned[a][:], ACT.Copy
                                                 ).then_inc(cols_a, 1)
                act.wait_ge(logits_done, BLOCKS)
                nc.scalar.activation(score[:], logits[:, :].rearrange("p (i e) -> p i e", e=E), ACT.Sigmoid
                                     ).then_inc(scored, 1)

            @block.vector
            def _(dve):
                dve.sem_inc(cols_v, 2)
                dve.wait_ge(small_turned, 1)
                for w in range(2):
                    nc.vector.tensor_copy(router_t[:, :, w, :], small_t[:, w, :, :]).then_inc(small_kept, 1)
                nc.vector.tensor_copy(g.cond_t[:], small_t[:, 2, :, 0:B]).then_inc(small_kept, 1)
                dve.wait_ge(t_bias_done, 1)
                nc.vector.tensor_copy(t_bias[:], logits[0:1, 0:B * E]).then_inc(t_bias_kept, 1)
                with dve.Fori(0, half_tiles) as pair:
                    for q in range(2):
                        dve.wait_ge(x_stored[q], 16 * (pair + 1))
                        for a in (0, 1):
                            dve.wait_ge(x_turned, TT * (2 * pair + q) + a + 1)
                            nc.vector.tensor_copy(x_cols[q][:, :, a * P:(a + 1) * P], turned[a][:]
                                                  ).then_inc(cols_v, 1)

                count = [0]

                def in_turn(ins):
                    count[0] += 1
                    ins.then_inc(step, 1)
                    dve.wait_ge(step, count[0])

                wide = lambda t: t[:, :, :].to_broadcast([P, BLOCKS, E])
                dve.wait_ge(scored, 1)
                in_turn(nc.vector.tensor_tensor(chosen[:], score[:], bias[:].to_broadcast([P, BLOCKS, E]), ALU.add))
                for i in range(BLOCKS - 1):
                    nc.vector.max(top[:, i, :], chosen[:, i, :])
                in_turn(nc.vector.max(top[:, BLOCKS - 1, :], chosen[:, BLOCKS - 1, :]))
                in_turn(nc.vector.memset(find[:], NONE))
                in_turn(nc.vector.tensor_copy(find[:, :, 0:TOP_K], top[:, :, 0:TOP_K]))
                for i in range(BLOCKS - 1):
                    nc.vector.match_replace(replaced[:, i, :], find[:, i, :], chosen[:, i, :], NONE)
                in_turn(nc.vector.match_replace(replaced[:, BLOCKS - 1, :], find[:, BLOCKS - 1, :],
                                                chosen[:, BLOCKS - 1, :], NONE))
                in_turn(nc.vector.tensor_tensor(mask[:], replaced[:], chosen[:], ALU.not_equal))
                in_turn(nc.vector.tensor_tensor(kept[:], mask[:], score[:], ALU.mult))
                in_turn(nc.vector.tensor_reduce(total[:, :, 0], kept[:], AX.X, ALU.add))
                in_turn(nc.vector.tensor_scalar(good[:], total[:], EPS, None, ALU.is_gt))
                in_turn(nc.vector.tensor_scalar(half[:], good[:], -1.0 / TOP_K, 1.0 / TOP_K, ALU.mult, ALU.add))
                in_turn(nc.vector.tensor_scalar(total[:], total[:], EPS, None, ALU.add))
                in_turn(nc.vector.reciprocal(inverse[:], total[:]))
                in_turn(nc.vector.tensor_tensor(inverse[:], inverse[:], good[:], ALU.mult))
                in_turn(nc.vector.tensor_tensor(kept[:], kept[:], wide(inverse), ALU.mult))
                in_turn(nc.vector.tensor_tensor(mask[:], mask[:], wide(half), ALU.mult))
                in_turn(nc.vector.tensor_tensor(gate[:], kept[:], mask[:], ALU.add))
                left = [gate, rest, gate]
                for q in range(PARTS):
                    last = nc.vector.tensor_copy(parts[:, :, q, :], left[q][:])
                    if q < PARTS - 1:
                        in_turn(last)
                        in_turn(nc.vector.tensor_tensor(left[q + 1][:], left[q][:], parts[:, :, q, :], ALU.subtract))
                last.then_inc(routed, 1)
                for i in range(BLOCKS // 8):
                    dve.wait_ge(gates_turned, i + 1)
                    nc.vector.tensor_copy(g.gates_t[:, i * 8 * P:(i + 1) * 8 * P], gates_p[i % 2][:]
                                          ).then_inc(gates_kept, 1)


def turned_weights(nc, g, families, hi, lo, tag):
    with ExitStack() as ctx:
        sem = lambda n: ctx.enter_context(nc.semaphore(n + tag))
        ring = 4
        raw = [ctx.enter_context(nc.sbuf_tensor(f"raw{q}{tag}", [P, 4, P], F32)) for q in range(ring)]
        blocks = [ctx.enter_context(nc.psum_tensor(f"blocks{q}{tag}", [P, 4 * P], F32)) for q in range(ring)]
        loaded = [sem(f"raw_loaded{q}") for q in range(ring)]
        turned = sem("raw_turned")
        hi_done = sem("hi_done")
        lo_done = sem("lo_done")
        starts, total = [], 0
        for _, n in families:
            starts.append(total)
            total += n

        with nc.Block() as block:
            @block.sync
            def _(sp):
                for (view, n), start in zip(families, starts):
                    with sp.Fori(0, n // ring) as i:
                        for q in range(ring):
                            sp.wait_ge(turned, start + ring * i + q + 1)
                            sp.dma_start(raw[q][:], view(ring * i + q)).then_inc(loaded[q], 16)

            @block.tensor
            def _(pe):
                pe.sem_inc(turned, ring)
                with pe.Fori(0, total // ring) as i:
                    for q in range(ring):
                        pe.wait_ge(loaded[q], 16 * (i + 1))
                        pe.wait_ge(lo_done, ring * i + q + 1)
                        for k in range(4):
                            last = nc.tensor.transpose(blocks[q][:, k * P:(k + 1) * P], raw[q][:, k, :], g.ident[:])
                        last.then_inc(turned, 1)

            @block.scalar
            def _(act):
                with act.Fori(0, total // ring) as i:
                    for q in range(ring):
                        act.wait_ge(turned, ring * i + q + 1 + ring)
                        nc.scalar.activation(hi[:, ring * i + q, :], blocks[q][:], ACT.Copy).then_inc(hi_done, 1)

            @block.vector
            def _(dve):
                dve.sem_inc(lo_done, ring)
                with dve.Fori(0, total // ring) as i:
                    for q in range(ring):
                        dve.wait_ge(hi_done, ring * i + q + 1)
                        nc.vector.tensor_tensor(lo[:, ring * i + q, :], blocks[q][:],
                                                hi[:, ring * i + q, :].bitcast(F32), ALU.subtract).then_inc(lo_done, 1)


def experts(nc, g, hi, lo, blocks, gated, tag):
    with ExitStack() as ctx:
        sb = lambda n, s, d=F32: ctx.enter_context(nc.sbuf_tensor(n + tag, s, d))
        ps = lambda n, s, d=F32: ctx.enter_context(nc.psum_tensor(n + tag, s, d))
        sem = lambda n: ctx.enter_context(nc.semaphore(n + tag))
        x_cols = sb("x_cols", [P, KD, TILE])
        x_hi, x_lo = sb("x_hi", [P, KD, TILE], F32R), sb("x_lo", [P, KD, TILE], F32R)
        base = sb("base", [P, KD, TILE])
        table_in = sb("table_in", [P, 1])
        bent = [sb(f"bent{q}", [P, TILE]) for q in range(2)]
        hidden = [sb(f"hidden{q}", [P, TILE]) for q in range(2)]
        hid_hi = [sb(f"hid_hi{q}", [P, TILE], F32R) for q in range(2)]
        hid_lo = [sb(f"hid_lo{q}", [P, TILE], F32R) for q in range(2)]
        up = [ps(f"up{q}", [P, TILE]) for q in range(2)]
        factor = [ps(f"factor{q}", [P, TILE]) for q in range(2)]
        out = [ps(f"out{m}", [P, TILE]) for m in range(KD)]

        x_loaded, x_hi_done, x_split = sem("x_loaded"), sem("x_hi_done"), sem("x_split")
        up_done, factor_done = sem("up_done"), sem("factor_done")
        bent_done = sem("bent_done")
        product_done, hi_done, hid_split = sem("product_done"), sem("hid_hi_done"), sem("hid_split")
        hid_used = sem("hid_used")
        out_done = sem("out_done")
        out_kept = sem("out_kept")
        base_loaded = sem("base_loaded")
        base_stored = sem("base_stored")
        per = 1 if gated else HR // P
        stores = 1 if gated else PER_TILE

        down0 = 2 * blocks if gated else blocks

        with nc.Block() as block:
            @block.sync
            def _(sp):
                sp.dma_start(x_cols[:], g.x_t[0]).then_inc(x_loaded, 16)
                sp.sem_inc(base_stored, 16)
                with sp.Fori(0, TILES) as i:
                    sp.wait_ge(base_stored, 16 * stores * i + 16)
                    sp.dma_start(base[:], (g.x_t if gated else g.shared)[i]).then_inc(base_loaded, 16)
                    sp.wait_ge(x_split, i + 1)
                    sp.dma_start(x_cols[:], g.x_t[(i + 1) % TILES]).then_inc(x_loaded, 16)
                    sp.wait_ge(out_kept, KD * (i + 2))
                    if gated:
                        sp.dma_start(g.shared[i], base[:]).then_inc(base_stored, 16)
                    else:
                        for c in range(PER_TILE):
                            sp.dma_start(g.x1_t[PER_TILE * i + c], base[:, :, c * CH:(c + 1) * CH]
                                         ).then_inc(base_stored, 16)
                sp.wait_ge(base_stored, 16 * stores * TILES + 16)
                sp.wait_ge(x_loaded, 16 * (TILES + 1))

            @block.tensor
            def _(pe):
                pe.sem_inc(hid_used, 2)

                def product(to, slots, columns, first=True, last=True):
                    for k, (slot, col) in enumerate(slots):
                        a_hi, a_lo = hi[:, slot, col:col + P], lo[:, slot, col:col + P]
                        b_hi, b_lo = columns(k)
                        nc.tensor.matmul(to, a_hi, b_hi, start=first and k == 0, stop=False)
                        nc.tensor.matmul(to, a_hi, b_lo, start=False, stop=False)
                        ins = nc.tensor.matmul(to, a_lo, b_hi, start=False, stop=last and k == len(slots) - 1)
                    return ins

                x_at = lambda k: (x_hi[:, k, :], x_lo[:, k, :])

                def down(i, j):
                    pe.wait_ge(hid_split, blocks * i + j + 1)
                    if j == 0:
                        pe.wait_ge(out_kept, KD * (i + 1))
                    for m in range(KD):
                        ins = product(out[m][:], [(down0 + j, m * P)],
                                      lambda k: (hid_hi[j % 2][:], hid_lo[j % 2][:]), j == 0, j == blocks - 1)
                        if j == blocks - 1 and m < KD - 1:
                            ins.then_inc(out_done, 1)
                    ins.then_inc(hid_used, 1)

                with pe.Fori(0, TILES) as i:
                    pe.wait_ge(x_split, i + 1)
                    for j in range(blocks):
                        product(up[j % 2][:], [(j, k * P) for k in range(KD)], x_at).then_inc(up_done, 1)
                        if gated:
                            product(factor[j % 2][:], [(blocks + j, k * P) for k in range(KD)], x_at
                                    ).then_inc(factor_done, 1)
                        elif j % per == 0:
                            e = j // per
                            nc.tensor.matmul(factor[e % 2][:], g.select[:, e, :],
                                             g.gates_t[:, bass.ds(i * TILE, TILE)], start=True, stop=True
                                             ).then_inc(factor_done, 1)
                        if j >= 1:
                            down(i, j - 1)
                    down(i, blocks - 1)

            @block.scalar
            def _(act):
                def split(i):
                    act.wait_ge(x_loaded, 16 * (i + 1))
                    for k in range(KD):
                        nc.scalar.activation(x_hi[:, k, :], x_cols[:, k, :], ACT.Copy).then_inc(x_hi_done, 1)

                nc.scalar.activation(table_in[:], g.ones[:, 0:1], ACT.Silu if gated else ACT.Gelu)
                split(0)
                with act.Fori(0, TILES) as i:
                    for j in range(blocks):
                        act.wait_ge(up_done, blocks * i + j + 1)
                        nc.scalar.activation(bent[j % 2][:], up[j % 2][:], ACT.Silu if gated else ACT.Gelu
                                             ).then_inc(bent_done, 1)
                    act.wait_ge(factor_done if gated else up_done, blocks * (i + 1))
                    split(i + 1)

            @block.vector
            def _(dve):
                dve.sem_inc(out_kept, KD)

                def split(i):
                    for k in range(KD):
                        dve.wait_ge(x_hi_done, KD * i + k + 1)
                        ins = nc.vector.tensor_tensor(x_lo[:, k, :], x_cols[:, k, :], x_hi[:, k, :].bitcast(F32),
                                                      ALU.subtract)
                    ins.then_inc(x_split, 1)

                split(0)
                with dve.Fori(0, TILES) as i:
                    for j in range(blocks):
                        n = blocks * i + j + 1
                        dve.wait_ge(bent_done, n)
                        if j % per == 0:
                            dve.wait_ge(factor_done, (blocks // per) * i + j // per + 1)
                        dve.wait_ge(hid_used, n)
                        nc.vector.tensor_tensor(hidden[j % 2][:], bent[j % 2][:], factor[j // per % 2][:], ALU.mult
                                                ).then_inc(product_done, 1)
                        dve.wait_ge(product_done, n)
                        nc.vector.tensor_copy(hid_hi[j % 2][:], hidden[j % 2][:]).then_inc(hi_done, 1)
                        dve.wait_ge(hi_done, n)
                        nc.vector.tensor_tensor(hid_lo[j % 2][:], hidden[j % 2][:], hid_hi[j % 2][:].bitcast(F32),
                                                ALU.subtract).then_inc(hid_split, 1)
                    split(i + 1)
                    dve.wait_ge(base_loaded, 16 * (i + 1))
                    for m in range(KD):
                        if m < KD - 1:
                            dve.wait_ge(out_done, (KD - 1) * i + m + 1)
                        else:
                            dve.wait_ge(hid_used, blocks * (i + 1) + 2)
                        nc.vector.scalar_tensor_tensor(base[:, m, :], out[m][:], SCALE, base[:, m, :],
                                                       ALU.mult, ALU.add).then_inc(out_kept, 1)


def gru_weights(nc, g, weights, steps, conds, biases):
    with ExitStack() as ctx:
        sem = lambda n: ctx.enter_context(nc.semaphore("gw_" + n))
        sb = lambda n, s, d=F32: ctx.enter_context(nc.sbuf_tensor("gw_" + n, s, d))
        w_raw, u_raw, c_raw, rest = [[sb(f"{n}{c}", [P, KD, D]) for c in range(3)] for n in "wucr"]
        bias = sb("bias", [1, 3, D])
        rows = [ctx.enter_context(nc.psum_tensor(f"gw_rows{c}", [B, D], F32)) for c in range(3)]
        w_loaded, u_loaded, c_loaded = sem("w_loaded"), sem("u_loaded"), sem("c_loaded")
        w_hi_done, u_hi_done, u_rest_done = sem("w_hi_done"), sem("u_hi_done"), sem("u_rest_done")
        rows_done, row_hi_done = sem("rows_done"), sem("row_hi_done")
        by_block = lambda w: w.rearrange("(k p) n -> p k n", p=P)

        with nc.Block() as block:
            @block.sync
            def _(sp):
                for c in range(3):
                    sp.dma_start(w_raw[c][:], by_block(weights[c])).then_inc(w_loaded, 16)
                for c in range(3):
                    sp.dma_start(u_raw[c][:], by_block(steps[c])).then_inc(u_loaded, 16)
                for c in range(3):
                    sp.dma_start(c_raw[c][:], by_block(conds[c])).then_inc(c_loaded, 16)
                    sp.dma_start(bias[0:1, c, :], biases[c].rearrange("(a n) -> a n", a=1)).then_inc(c_loaded, 16)

            @block.tensor
            def _(pe):
                pe.wait_ge(c_loaded, 6 * 16)
                for c in range(3):
                    for k in range(KD):
                        nc.tensor.matmul(rows[c][:], g.cond_t[:, k, :], c_raw[c][:, k, :], start=k == 0, stop=False)
                    nc.tensor.matmul(rows[c][:], g.ones[0:1, 0:B], bias[0:1, c, :], start=False, stop=True
                                     ).then_inc(rows_done, 1)

            @block.scalar
            def _(act):
                act.wait_ge(w_loaded, 3 * 16)
                for c in range(3):
                    nc.scalar.activation(g.w_hi[:, c, :, :], w_raw[c][:], ACT.Copy).then_inc(w_hi_done, 1)
                act.wait_ge(u_loaded, 3 * 16)
                for c in range(3):
                    nc.scalar.activation(g.u_hi[:, c, :, :], u_raw[c][:], ACT.Copy).then_inc(u_hi_done, 1)
                for c in range(3):
                    act.wait_ge(u_rest_done, c + 1)
                    nc.scalar.activation(g.u_lo[:, c, :, :], rest[c][:], ACT.Copy, scale=LOW)
                for c in range(3):
                    act.wait_ge(rows_done, c + 1)
                    nc.scalar.activation(g.row_hi[:, c, :], rows[c][:], ACT.Copy).then_inc(row_hi_done, 1)

            @block.vector
            def _(dve):
                nc.vector.tensor_copy(g.pick[:], g.pick_f[:])
                for c in range(3):
                    dve.wait_ge(w_hi_done, c + 1)
                    nc.vector.tensor_tensor(g.w_lo[:, c, :, :], w_raw[c][:], g.w_hi[:, c, :, :].bitcast(F32),
                                            ALU.subtract)
                for c in range(3):
                    dve.wait_ge(u_hi_done, c + 1)
                    nc.vector.tensor_tensor(rest[c][:], u_raw[c][:], g.u_hi[:, c, :, :], ALU.subtract
                                            ).then_inc(u_rest_done, 1)
                for c in range(3):
                    dve.wait_ge(row_hi_done, c + 1)
                    nc.vector.tensor_tensor(g.row_lo[:, c, :], rows[c][:], g.row_hi[:, c, :].bitcast(F32),
                                            ALU.subtract)


def input_share(nc, g, bank, c, b, x_hi, x_lo):
    def add(to, weights, columns, first=False, last=False):
        return nc.tensor.matmul(to, weights, columns, start=first, stop=last, skip_group_check=True)

    for m in range(KD):
        to, cols = bank[:, m, :], slice(m * P, (m + 1) * P)
        for k in range(KD):
            add(to, g.w_hi[:, c, k, cols], x_hi[:, k, :], first=m == 0 and k == 0)
            add(to, g.w_hi[:, c, k, cols], x_lo[:, k, :])
            add(to, g.w_lo[:, c, k, cols], x_hi[:, k, :])
        add(to, g.row_hi[:, c, cols], g.pick[:, b, :])
        ins = add(to, g.row_lo[:, c, cols], g.pick[:, b, :], last=m == KD - 1)
    return ins


def gru(nc, g, out):
    with ExitStack() as ctx:
        sb = lambda n, s, d=F32: [ctx.enter_context(nc.sbuf_tensor(f"{n}_b{b}", s, d)) for b in range(B)]
        sem = lambda n: [ctx.enter_context(nc.semaphore(f"{n}_b{b}")) for b in range(B)]
        flat = [P, KD, CH]
        long = [P, KD, CH + 1]
        x_in, x_add = sb("x_in", flat), sb("x_add", flat)
        x_hi, x_lo = sb("gx_hi", flat, F32R), sb("gx_lo", flat, F32R)
        h, keep, gain = sb("h", long), sb("keep", long), sb("gain", long)
        h_first = sb("h_first", [P, KD, 1])
        r, z, cand, rh = sb("r", flat), sb("z", flat), sb("cand", flat), sb("rh", flat)
        h_sent, rh_sent = sb("h_sent", flat), sb("rh_sent", flat)
        h_step, rh_step = sb("h_step", flat, F16), sb("rh_step", flat, F16)
        h_fine, rh_fine = sb("h_fine", flat, F16), sb("rh_fine", flat, F16)
        off, square = sb("off", [P, 2, KD, CH]), sb("square", [P, CHECKS, KD, CH])
        y, y_rows = sb("y", flat), sb("y_rows", [P, D])
        bank = [[ctx.enter_context(nc.psum_tensor(f"gate{c}_b{b}", flat, F32)) for c in range(3)] for b in range(B)]
        y_turned = [ctx.enter_context(nc.psum_tensor(f"y_turned_b{b}", [P, D], F32)) for b in range(B)]

        x_in_loaded, x_add_loaded = sem("x_in_loaded"), sem("x_add_loaded")
        x_hi_done, x_split = sem("gx_hi_done"), sem("gx_split")
        share_done = sem("share_done")
        cleared, first_done, start_done = sem("cleared"), sem("first_done"), sem("start_done")
        h_step_done = sem("h_step_done")
        rh_done, rh_step_done = sem("rh_done"), sem("rh_step_done")
        h_sent_done, rh_sent_done = sem("h_sent_done"), sem("rh_sent_done")
        r_sum, z_sum, c_sum = sem("r_sum"), sem("z_sum"), sem("c_sum")
        r_done, z_done, keep_done, gain_done = sem("r_done"), sem("z_done"), sem("keep_done"), sem("gain_done")
        cand_done = sem("cand_done")
        h_done = sem("h_done")
        h_fine_done, rh_fine_done = sem("h_fine_done"), sem("rh_fine_done")
        off_done, squared = sem("off_done"), sem("squared")
        y_done, y_turn_done, y_kept = sem("y_done"), sem("y_turn_done"), sem("y_kept")
        y_stored = sem("y_stored")
        table_in = ctx.enter_context(nc.sbuf_tensor("table_warmed", [P, 1], F32))
        zeros = ctx.enter_context(nc.sbuf_tensor("zeros", flat, F32))
        zeros_made = ctx.enter_context(nc.semaphore("zeros_made"))

        streams = range(B)
        before = lambda t: t[:, :, 0:CH]
        after = lambda t: t[:, :, 1:CH + 1]
        line = lambda t: t[:].rearrange("p k t -> p (k t)")

        def turns(eng, turn, c):
            with eng.Fori(0, FINE) as k:
                turn(c * TURNS + k, False)
            turn(c * TURNS + FINE, True)
            with eng.Fori(FINE + 1, TURNS) as k:
                turn(c * TURNS + k, False)

        with nc.Block() as block:
            @block.sync
            def _(sp):
                for b in streams:
                    sp.sem_inc(y_stored[b], 16)
                    sp.dma_start(x_in[b][:], g.x1_t[b * CHUNKS]).then_inc(x_in_loaded[b], 16)
                with sp.Fori(0, CHUNKS) as c:
                    for b in streams:
                        sp.wait_ge(y_done[b], c + 1)
                        sp.dma_start(x_add[b][:], g.x1_t[b * CHUNKS + c]).then_inc(x_add_loaded[b], 16)
                    for b in streams:
                        sp.wait_ge(x_split[b], c + 1)
                        sp.dma_start(x_in[b][:], g.x1_t[b * CHUNKS + (c + 1) % CHUNKS]).then_inc(x_in_loaded[b], 16)
                    for b in streams:
                        sp.wait_ge(y_kept[b], c + 2)
                        sp.dma_start(out[b, bass.ds(c * CH, CH), :], y_rows[b][:]).then_inc(y_stored[b], 16)
                for b in streams:
                    sp.wait_ge(y_stored[b], 16 * (CHUNKS + 1))
                    sp.wait_ge(x_in_loaded[b], 16 * (CHUNKS + 1))

            @block.tensor
            def _(pe):
                for b in streams:
                    pe.sem_inc(y_turn_done[b], 1)

                def add(to, weights, columns):
                    for m in range(KD):
                        for k in range(KD):
                            ins = nc.tensor.matmul(to[:, m, :], weights[:, k, m * P:(m + 1) * P], columns[:, k, :],
                                                   start=False, stop=m == KD - 1 and k == KD - 1,
                                                   skip_group_check=True)
                    return ins

                with pe.Fori(0, CHUNKS) as c:
                    for b in streams:
                        pe.wait_ge(x_split[b], c + 1)
                        pe.wait_ge(cand_done[b], TURNS * c + 1)
                        for gate in (R, Z):
                            input_share(nc, g, bank[b][gate], gate, b, x_hi[b], x_lo[b])
                        input_share(nc, g, bank[b][C], C, b, x_hi[b], x_lo[b]).then_inc(share_done[b], 1)

                    def turn(n, fine):
                        for b in streams:
                            pe.wait_ge(h_step_done[b], n + c + 1)
                            if fine:
                                pe.wait_ge(h_fine_done[b], c + 1)
                            for gate, done in ((R, r_sum), (Z, z_sum)):
                                if fine:
                                    add(bank[b][gate], g.u_lo[:, gate], h_fine[b])
                                add(bank[b][gate], g.u_hi[:, gate], h_step[b]).then_inc(done[b], 1)
                        for b in streams:
                            pe.wait_ge(rh_step_done[b], n + 1)
                            if fine:
                                pe.wait_ge(rh_fine_done[b], c + 1)
                                add(bank[b][C], g.u_lo[:, C], rh_fine[b])
                            add(bank[b][C], g.u_hi[:, C], rh_step[b]).then_inc(c_sum[b], 1)

                    turns(pe, turn, c)
                    for b in streams:
                        pe.wait_ge(y_done[b], c + 2)
                        pe.wait_ge(y_kept[b], c + 1)
                        for k in range(KD):
                            ins = nc.tensor.transpose(y_turned[b][:, k * P:(k + 1) * P], y[b][:, k, :], g.ident[:])
                        ins.then_inc(y_turn_done[b], 1)

            @block.scalar
            def _(act):
                for b in streams:
                    act.sem_inc(cand_done[b], 1)
                    act.sem_inc(squared[b], 1)
                    act.sem_inc(y_kept[b], 1)
                nc.scalar.activation(table_in[:], g.ones[:, 0:1], ACT.Sigmoid)

                with act.Fori(0, CHUNKS) as c:
                    def turn(n, fine):
                        for b in streams:
                            if fine:
                                act.wait_ge(h_done[b], n + 1)
                                nc.scalar.activation(h_fine[b][:], before(h[b]), ACT.Copy, scale=1 / LOW
                                                     ).then_inc(h_fine_done[b], 1)
                            act.wait_ge(r_sum[b], n + 1)
                            nc.scalar.activation(r[b][:], bank[b][R][:], ACT.Sigmoid).then_inc(r_done[b], 1)
                        for b in streams:
                            act.wait_ge(z_sum[b], n + 1)
                            nc.scalar.activation(z[b][:], bank[b][Z][:], ACT.Sigmoid).then_inc(z_done[b], 1)
                            nc.scalar.activation(after(keep[b]), bank[b][Z][:], ACT.Sigmoid, scale=-1.0
                                                 ).then_inc(keep_done[b], 1)
                            if fine:
                                act.wait_ge(rh_done[b], n + 1)
                                nc.scalar.activation(rh_fine[b][:], rh[b][:], ACT.Copy, scale=1 / LOW
                                                     ).then_inc(rh_fine_done[b], 1)
                        for b in streams:
                            act.wait_ge(c_sum[b], n + 1)
                            nc.scalar.activation(cand[b][:], bank[b][C][:], ACT.Tanh).then_inc(cand_done[b], 1)

                    turns(act, turn, c)
                    for b in streams:
                        act.wait_ge(h_step_done[b], (TURNS + 1) * (c + 1))
                        act.wait_ge(off_done[b], 2 * (c + 1))
                        for kind, what in enumerate((h_step[b][:], rh_step[b][:], off[b][:, 0], off[b][:, 1])):
                            ins = nc.scalar.activation(square[b][:, kind], what, ACT.Square,
                                                       accum_out=g.left[:, kind, b, bass.ds(c, 1)])
                        ins.then_inc(squared[b], 1)
                        act.wait_ge(y_turn_done[b], c + 2)
                        act.wait_ge(y_stored[b], 16 * (c + 1))
                        nc.scalar.activation(y_rows[b][:], y_turned[b][:], ACT.Copy).then_inc(y_kept[b], 1)

            @block.gpsimd
            def _(pool):
                def split(b, c):
                    pool.wait_ge(x_in_loaded[b], 16 * (c + 1))
                    nc.gpsimd.tensor_tensor(x_hi[b][:], x_in[b][:], zeros[:], ALU.add).then_inc(x_hi_done[b], 1)
                    pool.wait_ge(x_hi_done[b], c + 1)
                    nc.gpsimd.tensor_tensor(x_lo[b][:], x_in[b][:], x_hi[b][:].bitcast(F32), ALU.subtract
                                            ).then_inc(x_split[b], 1)

                def reset(b):
                    nc.gpsimd.memset(h_sent[b][:], 0.0).then_inc(h_sent_done[b], 1)
                    nc.gpsimd.memset(rh_sent[b][:], 0.0).then_inc(rh_sent_done[b], 1)

                nc.gpsimd.memset(zeros[:], 0.0).then_inc(zeros_made, 1)
                pool.wait_ge(zeros_made, 1)
                for b in streams:
                    pool.sem_inc(y_done[b], 1)
                    reset(b)
                    split(b, 0)
                with pool.Fori(0, CHUNKS) as c:
                    def turn(n, fine):
                        for b in streams:
                            pool.wait_ge(h_step_done[b], n + c + 1)
                            pool.wait_ge(h_sent_done[b], n + c + 1)
                            nc.gpsimd.tensor_tensor(h_sent[b][:], h_sent[b][:], h_step[b][:], ALU.add
                                                    ).then_inc(h_sent_done[b], 1)
                        for b in streams:
                            pool.wait_ge(rh_step_done[b], n + 1)
                            pool.wait_ge(rh_sent_done[b], n + c + 1)
                            nc.gpsimd.tensor_tensor(rh_sent[b][:], rh_sent[b][:], rh_step[b][:], ALU.add
                                                    ).then_inc(rh_sent_done[b], 1)

                    turns(pool, turn, c)
                    for b in streams:
                        pool.wait_ge(h_step_done[b], (TURNS + 1) * (c + 1))
                        pool.wait_ge(h_sent_done[b], (TURNS + 1) * (c + 1))
                        pool.wait_ge(rh_sent_done[b], (TURNS + 1) * (c + 1))
                        pool.wait_ge(x_add_loaded[b], 16 * (c + 1))
                        pool.wait_ge(y_turn_done[b], c + 1)
                        nc.gpsimd.tensor_tensor(y[b][:], x_add[b][:], after(h[b]), ALU.add).then_inc(y_done[b], 1)
                        reset(b)
                        pool.wait_ge(share_done[b], c + 1)
                        split(b, c + 1)

            @block.vector
            def _(dve):
                for b in streams:
                    nc.vector.memset(h[b][:], 0.0).then_inc(cleared[b], 1)
                    nc.vector.memset(keep[b][:, :, 0:1], 0.0).then_inc(cleared[b], 1)
                    dve.wait_ge(cleared[b], 2)
                    dve.sem_inc(h_done[b], 1)

                def step_of(b, n, c):
                    dve.wait_ge(h_sent_done[b], n + c + 1)
                    nc.vector.tensor_tensor(h_step[b][:], before(h[b]), h_sent[b][:], ALU.subtract
                                            ).then_inc(h_step_done[b], 1)

                with dve.Fori(0, CHUNKS) as c:
                    for b in streams:
                        dve.wait_ge(y_done[b], c + 1)
                        dve.wait_ge(squared[b], c + 1)
                        nc.vector.tensor_copy(h_first[b][:], h[b][:, :, CH:CH + 1]).then_inc(first_done[b], 1)
                        dve.wait_ge(first_done[b], c + 1)
                        nc.vector.tensor_copy(gain[b][:, :, 0:1], h_first[b][:]).then_inc(start_done[b], 1)
                        nc.vector.tensor_copy(h[b][:], h_first[b][:].to_broadcast(long)).then_inc(start_done[b], 1)
                        dve.wait_ge(start_done[b], 2 * (c + 1))
                        step_of(b, TURNS * c, c)

                    def turn(n, fine):
                        for b in streams:
                            dve.wait_ge(r_done[b], n + 1)
                            nc.vector.tensor_tensor(rh[b][:], r[b][:], before(h[b]), ALU.mult).then_inc(rh_done[b], 1)
                            dve.wait_ge(rh_done[b], n + 1)
                            dve.wait_ge(rh_sent_done[b], n + c + 1)
                            nc.vector.tensor_tensor(rh_step[b][:], rh[b][:], rh_sent[b][:], ALU.subtract
                                                    ).then_inc(rh_step_done[b], 1)
                        for b in streams:
                            dve.wait_ge(cand_done[b], n + 2)
                            nc.vector.tensor_tensor(after(gain[b]), z[b][:], cand[b][:], ALU.mult
                                                    ).then_inc(gain_done[b], 1)
                            dve.wait_ge(gain_done[b], n + 1)
                            nc.vector.tensor_tensor_scan(line(h[b]), line(keep[b]), line(gain[b]), 0.0,
                                                         ALU.mult, ALU.add).then_inc(h_done[b], 1)
                            dve.wait_ge(h_done[b], n + 2)
                            step_of(b, n + 1, c)

                    turns(dve, turn, c)
                    for b in streams:
                        for kind, (fine, all_of) in enumerate(((h_fine[b], before(h[b])), (rh_fine[b], rh[b][:]))):
                            nc.vector.scalar_tensor_tensor(off[b][:, kind], fine[:], LOW, all_of, ALU.mult,
                                                           ALU.subtract).then_inc(off_done[b], 1)


def all_settled(nc, g):
    with ExitStack() as ctx:
        below = ctx.enter_context(nc.sbuf_tensor("below", [P, CHECKS, B, CHUNKS], F32))
        count = ctx.enter_context(nc.sbuf_tensor("count", [P, 1], F32))
        number = ctx.enter_context(nc.psum_tensor("number", [1, 1], F32))
        compared, counted, summed = [ctx.enter_context(nc.semaphore(n)) for n in ("compared", "counted", "summed")]
        with nc.Block() as block:
            @block.vector
            def _(dve):
                for kind in range(CHECKS):
                    nc.vector.tensor_scalar(below[:, kind], g.left[:, kind], BOUNDS[kind], None, ALU.is_le
                                            ).then_inc(compared, 1)
                dve.wait_ge(compared, CHECKS)
                nc.vector.tensor_reduce(count[:], below[:].rearrange("p a b c -> p (a b c)"), AX.X, ALU.add
                                        ).then_inc(counted, 1)
                dve.wait_ge(summed, 1)
                nc.vector.tensor_scalar(g.settled[:], number[:], float(P * CHECKS * B * CHUNKS), None, ALU.is_equal)

            @block.tensor
            def _(pe):
                pe.wait_ge(counted, 1)
                nc.tensor.matmul(number[:], count[:], g.ones[:, 0:1], start=True, stop=True).then_inc(summed, 1)


def step_by_step(nc, g, steps, out):
    with ExitStack() as ctx:
        sb = lambda n, s, d=F32: ctx.enter_context(nc.sbuf_tensor("st_" + n, s, d))
        ps = lambda n, s: ctx.enter_context(nc.psum_tensor("st_" + n, s, F32))
        sem = lambda n: ctx.enter_context(nc.semaphore("st_" + n))
        flat = [P, B, KD, CH]
        x_in, x_hi, x_lo = sb("x_in", flat), sb("x_hi", flat, F32R), sb("x_lo", flat, F32R)
        share = sb("share", [P, 3, B, KD, CH])
        states, y, y_rows = sb("states", flat), sb("y", flat), sb("y_rows", [P, B, D])
        u = [sb(f"u{c}", [P, KD, D]) for c in range(3)]
        h, rh, keep, cand = [sb(n, [P, B, KD]) for n in ("h", "rh", "keep", "cand")]
        sums, gates = sb("sums", [P, 3, B, KD]), sb("gates", [P, 2, B, KD])
        kept, gain = sb("kept", [P, B, KD]), sb("gain", [P, B, KD])
        bank = [ps(f"bank{c}", [P, KD, CH]) for c in range(3)]
        of_h, of_rh, y_turned = ps("of_h", [P, 2, B, KD]), ps("of_rh", [P, B, KD]), ps("y_turned", [P, D])
        u_loaded, x_loaded, x_hi_done, x_split = sem("u_loaded"), sem("x_loaded"), sem("x_hi_done"), sem("x_split")
        share_done, share_kept = sem("share_done"), sem("share_kept")
        h_done = sem("h_done")
        of_h_done, rz_sum, rz_done, keep_done, rh_done = [
            sem(n) for n in ("of_h_done", "rz_sum", "rz_done", "keep_done", "rh_done")]
        of_rh_done, c_sum, cand_done, parts_done = [sem(n) for n in ("of_rh_done", "c_sum", "cand_done", "parts_done")]
        state_kept, y_done, y_turn_done, y_kept, y_stored = [
            sem(n) for n in ("state_kept", "y_done", "y_turn_done", "y_kept", "y_stored")]

        def where_unsettled(eng, run):
            settled = eng.value_load(g.settled[0:1, 0:1], min_val=0, max_val=1)
            with eng.If(settled == 0):
                run()
            with eng.Else():
                eng.nop()

        with nc.Block() as block:
            @block.sync
            def _(sp):
                def run():
                    sp.sem_inc(y_stored, 16 * B)
                    for c in range(3):
                        sp.dma_start(u[c][:], steps[c].rearrange("(k p) n -> p k n", p=P)).then_inc(u_loaded, 16)
                    for b in range(B):
                        sp.dma_start(x_in[:, b], g.x1_t[b * CHUNKS]).then_inc(x_loaded, 16)
                    with sp.Fori(0, CHUNKS) as c:
                        for b in range(B):
                            sp.wait_ge(y_kept, B * c + b + 1)
                            sp.dma_start(out[b, bass.ds(c * CH, CH), :], y_rows[:, b]).then_inc(y_stored, 16)
                        for b in range(B):
                            sp.dma_start(x_in[:, b], g.x1_t[b * CHUNKS + (c + 1) % CHUNKS]).then_inc(x_loaded, 16)
                    sp.wait_ge(y_stored, 16 * B * (CHUNKS + 1))
                    sp.wait_ge(x_loaded, 16 * B * (CHUNKS + 1))
                where_unsettled(sp, run)

            @block.tensor
            def _(pe):
                def add(to, weights, columns):
                    for m in range(KD):
                        for k in range(KD):
                            ins = nc.tensor.matmul(to[:, :, m], weights[:, k, m * P:(m + 1) * P], columns[:, :, k],
                                                   start=k == 0, stop=k == KD - 1)
                    return ins

                def run():
                    pe.wait_ge(u_loaded, 3 * 16)
                    with pe.Fori(0, CHUNKS) as c:
                        pe.wait_ge(x_split, c + 1)
                        for b in range(B):
                            for gate in range(3):
                                if b == 1:
                                    pe.wait_ge(share_kept, 6 * c + gate + 1)
                                input_share(nc, g, bank[gate], gate, b, x_hi[:, b], x_lo[:, b]
                                            ).then_inc(share_done, 1)
                        with pe.Fori(0, CH) as t:
                            n = c * CH + t + 1
                            pe.wait_ge(h_done, n)
                            for gate in (R, Z):
                                ins = add(of_h[:, gate], u[gate], h)
                            ins.then_inc(of_h_done, 1)
                            pe.wait_ge(rh_done, n)
                            add(of_rh, u[C], rh).then_inc(of_rh_done, 1)
                        pe.wait_ge(y_done, c + 1)
                        for b in range(B):
                            if b == 1:
                                pe.wait_ge(y_kept, B * c + 1)
                            for k in range(KD):
                                ins = nc.tensor.transpose(y_turned[:, k * P:(k + 1) * P], y[:, b, k, :], g.ident[:])
                            ins.then_inc(y_turn_done, 1)
                where_unsettled(pe, run)

            @block.scalar
            def _(act):
                def run():
                    with act.Fori(0, CHUNKS) as c:
                        act.wait_ge(x_loaded, 16 * B * (c + 1))
                        nc.scalar.activation(x_hi[:], x_in[:], ACT.Copy).then_inc(x_hi_done, 1)
                        with act.Fori(0, CH) as t:
                            n = c * CH + t + 1
                            act.wait_ge(rz_sum, n)
                            nc.scalar.activation(gates[:], sums[:, 0:2], ACT.Sigmoid).then_inc(rz_done, 1)
                            nc.scalar.activation(keep[:], sums[:, Z], ACT.Sigmoid, scale=-1.0).then_inc(keep_done, 1)
                            act.wait_ge(c_sum, n)
                            nc.scalar.activation(cand[:], sums[:, C], ACT.Tanh).then_inc(cand_done, 1)
                        for b in range(B):
                            act.wait_ge(y_turn_done, B * c + b + 1)
                            act.wait_ge(y_stored, 16 * B * (c + 1))
                            nc.scalar.activation(y_rows[:, b], y_turned[:], ACT.Copy).then_inc(y_kept, 1)
                where_unsettled(act, run)

            @block.gpsimd
            def _(pool):
                pool.nop()

            @block.vector
            def _(dve):
                def run():
                    nc.vector.memset(h[:], 0.0).then_inc(h_done, 1)
                    with dve.Fori(0, CHUNKS) as c:
                        dve.wait_ge(x_hi_done, c + 1)
                        nc.vector.tensor_tensor(x_lo[:], x_in[:], x_hi[:].bitcast(F32), ALU.subtract
                                                ).then_inc(x_split, 1)
                        for b in range(B):
                            for gate in range(3):
                                dve.wait_ge(share_done, 6 * c + 3 * b + gate + 1)
                                nc.vector.tensor_copy(share[:, gate, b], bank[gate][:]).then_inc(share_kept, 1)
                        with dve.Fori(0, CH) as t:
                            n = c * CH + t + 1
                            at = bass.ds(t, 1)
                            dve.wait_ge(share_kept, 6 * (c + 1))
                            dve.wait_ge(of_h_done, n)
                            for gate in (R, Z):
                                ins = nc.vector.tensor_tensor(sums[:, gate], of_h[:, gate],
                                                              share[:, gate, :, :, at].rearrange("p b k t -> p b (k t)"),
                                                              ALU.add)
                            ins.then_inc(rz_sum, 1)
                            dve.wait_ge(rz_done, n)
                            nc.vector.tensor_tensor(rh[:], gates[:, R], h[:], ALU.mult).then_inc(rh_done, 1)
                            dve.wait_ge(keep_done, n)
                            nc.vector.tensor_tensor(kept[:], keep[:], h[:], ALU.mult).then_inc(parts_done, 1)
                            dve.wait_ge(of_rh_done, n)
                            nc.vector.tensor_tensor(sums[:, C], of_rh[:],
                                                    share[:, C, :, :, at].rearrange("p b k t -> p b (k t)"), ALU.add
                                                    ).then_inc(c_sum, 1)
                            dve.wait_ge(cand_done, n)
                            nc.vector.tensor_tensor(gain[:], gates[:, Z], cand[:], ALU.mult).then_inc(parts_done, 1)
                            dve.wait_ge(parts_done, 2 * n)
                            nc.vector.tensor_tensor(h[:], kept[:], gain[:], ALU.add).then_inc(h_done, 1)
                            dve.wait_ge(h_done, n + 1)
                            nc.vector.tensor_copy(states[:, :, :, at].rearrange("p b k t -> p b (k t)"), h[:]
                                                  ).then_inc(state_kept, 1)
                        dve.wait_ge(state_kept, CH * (c + 1))
                        nc.vector.tensor_tensor(y[:], x_in[:], states[:], ALU.add).then_inc(y_done, 1)
                where_unsettled(dve, run)


def build(nc, x, cond, router_w, router_t_w, router_bias, sw1, sw3, sw2, rw1, rw2,
          w_z, u_z, c_z, b_z, w_r, u_r, c_r, b_r, w_c, u_c, c_c, b_c, out):
    g = Shared()
    g.x_t = nc.dram_tensor("x_t", [TILES, P, KD, TILE], F32, kind="Internal").ap()
    g.shared = nc.dram_tensor("shared_t", [TILES, P, KD, TILE], F32, kind="Internal").ap()
    g.x1_t = nc.dram_tensor("x1_t", [B * CHUNKS, P, KD, CH], F32, kind="Internal").ap()
    rows4 = lambda w, j: w[bass.ds(j * P, P), :].rearrange("p (k q) -> p k q", q=P)
    cols4 = lambda w, j: w[:, bass.ds(j * P, P)].rearrange("(k p) q -> p k q", p=P)
    with ExitStack() as ctx:
        constants(nc, ctx, g)
        tokens(nc, g, x, cond, router_w, router_t_w, router_bias)
        with ExitStack() as weights:
            n = HS // P
            hi, lo = [weights.enter_context(nc.sbuf_tensor(f"shared_{s}", [P, 3 * n, D], F32R)) for s in ("hi", "lo")]
            turned_weights(nc, g, [(lambda j: rows4(sw1, j), n), (lambda j: rows4(sw3, j), n),
                                   (lambda j: cols4(sw2, j), n)], hi, lo, "_s")
            experts(nc, g, hi, lo, n, True, "_s")
        with ExitStack() as weights:
            n = E * HR // P
            hi, lo = [weights.enter_context(nc.sbuf_tensor(f"routed_{s}", [P, 2 * n, D], F32R)) for s in ("hi", "lo")]
            up = rw1.rearrange("e h d -> (e h) d")
            down = rw2.rearrange("e (k p) (j q) -> e j p k q", p=P, q=P)
            turned_weights(nc, g, [(lambda j: rows4(up, j), n),
                                   (lambda j: down[j // (HR // P), j % (HR // P)], n)], hi, lo, "_r")
            experts(nc, g, hi, lo, n, False, "_r")
        sb = lambda n, s, d: ctx.enter_context(nc.sbuf_tensor(n, s, d))
        g.w_hi, g.w_lo = sb("w_hi", [P, 3, KD, D], F32R), sb("w_lo", [P, 3, KD, D], F32R)
        g.u_hi, g.u_lo = sb("u_hi", [P, 3, KD, D], F16), sb("u_lo", [P, 3, KD, D], F16)
        g.row_hi, g.row_lo = sb("row_hi", [B, 3, D], F32R), sb("row_lo", [B, 3, D], F32R)
        g.pick = sb("pick", [B, B, P], F32R)
        g.left = sb("left", [P, CHECKS, B, CHUNKS], F32)
        g.settled = sb("settled", [1, 1], I32)
        gru_weights(nc, g, (w_r, w_z, w_c), (u_r, u_z, u_c), (c_r, c_z, c_c), (b_r, b_z, b_c))
        gru(nc, g, out)
        all_settled(nc, g)
        step_by_step(nc, g, (u_r, u_z, u_c), out)


_INS = ['x', 'cond_1024', 'L0_cond_router_w', 'L0_cond_router_t_w', 'L0_cond_router_bias', 'L0_cond_sw1',
        'L0_cond_sw3', 'L0_cond_sw2', 'L0_cond_rw1', 'L0_cond_rw2', 'L1_cond_W_z', 'L1_cond_U_z', 'L1_cond_C_z',
        'L1_cond_b_z', 'L1_cond_W_r', 'L1_cond_U_r', 'L1_cond_C_r', 'L1_cond_b_r', 'L1_cond_W', 'L1_cond_U',
        'L1_cond_C', 'L1_cond_b']
_OUTS = [((2, 2048, 512), 'float32')]


def kernel(**inputs):
    import numpy as _np
    import concourse.bacc as _bacc
    from concourse import mybir as _mybir
    from concourse.bass_utils import run_bass_kernel_spmd as _run

    nc = _bacc.Bacc("TRN2", target_bir_lowering=False, num_devices=1)
    arrays, args = {}, []
    for name in _INS:
        a = _np.ascontiguousarray(inputs[name])
        arrays[f"in_{name}_dram"] = a
        args.append(nc.dram_tensor(f"in_{name}_dram", a.shape, _mybir.dt.from_np(a.dtype), kind="ExternalInput").ap())
    for i, (shape, dtype) in enumerate(_OUTS):
        dt = _mybir.dt.from_np(_np.dtype(dtype))
        args.append(nc.dram_tensor(f"out_{i}_dram", shape, dt, kind="ExternalOutput").ap())
    build(nc, *args)
    r = _run(nc, [arrays], core_ids=[0])
    return r.results[0]["out_0_dram"]
```

```python
from contextlib import ExitStack

import concourse.bass as bass
from concourse import mybir

ALU = mybir.AluOpType
ACT = mybir.ActivationFunctionType
AX = mybir.AxisListType
F32 = mybir.dt.float32
F32R = mybir.dt.float32r
F16 = mybir.dt.float16
BF16 = mybir.dt.bfloat16
I32 = mybir.dt.int32

P = 128
D = 512
KD = D // P
B = 2
T = 2048
TILE = 512
TILES = B * T // TILE
TT = TILE // P
BLOCKS = B * T // P
E = 8
HS = 1024
HR = 256
TOP_K = 2
EPS = 1e-9
SCALE = 1.0 / 3.0
PARTS = 3
NONE = -3.0e38

CH = 128
CHUNKS = T // CH
PER_TILE = TILE // CH
TURNS = 7
FINE = 4
LATE = TURNS - 1 - FINE
LOW = 2048.0
R, Z, C = range(3)
CHECKS = 2 * LATE + 1
BOUNDS = [KD * CH * x * x for x in [1e-3] * (2 * LATE) + [1e-6]]


class Shared:
    pass


def constants(nc, ctx, g):
    sb = lambda n, s, d: ctx.enter_context(nc.sbuf_tensor(n, s, d))
    g.ident = sb("ident", [P, P], F32)
    g.ident_b = sb("ident_b", [P, P], BF16)
    g.ones = sb("ones", [P, P], F32)
    g.select = sb("select", [PARTS * E, E, P], BF16)
    g.gates_t = sb("gates_t", [PARTS * E, B * T], BF16)
    g.cond_t = sb("cond_t", [P, KD, B], F32)
    g.made = ctx.enter_context(nc.semaphore("constants_made"))
    with nc.Block() as block:
        @block.gpsimd
        def _(pool):
            nc.gpsimd.memset(g.ident[:], 0.0).then_inc(g.made, 1)
            nc.gpsimd.memset(g.ident_b[:], 0.0).then_inc(g.made, 1)
            nc.gpsimd.memset(g.select[:], 0.0).then_inc(g.made, 1)
            nc.gpsimd.memset(g.ones[:], 1.0).then_inc(g.made, 1)
            pool.wait_ge(g.made, 4)
            for t in (g.ident, g.ident_b):
                nc.gpsimd.affine_select(out=t[:], in_=t[:], compare_op=ALU.not_equal, fill=1.0, base=0,
                                        pattern=[[-1, P]], channel_multiplier=1).then_inc(g.made, 1)
            for q in range(PARTS):
                nc.gpsimd.affine_select(out=g.select[:], in_=g.select[:], compare_op=ALU.not_equal, fill=1.0,
                                        base=-q * E, pattern=[[-1, E], [0, P]], channel_multiplier=1
                                        ).then_inc(g.made, 1)
                pool.wait_ge(g.made, 7 + q)


def tokens(nc, g, x, cond, router_w, router_t_w, router_bias, ahead):
    with ExitStack() as ctx:
        sb = lambda n, s, d=F32: ctx.enter_context(nc.sbuf_tensor(n, s, d))
        ps = lambda n, s, d=F32: ctx.enter_context(nc.psum_tensor(n, s, d))
        sem = lambda n: ctx.enter_context(nc.semaphore(n))
        x_rows = [sb(f"x_rows{q}", [P, TT, D]) for q in range(2)]
        x_cols = [sb(f"x_cols{q}", [P, KD, TILE]) for q in range(2)]
        small = sb("small_rows", [E, 3, D])
        router_t = sb("router_t", [P, KD, 2, E])
        t_bias = sb("t_bias", [E, B])
        logits = sb("logits", [E, B * T])
        bias = sb("bias_all", [P, 1, E])
        score, chosen, replaced, mask, kept, gate, rest, top, find = [sb(n, [P, BLOCKS, E]) for n in (
            "score", "chosen", "replaced", "mask", "kept", "gate", "rest", "top", "find")]
        total, good, inverse, half = [sb(n, [P, BLOCKS, 1]) for n in ("total", "good", "inverse", "half")]
        parts = sb("parts", [P, BLOCKS, PARTS, E], BF16)
        turned = [ps(f"turned{a}", [P, KD, P]) for a in range(TT)]
        logits_p = [ps(f"logits_p{q}", [E, TILE]) for q in range(2)]
        small_t = ps("small_t", [P, 3, KD, E])
        gates_p = ps("gates_p", [PARTS * E, 8 * P], BF16)

        x_loaded = [sem(f"x_loaded{q}") for q in range(2)]
        x_stored = [sem(f"x_stored{q}") for q in range(2)]
        small_loaded, x_turned = sem("small_loaded"), sem("x_turned")
        cols_v, cols_a = sem("cols_v"), sem("cols_a")
        small_turned, small_kept = sem("small_turned"), sem("small_kept")
        t_bias_done, t_bias_kept = sem("t_bias_done"), sem("t_bias_kept")
        logits_done, logits_kept = sem("logits_done"), sem("logits_kept")
        logits_turned, scored, routed = sem("logits_turned"), sem("scored"), sem("routed")
        gates_turned, gates_kept, step = sem("gates_turned"), sem("gates_kept"), sem("route_step")
        x_v = x.rearrange("b (i a p) d -> (b i) p a d", a=TT, p=P)
        half_tiles = TILES // 2
        scores_p = small_t[:, :, :, :].rearrange("p a b c -> p (a b c)")

        with nc.Block() as block:
            @block.sync
            def _(sp):
                sp.dma_start(small[0:E, 0, :], router_w).then_inc(small_loaded, 16)
                sp.dma_start(small[0:E, 1, :], router_t_w).then_inc(small_loaded, 16)
                sp.dma_start(small[0:B, 2, :], cond).then_inc(small_loaded, 16)
                sp.dma_start(bias[:, 0, :], router_bias.partition_broadcast(P)).then_inc(small_loaded, 16)
                for q in range(2):
                    sp.dma_start(x_rows[q][:], x_v[q]).then_inc(x_loaded[q], 16)
                    sp.sem_inc(x_stored[q], 16)
                with sp.Fori(0, half_tiles) as pair:
                    for q in range(2):
                        sp.wait_ge(cols_v, 2 * (2 * pair + q) + 4)
                        sp.wait_ge(cols_a, 2 * (2 * pair + q) + 4)
                        sp.dma_start(x_rows[q][:], x_v[(2 * pair + (2 + q)) % TILES]).then_inc(x_loaded[q], 16)
                        sp.dma_start(g.x_t[2 * pair + q], x_cols[q][:]).then_inc(x_stored[q], 16)
                ahead(sp)
                for q in range(2):
                    sp.wait_ge(x_stored[q], 16 * (half_tiles + 1))
                    sp.wait_ge(x_loaded[q], 16 * (half_tiles + 1))

            @block.tensor
            def _(pe):
                pe.wait_ge(small_loaded, 64)
                for w, n in ((0, E), (1, E), (2, B)):
                    for k in range(KD):
                        last = nc.tensor.transpose(small_t[:, w, k, 0:n], small[0:n, w, k * P:(k + 1) * P],
                                                   g.ident[0:n, 0:n])
                last.then_inc(small_turned, 1)
                pe.wait_ge(small_kept, 3)
                for k in range(KD):
                    last = nc.tensor.matmul(logits_p[0][:, 0:B], router_t[:, k, 1, :], g.cond_t[:, k, :],
                                            start=k == 0, stop=k == KD - 1)
                last.then_inc(t_bias_done, 1)
                pe.wait_ge(t_bias_kept, 1)
                with pe.Fori(0, half_tiles) as pair:
                    for q in range(2):
                        tile = 2 * pair + q
                        pe.wait_ge(x_loaded[q], 16 * (pair + 1))
                        for a in range(TT):
                            if a == 0:
                                pe.wait_ge(cols_v, 2 * tile + 2)
                            if a == 2:
                                pe.wait_ge(cols_a, 2 * tile + 2)
                            for k in range(KD):
                                last = nc.tensor.transpose(turned[a][:, k, :], x_rows[q][:, a, k * P:(k + 1) * P],
                                                           g.ident[:])
                            last.then_inc(x_turned, 1)
                        pe.wait_ge(cols_v, 2 * tile + 4)
                        pe.wait_ge(cols_a, 2 * tile + 4)
                        pe.wait_ge(logits_kept, tile + 1)
                        for k in range(KD):
                            last = nc.tensor.matmul(logits_p[q][:], router_t[:, k, 0, :], x_cols[q][:, k, :],
                                                    start=k == 0, stop=k == KD - 1)
                        last.then_inc(logits_done, 1)
                pe.wait_ge(logits_kept, TILES + 2)
                for i in range(BLOCKS):
                    last = nc.tensor.transpose(turned[0][:, :, :].rearrange("p k q -> p (k q)")[:, i * E:(i + 1) * E],
                                               logits[:, i * P:(i + 1) * P], g.ident[0:E, 0:E])
                last.then_inc(logits_turned, 1)
                pe.wait_ge(routed, 1)
                for i in range(BLOCKS // 8):
                    if i >= 1:
                        pe.wait_ge(gates_kept, i)
                    for a in range(8):
                        last = nc.tensor.transpose(
                            gates_p[:, a * P:(a + 1) * P],
                            parts[:, 8 * i + a, :, :].rearrange("p q e -> p (q e)"), g.ident_b[:])
                    last.then_inc(gates_turned, 1)

            @block.scalar
            def _(act):
                act.sem_inc(cols_a, 2)
                nc.scalar.activation(score[:, 0, 0:1], g.ones[:, 0:1], ACT.Sigmoid)
                with act.Fori(0, half_tiles) as pair:
                    for q in range(2):
                        act.wait_ge(x_stored[q], 16 * (pair + 1))
                        for a in (2, 3):
                            act.wait_ge(x_turned, TT * (2 * pair + q) + a + 1)
                            nc.scalar.activation(x_cols[q][:, :, a * P:(a + 1) * P], turned[a][:], ACT.Copy
                                                 ).then_inc(cols_a, 1)
                act.wait_ge(logits_turned, 1)
                nc.scalar.activation(score[:].rearrange("p i e -> p (i e)"),
                                     turned[0][:, :, :].rearrange("p k q -> p (k q)")[:, 0:BLOCKS * E], ACT.Sigmoid
                                     ).then_inc(scored, 1)

            @block.vector
            def _(dve):
                dve.sem_inc(cols_v, 2)
                dve.sem_inc(logits_kept, 2)
                dve.wait_ge(small_turned, 1)
                for w in range(2):
                    nc.vector.tensor_copy(router_t[:, :, w, :], small_t[:, w, :, :]).then_inc(small_kept, 1)
                nc.vector.tensor_copy(g.cond_t[:], small_t[:, 2, :, 0:B]).then_inc(small_kept, 1)
                dve.wait_ge(t_bias_done, 1)
                nc.vector.tensor_copy(t_bias[:], logits_p[0][:, 0:B]).then_inc(t_bias_kept, 1)
                dve.wait_ge(t_bias_kept, 1)
                for b in range(B):
                    with dve.Fori(b * half_tiles // B, (b + 1) * half_tiles // B) as pair:
                        for q in range(2):
                            dve.wait_ge(x_stored[q], 16 * (pair + 1))
                            for a in (0, 1):
                                dve.wait_ge(x_turned, TT * (2 * pair + q) + a + 1)
                                nc.vector.tensor_copy(x_cols[q][:, :, a * P:(a + 1) * P], turned[a][:]
                                                      ).then_inc(cols_v, 1)
                            dve.wait_ge(logits_done, 2 * pair + q + 1)
                            nc.vector.tensor_scalar(logits[:, bass.ds((2 * pair + q) * TILE, TILE)], logits_p[q][:],
                                                    t_bias[:, b:b + 1], None, ALU.add).then_inc(logits_kept, 1)

                count = [0]

                def in_turn(ins):
                    count[0] += 1
                    ins.then_inc(step, 1)
                    dve.wait_ge(step, count[0])

                wide = lambda t: t[:, :, :].to_broadcast([P, BLOCKS, E])
                in_turn(nc.vector.memset(find[:], NONE))
                dve.wait_ge(scored, 1)
                in_turn(nc.vector.tensor_tensor(chosen[:], score[:], bias[:].to_broadcast([P, BLOCKS, E]), ALU.add))
                for i in range(BLOCKS - 1):
                    nc.vector.max(top[:, i, :], chosen[:, i, :])
                in_turn(nc.vector.max(top[:, BLOCKS - 1, :], chosen[:, BLOCKS - 1, :]))
                in_turn(nc.vector.tensor_copy(find[:, :, 0:TOP_K], top[:, :, 0:TOP_K]))
                for i in range(BLOCKS - 1):
                    nc.vector.match_replace(replaced[:, i, :], find[:, i, :], chosen[:, i, :], NONE)
                in_turn(nc.vector.match_replace(replaced[:, BLOCKS - 1, :], find[:, BLOCKS - 1, :],
                                                chosen[:, BLOCKS - 1, :], NONE))
                in_turn(nc.vector.tensor_tensor(mask[:], replaced[:], chosen[:], ALU.not_equal))
                in_turn(nc.vector.tensor_tensor(kept[:], mask[:], score[:], ALU.mult))
                in_turn(nc.vector.tensor_reduce(total[:, :, 0], kept[:], AX.X, ALU.add))
                in_turn(nc.vector.tensor_scalar(good[:], total[:], EPS, None, ALU.is_gt))
                in_turn(nc.vector.tensor_scalar(half[:], good[:], -1.0 / TOP_K, 1.0 / TOP_K, ALU.mult, ALU.add))
                in_turn(nc.vector.tensor_scalar(total[:], total[:], EPS, None, ALU.add))
                in_turn(nc.vector.reciprocal(inverse[:], total[:]))
                in_turn(nc.vector.tensor_tensor(inverse[:], inverse[:], good[:], ALU.mult))
                in_turn(nc.vector.tensor_tensor(kept[:], kept[:], wide(inverse), ALU.mult))
                in_turn(nc.vector.tensor_tensor(mask[:], mask[:], wide(half), ALU.mult))
                in_turn(nc.vector.tensor_tensor(gate[:], kept[:], mask[:], ALU.add))
                left = [gate, rest, gate]
                for q in range(PARTS):
                    last = nc.vector.tensor_copy(parts[:, :, q, :], left[q][:])
                    if q < PARTS - 1:
                        in_turn(last)
                        in_turn(nc.vector.tensor_tensor(left[q + 1][:], left[q][:], parts[:, :, q, :], ALU.subtract))
                last.then_inc(routed, 1)
                for i in range(BLOCKS // 8):
                    dve.wait_ge(gates_turned, i + 1)
                    nc.vector.tensor_copy(g.gates_t[:, i * 8 * P:(i + 1) * 8 * P], gates_p[:]
                                          ).then_inc(gates_kept, 1)


GROUP = 8
RAW = 16


def load_units(eng, raw, views, first, loaded):
    for u, view in enumerate(views, first):
        eng.dma_start(raw[:, u % RAW], view).then_inc(loaded[u // GROUP], 16)


def turned_weights(nc, g, raw, views, loaded, hi, lo, tag):
    with ExitStack() as ctx:
        sem = lambda n: ctx.enter_context(nc.semaphore(n + tag))
        banks = 8
        blocks = [ctx.enter_context(nc.psum_tensor(f"blocks{q}{tag}", [P, 4 * P], F32)) for q in range(banks)]
        turned, hi_done, lo_done = sem("raw_turned"), sem("hi_done"), sem("lo_done")
        units = range(len(views))

        with nc.Block() as block:
            @block.sync
            def _(sp):
                for u in units[RAW:]:
                    sp.wait_ge(turned, u - RAW + 1)
                    load_units(sp, raw, [views[u]], u, loaded)

            @block.tensor
            def _(pe):
                for u in units:
                    if u % GROUP == 0:
                        pe.wait_ge(loaded[u // GROUP], 16 * GROUP)
                    if u >= banks:
                        pe.wait_ge(lo_done, u - banks + 1)
                    for k in range(4):
                        last = nc.tensor.transpose(blocks[u % banks][:, k * P:(k + 1) * P], raw[:, u % RAW, k, :],
                                                   g.ident[:])
                    last.then_inc(turned, 1)

            @block.scalar
            def _(act):
                for u in units:
                    act.wait_ge(turned, u + 1)
                    nc.scalar.activation(hi[:, u, :], blocks[u % banks][:], ACT.Copy).then_inc(hi_done, 1)

            @block.vector
            def _(dve):
                for u in units:
                    dve.wait_ge(hi_done, u + 1)
                    nc.vector.tensor_tensor(lo[:, u, :], blocks[u % banks][:], hi[:, u, :].bitcast(F32),
                                            ALU.subtract).then_inc(lo_done, 1)


PLAIN = 2 * KD + 4


def experts(nc, g, hi, lo, plain, blocks, gated, ahead, tag):
    with ExitStack() as ctx:
        sb = lambda n, s, d=F32: ctx.enter_context(nc.sbuf_tensor(n + tag, s, d))
        ps = lambda n, s, d=F32: ctx.enter_context(nc.psum_tensor(n + tag, s, d))
        sem = lambda n: ctx.enter_context(nc.semaphore(n + tag))
        x_cols, base = plain[:, 0:KD], plain[:, KD:2 * KD]
        bent, hidden = [[plain[:, 2 * KD + 2 * t + q] for q in range(2)] for t in range(2)]
        x_hi, x_lo = sb("x_hi", [P, KD, TILE], F32R), sb("x_lo", [P, KD, TILE], F32R)
        table_in = sb("table_in", [P, 1])
        hid_hi = [sb(f"hid_hi{q}", [P, TILE], F32R) for q in range(2)]
        hid_lo = [sb(f"hid_lo{q}", [P, TILE], F32R) for q in range(2)]
        up = [ps(f"up{q}", [P, TILE]) for q in range(2)]
        factor = [ps(f"factor{q}", [P, TILE]) for q in range(2)]
        out = [ps(f"out{m}", [P, TILE]) for m in range(KD)]

        x_loaded, x_hi_done, x_split = sem("x_loaded"), sem("x_hi_done"), sem("x_split")
        up_done, factor_done = sem("up_done"), sem("factor_done")
        bent_done = sem("bent_done")
        product_done, hi_done, hid_split = sem("product_done"), sem("hid_hi_done"), sem("hid_split")
        hid_used = sem("hid_used")
        out_done = sem("out_done")
        out_kept = sem("out_kept")
        base_loaded = sem("base_loaded")
        base_stored = sem("base_stored")
        per = 1 if gated else HR // P

        down0 = 2 * blocks if gated else blocks

        with nc.Block() as block:
            @block.sync
            def _(sp):
                sp.dma_start(x_cols[:], g.x_t[0]).then_inc(x_loaded, 16)
                sp.sem_inc(base_stored, 16)
                ahead(sp)
                with sp.Fori(0, TILES) as i:
                    sp.wait_ge(base_stored, 16 * (i + 1))
                    sp.dma_start(base[:], (g.x_t if gated else g.shared)[i]).then_inc(base_loaded, 16)
                    sp.wait_ge(x_split, i + 1)
                    sp.dma_start(x_cols[:], g.x_t[(i + 1) % TILES]).then_inc(x_loaded, 16)
                    sp.wait_ge(out_kept, KD * (i + 2))
                    sp.dma_start((g.shared if gated else g.x1_t)[i], base[:]).then_inc(base_stored, 16)
                sp.wait_ge(base_stored, 16 * (TILES + 1))
                sp.wait_ge(x_loaded, 16 * (TILES + 1))

            @block.tensor
            def _(pe):
                pe.sem_inc(hid_used, 2)

                def product(to, slots, columns, first=True, last=True):
                    for k, (slot, col) in enumerate(slots):
                        a_hi, a_lo = hi[:, slot, col:col + P], lo[:, slot, col:col + P]
                        b_hi, b_lo = columns(k)
                        nc.tensor.matmul(to, a_hi, b_hi, start=first and k == 0, stop=False)
                        nc.tensor.matmul(to, a_hi, b_lo, start=False, stop=False)
                        ins = nc.tensor.matmul(to, a_lo, b_hi, start=False, stop=last and k == len(slots) - 1)
                    return ins

                x_at = lambda k: (x_hi[:, k, :], x_lo[:, k, :])

                def down(i, j):
                    pe.wait_ge(hid_split, blocks * i + j + 1)
                    if j == 0:
                        pe.wait_ge(out_kept, KD * (i + 1))
                    for m in range(KD):
                        ins = product(out[m][:], [(down0 + j, m * P)],
                                      lambda k: (hid_hi[j % 2][:], hid_lo[j % 2][:]), j == 0, j == blocks - 1)
                        if j == blocks - 1 and m < KD - 1:
                            ins.then_inc(out_done, 1)
                    ins.then_inc(hid_used, 1)

                with pe.Fori(0, TILES) as i:
                    pe.wait_ge(x_split, i + 1)
                    for j in range(blocks):
                        product(up[j % 2][:], [(j, k * P) for k in range(KD)], x_at).then_inc(up_done, 1)
                        if gated:
                            product(factor[j % 2][:], [(blocks + j, k * P) for k in range(KD)], x_at
                                    ).then_inc(factor_done, 1)
                        elif j % per == 0:
                            e = j // per
                            nc.tensor.matmul(factor[e % 2][:], g.select[:, e, :],
                                             g.gates_t[:, bass.ds(i * TILE, TILE)], start=True, stop=True
                                             ).then_inc(factor_done, 1)
                        if j >= 1:
                            down(i, j - 1)
                    down(i, blocks - 1)

            @block.scalar
            def _(act):
                def split(i):
                    act.wait_ge(x_loaded, 16 * (i + 1))
                    for k in range(KD):
                        nc.scalar.activation(x_hi[:, k, :], x_cols[:, k, :], ACT.Copy).then_inc(x_hi_done, 1)

                nc.scalar.activation(table_in[:], g.ones[:, 0:1], ACT.Silu if gated else ACT.Gelu)
                split(0)
                with act.Fori(0, TILES) as i:
                    for j in range(blocks):
                        act.wait_ge(up_done, blocks * i + j + 1)
                        nc.scalar.activation(bent[j % 2], up[j % 2][:], ACT.Silu if gated else ACT.Gelu
                                             ).then_inc(bent_done, 1)
                    act.wait_ge(factor_done if gated else up_done, blocks * (i + 1))
                    split(i + 1)

            @block.vector
            def _(dve):
                dve.sem_inc(out_kept, KD)

                def split(i):
                    for k in range(KD):
                        dve.wait_ge(x_hi_done, KD * i + k + 1)
                        ins = nc.vector.tensor_tensor(x_lo[:, k, :], x_cols[:, k, :], x_hi[:, k, :].bitcast(F32),
                                                      ALU.subtract)
                    ins.then_inc(x_split, 1)

                split(0)
                with dve.Fori(0, TILES) as i:
                    for j in range(blocks):
                        n = blocks * i + j + 1
                        dve.wait_ge(bent_done, n)
                        if j % per == 0:
                            dve.wait_ge(factor_done, (blocks // per) * i + j // per + 1)
                        dve.wait_ge(hid_used, n)
                        nc.vector.tensor_tensor(hidden[j % 2], bent[j % 2], factor[j // per % 2][:], ALU.mult
                                                ).then_inc(product_done, 1)
                        dve.wait_ge(product_done, n)
                        nc.vector.tensor_copy(hid_hi[j % 2][:], hidden[j % 2]).then_inc(hi_done, 1)
                        dve.wait_ge(hi_done, n)
                        nc.vector.tensor_tensor(hid_lo[j % 2][:], hidden[j % 2], hid_hi[j % 2][:].bitcast(F32),
                                                ALU.subtract).then_inc(hid_split, 1)
                    split(i + 1)
                    dve.wait_ge(base_loaded, 16 * (i + 1))
                    for m in range(KD):
                        if m < KD - 1:
                            dve.wait_ge(out_done, (KD - 1) * i + m + 1)
                        else:
                            dve.wait_ge(hid_used, blocks * (i + 1) + 2)
                        nc.vector.scalar_tensor_tensor(base[:, m, :], out[m][:], SCALE, base[:, m, :],
                                                       ALU.mult, ALU.add).then_inc(out_kept, 1)


def input_shares(nc, g, weights, steps, conds, biases):
    with ExitStack() as ctx:
        sem = lambda n: ctx.enter_context(nc.semaphore("in_" + n))
        sb = lambda n, s, d=F32: ctx.enter_context(nc.sbuf_tensor("in_" + n, s, d))
        ps = lambda n, s: ctx.enter_context(nc.psum_tensor("in_" + n, s, F32))
        w_raw = [sb(f"w{c}", [P, KD, D]) for c in range(3)]
        u_raw = w_raw
        bias, rows_sb = sb("bias", [1, 3, D]), sb("rows_sb", [B, 3, D])
        x1, table_in = sb("x1", [P, KD, TILE]), sb("table_in", [P, 1])
        x_hi, x_lo = [[sb(f"x_{n}{q}", [P, KD, TILE], F32R) for q in range(2)] for n in ("hi", "lo")]
        shares = sb("shares", [P, PER_TILE, 3, KD, CH])
        c_raw = shares[:].rearrange("p q c k t -> p (q c k t)").rearrange("p (c k n) -> p c k n", c=3, k=KD)
        z0, cand0 = [sb(n, [P, PER_TILE, KD, CH], F16) for n in ("z0", "cand0")]
        guess = sb("guess", [P, PER_TILE, 2, KD, CH + 1], F16)
        banks = 6
        bank = [ps(f"bank{q}", [P, PER_TILE, CH]) for q in range(banks)]
        rows, cols = ps("rows", [B, D]), ps("cols", [P, 3, KD, B])
        w_loaded, u_loaded, c_loaded = sem("w_loaded"), sem("u_loaded"), sem("c_loaded")
        w_hi_done, w_lo_done = sem("w_hi_done"), sem("w_lo_done")
        u_hi_done, u_rest_done = sem("u_hi_done"), sem("u_rest_done")
        rows_done, rows_kept, cols_done, cols_kept = sem("rows_done"), sem("rows_kept"), sem("cols_done"), sem("cols_kept")
        x1_loaded, x_hi_done, x_split = sem("x1_loaded"), sem("x_hi_done"), sem("x_split")
        sum_done = sem("sum_done")
        kept_a, kept_v = sem("kept_a"), sem("kept_v")
        stored = sem("stored")
        gates_done = sem("gates_done")
        cleared, gain_done = sem("cleared"), sem("gain_done")
        guess_stored = sem("guess_stored")
        by_block = lambda w: w.rearrange("(k p) n -> p k n", p=P)
        blocks = [(c, m) for c in range(3) for m in range(KD)]
        each = len(blocks) // 2

        with nc.Block() as block:
            @block.sync
            def _(sp):
                for c in range(3):
                    sp.dma_start(w_raw[c][:], by_block(weights[c])).then_inc(w_loaded, 16)
                sp.dma_start(x1[:], g.x1_t[0]).then_inc(x1_loaded, 16)
                for c in range(3):
                    sp.dma_start(c_raw[:, c], by_block(conds[c])).then_inc(c_loaded, 16)
                    sp.dma_start(bias[0:1, c, :], biases[c].rearrange("(a n) -> a n", a=1)).then_inc(c_loaded, 16)
                sp.sem_inc(stored, 3 * 16)
                sp.sem_inc(guess_stored, 16)
                sp.wait_ge(w_lo_done, 3)
                for c in range(3):
                    sp.dma_start(u_raw[c][:], by_block(steps[c])).then_inc(u_loaded, 16)
                with sp.Fori(0, TILES) as i:
                    sp.wait_ge(x_split, i + 1)
                    sp.dma_start(x1[:], g.x1_t[(i + 1) % TILES]).then_inc(x1_loaded, 16)
                    for c in range(3):
                        sp.wait_ge(kept_a, each * i + 2 * c + 5)
                        sp.wait_ge(kept_v, each * i + 2 * c + 5)
                        sp.dma_start(g.shares[i].rearrange("q p c k t -> c p q k t")[c], shares[:, :, c]
                                     ).then_inc(stored, 16)
                    sp.wait_ge(gain_done, i + 1)
                    sp.dma_start(g.guess[i].rearrange("q p a k t -> p q (a k t)"), guess[:].rearrange("p q a k t -> p q (a k t)")
                                 ).then_inc(guess_stored, 16)
                sp.wait_ge(stored, 3 * 16 * (TILES + 1))
                sp.wait_ge(guess_stored, 16 * (TILES + 1))
                sp.wait_ge(x1_loaded, 16 * (TILES + 1))

            @block.tensor
            def _(pe):
                pe.wait_ge(c_loaded, 6 * 16)
                for c in range(3):
                    if c >= 1:
                        pe.wait_ge(rows_kept, c)
                    for k in range(KD):
                        nc.tensor.matmul(rows[:], g.cond_t[:, k, :], c_raw[:, c, k, :], start=k == 0, stop=False)
                    nc.tensor.matmul(rows[:], g.ones[0:1, 0:B], bias[0:1, c, :], start=False, stop=True
                                     ).then_inc(rows_done, 1)
                pe.wait_ge(rows_kept, 3)
                for c, m in blocks:
                    last = nc.tensor.transpose(cols[:, c, m, :], rows_sb[:, c, m * P:(m + 1) * P], g.ident[0:B, 0:B])
                last.then_inc(cols_done, 1)
                pe.wait_ge(w_lo_done, 3)
                with pe.Fori(0, TILES // 2) as pair:
                    for q in range(2):
                        i = 2 * pair + q
                        pe.wait_ge(x_split, i + 1)
                        for n, (c, m) in enumerate(blocks):
                            pe.wait_ge(kept_a if n % 2 == 0 else kept_v, each * i + n // 2 + 1)
                            to, cut = bank[n % banks][:], slice(m * P, (m + 1) * P)
                            for k in range(KD):
                                nc.tensor.matmul(to, g.w_hi[:, c, k, cut], x_hi[q][:, k, :], start=k == 0, stop=False)
                                nc.tensor.matmul(to, g.w_hi[:, c, k, cut], x_lo[q][:, k, :], start=False, stop=False)
                                last = nc.tensor.matmul(to, g.w_lo[:, c, k, cut], x_hi[q][:, k, :], start=False,
                                                        stop=k == KD - 1)
                            last.then_inc(sum_done, 1)

            @block.scalar
            def _(act):
                act.sem_inc(kept_a, 3)
                act.sem_inc(gates_done, 3)
                nc.scalar.activation(table_in[:], g.ones[:, 0:1], ACT.Sigmoid)
                act.wait_ge(w_loaded, 3 * 16)
                for c in range(3):
                    nc.scalar.activation(g.w_hi[:, c, :, :], w_raw[c][:], ACT.Copy).then_inc(w_hi_done, 1)

                def split(i, q):
                    act.wait_ge(x1_loaded, 16 * (i + 1))
                    nc.scalar.activation(x_hi[q][:], x1[:], ACT.Copy).then_inc(x_hi_done, 1)

                split(0, 0)
                act.wait_ge(cols_kept, 1)
                for b in range(B):
                    with act.Fori(b * TILES // 4, (b + 1) * TILES // 4) as pair:
                        for q in range(2):
                            i = 2 * pair + q
                            for n, (c, m) in enumerate(blocks):
                                if n % 2:
                                    continue
                                act.wait_ge(sum_done, len(blocks) * i + n + 1)
                                act.wait_ge(stored, 3 * 16 * (i + 1))
                                if n in (KD, KD + 1):
                                    act.wait_ge(gates_done, 3 * (i + 1))
                                nc.scalar.activation(shares[:, :, c, m, :], bank[n % banks][:], ACT.Identity,
                                                     bias=g.gate_bias[:, c, m, b:b + 1]).then_inc(kept_a, 1)
                                if n == 0:
                                    split(i + 1, 1 - q)
                                if n == 2 * KD:
                                    act.wait_ge(kept_a, each * i + 7)
                                    act.wait_ge(kept_v, each * i + 7)
                                    act.wait_ge(guess_stored, 16 * (i + 1))
                                    nc.scalar.activation(z0[:], shares[:, :, Z], ACT.Sigmoid).then_inc(gates_done, 1)
                                    nc.scalar.activation(guess[:, :, 0, :, 1:CH + 1], shares[:, :, Z], ACT.Sigmoid,
                                                         scale=-1.0).then_inc(gates_done, 1)
                            act.wait_ge(kept_a, each * i + 9)
                            act.wait_ge(kept_v, each * i + 9)
                            nc.scalar.activation(cand0[:], shares[:, :, C], ACT.Tanh).then_inc(gates_done, 1)
                    if b == 0:
                        act.wait_ge(u_loaded, 3 * 16)
                        for c in range(3):
                            nc.scalar.activation(g.u_hi[:, c, :, :], u_raw[c][:], ACT.Copy).then_inc(u_hi_done, 1)
                for c in range(3):
                    act.wait_ge(u_rest_done, c + 1)
                    nc.scalar.activation(g.u_lo[:, c, :, :], u_raw[c][:], ACT.Copy, scale=LOW)

            @block.vector
            def _(dve):
                dve.sem_inc(kept_v, 3)
                nc.vector.memset(guess[:, :, :, :, 0:1], 0.0).then_inc(cleared, 1)
                for c in range(3):
                    dve.wait_ge(w_hi_done, c + 1)
                    nc.vector.tensor_tensor(g.w_lo[:, c, :, :], w_raw[c][:], g.w_hi[:, c, :, :].bitcast(F32),
                                            ALU.subtract).then_inc(w_lo_done, 1)
                for c in range(3):
                    dve.wait_ge(rows_done, c + 1)
                    nc.vector.tensor_copy(rows_sb[:, c, :], rows[:]).then_inc(rows_kept, 1)

                def split(i, q):
                    dve.wait_ge(x_hi_done, i + 1)
                    nc.vector.tensor_tensor(x_lo[q][:], x1[:], x_hi[q][:].bitcast(F32), ALU.subtract
                                            ).then_inc(x_split, 1)

                split(0, 0)
                dve.wait_ge(cols_done, 1)
                nc.vector.tensor_copy(g.gate_bias[:], cols[:]).then_inc(cols_kept, 1)
                dve.wait_ge(cols_kept, 1)
                for b in range(B):
                    with dve.Fori(b * TILES // 4, (b + 1) * TILES // 4) as pair:
                        for q in range(2):
                            i = 2 * pair + q
                            for n, (c, m) in enumerate(blocks):
                                if n % 2 == 0:
                                    continue
                                dve.wait_ge(sum_done, len(blocks) * i + n + 1)
                                dve.wait_ge(stored, 3 * 16 * (i + 1))
                                if n in (KD, KD + 1):
                                    dve.wait_ge(gates_done, 3 * (i + 1))
                                nc.vector.tensor_scalar(shares[:, :, c, m, :], bank[n % banks][:],
                                                        g.gate_bias[:, c, m, b:b + 1], None, ALU.add
                                                        ).then_inc(kept_v, 1)
                                if n == 1:
                                    split(i + 1, 1 - q)
                            dve.wait_ge(gates_done, 3 * (i + 2))
                            nc.vector.tensor_tensor(guess[:, :, 1, :, 1:CH + 1], z0[:], cand0[:], ALU.mult
                                                    ).then_inc(gain_done, 1)
                    if b == 0:
                        for c in range(3):
                            dve.wait_ge(u_hi_done, c + 1)
                            nc.vector.tensor_tensor(u_raw[c][:], u_raw[c][:], g.u_hi[:, c, :, :], ALU.subtract
                                                    ).then_inc(u_rest_done, 1)


def gru(nc, g, out):
    with ExitStack() as ctx:
        sb = lambda n, s, d=F32: [ctx.enter_context(nc.sbuf_tensor(f"{n}_b{b}", s, d)) for b in range(B)]
        sem = lambda n: [ctx.enter_context(nc.semaphore(f"{n}_b{b}")) for b in range(B)]
        flat = [P, KD, CH]
        long = [P, KD, CH + 1]
        share_in, guess, x_add = sb("share_in", [P, 3, KD, CH]), sb("guess_in", [P, 2, KD, CH + 1], F16), sb("x_add", flat)
        h, keep, gain, h_guess = sb("h", long), sb("keep", long), sb("gain", long), sb("h_guess", long)
        r, z, cand, rh = sb("r", flat), sb("z", flat), sb("cand", flat), sb("rh", flat)
        h_sent, rh_sent = sb("h_sent", flat), sb("rh_sent", flat)
        h_head, rh_head = sb("h_head", flat, F16), sb("rh_head", flat, F16)
        h_step, rh_step = sb("h_step", flat, F16), sb("rh_step", flat, F16)
        h_fine, rh_fine = sb("h_fine", flat, F16), sb("rh_fine", flat, F16)
        change, square = sb("change", flat), sb("square", [P, CHECKS, KD, CH])
        y, y_rows = sb("y", flat), sb("y_rows", [P, D])
        bank = [[ctx.enter_context(nc.psum_tensor(f"gate{c}_b{b}", flat, F32)) for c in range(3)] for b in range(B)]
        y_turned = [ctx.enter_context(nc.psum_tensor(f"y_turned_b{b}", [P, D], F32)) for b in range(B)]

        share_loaded, guess_loaded, x_add_loaded = sem("share_loaded"), sem("guess_loaded"), sem("x_add_loaded")
        seeded = sem("seeded")
        cleared, start_done, h_guess_done = sem("cleared"), sem("start_done"), sem("h_guess_done")
        h_step_done, rh_step_done = sem("h_step_done"), sem("rh_step_done")
        r_sum, z_sum, c_sum = sem("r_sum"), sem("z_sum"), sem("c_sum")
        r_done, z_done, keep_done, cand_done = sem("r_done"), sem("z_done"), sem("keep_done"), sem("cand_done")
        gain_done, h_done = sem("gain_done"), sem("h_done")
        rh_done, h_sent_done = sem("rh_done"), sem("h_sent_done")
        rh_sent_done = sem("rh_sent_done")
        h_fine_done, rh_fine_done = sem("h_fine_done"), sem("rh_fine_done")
        h_squared, rh_squared = sem("h_squared"), sem("rh_squared")
        change_done, change_squared = sem("change_done"), sem("change_squared")
        y_done, y_turn_done, y_kept = sem("y_done"), sem("y_turn_done"), sem("y_kept")
        y_stored = sem("y_stored")
        table_in = ctx.enter_context(nc.sbuf_tensor("table_warmed", [P, 1], F32))
        banks_taken = ctx.enter_context(nc.semaphore("banks_taken"))

        shares, guesses = [t.rearrange("i q p c k t -> (i q) p c k t") for t in (g.shares, g.guess)]
        streams = range(B)
        before = lambda t: t[:, :, 0:CH]
        after = lambda t: t[:, :, 1:CH + 1]
        line = lambda t: t[:].rearrange("p k t -> p (k t)")

        def all_turns(eng, turn):
            turn(0, 0, None)
            with eng.Fori(0, CHUNKS) as c:
                for k in range(1, TURNS):
                    turn(c, k, None)
                turn(c + 1, 0, c)

        with nc.Block() as block:
            @block.sync
            def _(sp):
                for b in streams:
                    sp.sem_inc(y_stored[b], 16)
                    sp.dma_start(share_in[b][:], shares[b * CHUNKS]).then_inc(share_loaded[b], 16)
                    sp.dma_start(guess[b][:], guesses[b * CHUNKS]).then_inc(guess_loaded[b], 16)
                with sp.Fori(0, CHUNKS // PER_TILE) as i, sp.Fori(0, PER_TILE) as q:
                    c = i * PER_TILE + q
                    after_c = (c + 1) % CHUNKS
                    for b in streams:
                        sp.wait_ge(seeded[b], 3 * (c + 1))
                        sp.dma_start(share_in[b][:], shares[b * CHUNKS + after_c]).then_inc(share_loaded[b], 16)
                        sp.wait_ge(h_guess_done[b], c + 1)
                        sp.dma_start(guess[b][:], guesses[b * CHUNKS + after_c]).then_inc(guess_loaded[b], 16)
                        sp.wait_ge(y_done[b], c + 1)
                        sp.dma_start(x_add[b][:], g.x1_t[b * (TILES // B) + i]
                                     [:, :, bass.ds(q * CH, CH)]).then_inc(x_add_loaded[b], 16)
                    for b in streams:
                        sp.wait_ge(y_kept[b], c + 2)
                        sp.dma_start(out[b, bass.ds(c * CH, CH), :], y_rows[b][:]).then_inc(y_stored[b], 16)
                for b in streams:
                    sp.wait_ge(y_stored[b], 16 * (CHUNKS + 1))
                    sp.wait_ge(share_loaded[b], 16 * (CHUNKS + 1))
                    sp.wait_ge(guess_loaded[b], 16 * (CHUNKS + 1))

            @block.tensor
            def _(pe):
                for b in streams:
                    pe.sem_inc(y_turn_done[b], 1)
                    for c in range(3):
                        for k in range(KD):
                            ins = nc.tensor.matmul(bank[b][c][:, k, :], g.ident[:], g.ones[:], start=k == 0,
                                                   stop=k == KD - 1, skip_group_check=True)
                ins.then_inc(banks_taken, 1)

                def add(to, weights, columns):
                    for m in range(KD):
                        for k in range(KD):
                            ins = nc.tensor.matmul(to[:, m, :], weights[:, k, m * P:(m + 1) * P], columns[:, k, :],
                                                   start=False, stop=m == KD - 1 and k == KD - 1,
                                                   skip_group_check=True)
                    return ins

                def turn(c, k, y_of):
                    n = c * TURNS + k

                    def total(b, gate, done):
                        if k == 0:
                            pe.wait_ge(seeded[b], 3 * c + gate + 1)
                        if gate == C:
                            pe.wait_ge(rh_step_done[b], n + 1)
                            step, fine, fine_done = rh_head[b] if k == 0 else rh_step[b], rh_fine[b], rh_fine_done[b]
                        else:
                            pe.wait_ge(h_step_done[b], n + 1)
                            step, fine, fine_done = h_head[b] if k == 0 else h_step[b], h_fine[b], h_fine_done[b]
                        ins = add(bank[b][gate], g.u_hi[:, gate], step)
                        if k == FINE:
                            pe.wait_ge(fine_done, c + 1)
                            ins = add(bank[b][gate], g.u_lo[:, gate], fine)
                        ins.then_inc(done[b], 1)

                    total(0, R, r_sum)
                    total(0, Z, z_sum)
                    total(1, R, r_sum)
                    total(0, C, c_sum)
                    total(1, Z, z_sum)
                    total(1, C, c_sum)
                    if y_of is not None:
                        for b in streams:
                            pe.wait_ge(y_done[b], y_of + 2)
                            pe.wait_ge(y_kept[b], y_of + 1)
                            for k in range(KD):
                                ins = nc.tensor.transpose(y_turned[b][:, k * P:(k + 1) * P], y[b][:, k, :], g.ident[:])
                            ins.then_inc(y_turn_done[b], 1)

                all_turns(pe, turn)

            @block.scalar
            def _(act):
                for b in streams:
                    act.sem_inc(h_squared[b], LATE)
                    act.sem_inc(rh_squared[b], LATE)
                    act.sem_inc(change_squared[b], 1)
                    act.sem_inc(y_kept[b], 1)
                nc.scalar.activation(table_in[:], g.ones[:, 0:1], ACT.Sigmoid)

                def seed(b, gate, c):
                    act.wait_ge(share_loaded[b], 16 * (c + 1))
                    nc.scalar.activation(bank[b][gate][:], share_in[b][:, gate], ACT.Copy).then_inc(seeded[b], 1)

                def sum_squares(b, what, kind, c):
                    return nc.scalar.activation(square[b][:, kind], what, ACT.Square,
                                                accum_out=g.left[:, kind, b, bass.ds(c, 1)])

                def turn(c, k, y_of):
                    n = c * TURNS + k
                    last, late = k == TURNS - 1, k - FINE - 1

                    def fine_h(b):
                        if k == FINE:
                            act.wait_ge(h_done[b], n)
                            nc.scalar.activation(h_fine[b][:], before(h[b]), ACT.Copy, scale=1 / LOW
                                                 ).then_inc(h_fine_done[b], 1)

                    def fine_rh(b):
                        if k == FINE:
                            act.wait_ge(rh_done[b], c * (TURNS - 1) + k)
                            nc.scalar.activation(rh_fine[b][:], rh[b][:], ACT.Copy, scale=1 / LOW
                                                 ).then_inc(rh_fine_done[b], 1)

                    def reset_gate(b):
                        act.wait_ge(r_sum[b], n + 1)
                        nc.scalar.activation(r[b][:], bank[b][R][:], ACT.Sigmoid).then_inc(r_done[b], 1)

                    def update_gate(b):
                        act.wait_ge(z_sum[b], n + 1)
                        nc.scalar.activation(z[b][:], bank[b][Z][:], ACT.Sigmoid).then_inc(z_done[b], 1)
                        nc.scalar.activation(after(keep[b]), bank[b][Z][:], ACT.Sigmoid, scale=-1.0
                                             ).then_inc(keep_done[b], 1)

                    def candidate(b):
                        act.wait_ge(c_sum[b], n + 1)
                        nc.scalar.activation(cand[b][:], bank[b][C][:], ACT.Tanh).then_inc(cand_done[b], 1)

                    def late_h(b):
                        if late >= 0:
                            act.wait_ge(h_step_done[b], n + 1)
                            sum_squares(b, h_step[b][:], 2 * late, c).then_inc(h_squared[b], 1)

                    def late_rh(b):
                        if late >= 0:
                            act.wait_ge(rh_step_done[b], n + 1)
                            sum_squares(b, rh_step[b][:], 2 * late + 1, c).then_inc(rh_squared[b], 1)

                    fine_h(0)
                    late_h(0)
                    reset_gate(0)
                    update_gate(0)
                    fine_h(1)
                    reset_gate(1)
                    fine_rh(0)
                    if last:
                        act.wait_ge(r_done[0], n + 1)
                        seed(0, R, c + 1)
                    candidate(0)
                    update_gate(1)
                    fine_rh(1)
                    candidate(1)
                    if last:
                        act.wait_ge(cand_done[1], n + 1)
                        for b, gate in ((0, Z), (1, R), (0, C), (1, Z), (1, C)):
                            seed(b, gate, c + 1)
                    late_h(1)
                    for b in streams:
                        late_rh(b)
                    if y_of is not None:
                        for b in streams:
                            act.wait_ge(change_done[b], y_of + 2)
                            sum_squares(b, change[b][:], CHECKS - 1, y_of).then_inc(change_squared[b], 1)
                            act.wait_ge(y_turn_done[b], y_of + 2)
                            act.wait_ge(y_stored[b], 16 * (y_of + 1))
                            nc.scalar.activation(y_rows[b][:], y_turned[b][:], ACT.Copy).then_inc(y_kept[b], 1)

                act.wait_ge(banks_taken, 1)
                for gate in range(3):
                    for b in streams:
                        seed(b, gate, 0)
                all_turns(act, turn)

            @block.gpsimd
            def _(pool):
                for b in streams:
                    pool.sem_inc(y_done[b], 1)
                    pool.sem_inc(change_done[b], 1)

                def turn(c, k, y_of):
                    n = c * TURNS + k
                    if k >= 1:
                        for b in streams:
                            pool.wait_ge(h_step_done[b], n + 1)
                            if k == 1:
                                pool.wait_ge(change_done[b], c + 1)
                            else:
                                pool.wait_ge(h_sent_done[b], c * (TURNS - 1) + k - 1)
                            nc.gpsimd.tensor_tensor(h_sent[b][:], (h_head if k == 1 else h_sent)[b][:], h_step[b][:],
                                                    ALU.add).then_inc(h_sent_done[b], 1)
                        if k < TURNS - 1:
                            for b in streams:
                                pool.wait_ge(rh_step_done[b], n + 1)
                                if k > 1:
                                    pool.wait_ge(rh_sent_done[b], c * (TURNS - 2) + k - 1)
                                nc.gpsimd.tensor_tensor(rh_sent[b][:], (rh_head if k == 1 else rh_sent)[b][:],
                                                        rh_step[b][:], ALU.add).then_inc(rh_sent_done[b], 1)
                    if k == TURNS - 1:
                        for b in streams:
                            pool.wait_ge(h_done[b], n + 1)
                            pool.wait_ge(x_add_loaded[b], 16 * (c + 1))
                            pool.wait_ge(y_turn_done[b], c + 1)
                            nc.gpsimd.tensor_tensor(y[b][:], x_add[b][:], after(h[b]), ALU.add).then_inc(y_done[b], 1)
                            pool.wait_ge(h_sent_done[b], (TURNS - 1) * (c + 1))
                            pool.wait_ge(change_squared[b], c + 1)
                            nc.gpsimd.tensor_tensor(change[b][:], before(h[b]), h_sent[b][:], ALU.subtract
                                                    ).then_inc(change_done[b], 1)

                all_turns(pool, turn)

            @block.vector
            def _(dve):
                for b in streams:
                    nc.vector.memset(h[b][:], 0.0).then_inc(cleared[b], 1)
                    nc.vector.memset(keep[b][:, :, 0:1], 0.0).then_inc(cleared[b], 1)
                    dve.wait_ge(cleared[b], 2)

                def begin(b, c):
                    last = h[b][:, :, CH:CH + 1]
                    dve.wait_ge(guess_loaded[b], 16 * (c + 1))
                    nc.vector.tensor_copy(guess[b][:, 1, :, 0:1], last).then_inc(start_done[b], 1)
                    nc.vector.tensor_copy(gain[b][:, :, 0:1], last).then_inc(start_done[b], 1)
                    dve.wait_ge(start_done[b], 2 * (c + 1))
                    nc.vector.tensor_tensor_scan(line(h_guess[b]), guess[b][:, 0].rearrange("p k t -> p (k t)"),
                                                 guess[b][:, 1].rearrange("p k t -> p (k t)"), 0.0,
                                                 ALU.mult, ALU.add).then_inc(h_guess_done[b], 1)
                    dve.wait_ge(h_guess_done[b], c + 1)
                    nc.vector.tensor_copy(h_head[b][:], before(h_guess[b])).then_inc(h_step_done[b], 1)

                def turn(c, k, y_of):
                    n = c * TURNS + k
                    for b in streams:
                        dve.wait_ge(r_done[b], n + 1)
                        if k == 0:
                            nc.vector.tensor_tensor(rh_head[b][:], r[b][:], before(h_guess[b]), ALU.mult
                                                    ).then_inc(rh_step_done[b], 1)
                            continue
                        nc.vector.tensor_tensor(rh[b][:], r[b][:], before(h[b]), ALU.mult).then_inc(rh_done[b], 1)
                        dve.wait_ge(rh_done[b], c * (TURNS - 1) + k)
                        if k > 1:
                            dve.wait_ge(rh_sent_done[b], c * (TURNS - 2) + k - 1)
                        if k == 1 or k > FINE + 1:
                            dve.wait_ge(rh_squared[b], LATE * (c + 1) + max(k - FINE - 1, 0))
                        nc.vector.tensor_tensor(rh_step[b][:], rh[b][:], (rh_head if k == 1 else rh_sent)[b][:],
                                                ALU.subtract).then_inc(rh_step_done[b], 1)
                    for b in streams:
                        dve.wait_ge(cand_done[b], n + 1)
                        nc.vector.tensor_tensor(after(gain[b]), z[b][:], cand[b][:], ALU.mult
                                                ).then_inc(gain_done[b], 1)
                        dve.wait_ge(gain_done[b], n + 1)
                        if k == 0:
                            dve.wait_ge(change_done[b], c + 1)
                        nc.vector.tensor_tensor_scan(line(h[b]), line(keep[b]), line(gain[b]), 0.0,
                                                     ALU.mult, ALU.add).then_inc(h_done[b], 1)
                        dve.wait_ge(h_done[b], n + 1)
                        if k == TURNS - 1:
                            begin(b, c + 1)
                            continue
                        if k > 0:
                            dve.wait_ge(h_sent_done[b], c * (TURNS - 1) + k)
                        if k == 0 or k > FINE:
                            dve.wait_ge(h_squared[b], LATE * (c + 1) + max(k - FINE, 0))
                        nc.vector.tensor_tensor(h_step[b][:], before(h[b]), (h_head if k == 0 else h_sent)[b][:],
                                                ALU.subtract).then_inc(h_step_done[b], 1)

                for b in streams:
                    begin(b, 0)
                all_turns(dve, turn)


def all_settled(nc, g):
    with ExitStack() as ctx:
        below = ctx.enter_context(nc.sbuf_tensor("below", [P, CHECKS, B, CHUNKS], F32))
        count = ctx.enter_context(nc.sbuf_tensor("count", [P, 1], F32))
        number = ctx.enter_context(nc.psum_tensor("number", [1, 1], F32))
        compared, counted, summed = [ctx.enter_context(nc.semaphore(n)) for n in ("compared", "counted", "summed")]
        with nc.Block() as block:
            @block.vector
            def _(dve):
                for kind in range(CHECKS):
                    nc.vector.tensor_scalar(below[:, kind], g.left[:, kind], BOUNDS[kind], None, ALU.is_le
                                            ).then_inc(compared, 1)
                dve.wait_ge(compared, CHECKS)
                nc.vector.tensor_reduce(count[:], below[:].rearrange("p a b c -> p (a b c)"), AX.X, ALU.add
                                        ).then_inc(counted, 1)
                dve.wait_ge(summed, 1)
                nc.vector.tensor_scalar(g.settled[:], number[:], float(P * CHECKS * B * CHUNKS), None, ALU.is_equal)

            @block.tensor
            def _(pe):
                pe.wait_ge(counted, 1)
                nc.tensor.matmul(number[:], count[:], g.ones[:, 0:1], start=True, stop=True).then_inc(summed, 1)


def step_by_step(nc, g, steps, out):
    with ExitStack() as ctx:
        sb = lambda n, s, d=F32: ctx.enter_context(nc.sbuf_tensor("st_" + n, s, d))
        ps = lambda n, s: ctx.enter_context(nc.psum_tensor("st_" + n, s, F32))
        sem = lambda n: ctx.enter_context(nc.semaphore("st_" + n))
        flat = [P, B, KD, CH]
        shares = g.shares.rearrange("i q p c k t -> (i q) p c k t")
        x_in = sb("x_in", flat)
        share = sb("share", [P, 3, B, KD, CH])
        states, y, y_rows = sb("states", flat), sb("y", flat), sb("y_rows", [P, B, D])
        u = [sb(f"u{c}", [P, KD, D]) for c in range(3)]
        h, rh, keep, cand = [sb(n, [P, B, KD]) for n in ("h", "rh", "keep", "cand")]
        sums, gates = sb("sums", [P, 3, B, KD]), sb("gates", [P, 2, B, KD])
        kept, gain = sb("kept", [P, B, KD]), sb("gain", [P, B, KD])
        of_h, of_rh, y_turned = ps("of_h", [P, 2, B, KD]), ps("of_rh", [P, B, KD]), ps("y_turned", [P, D])
        u_loaded, x_loaded, share_loaded = sem("u_loaded"), sem("x_loaded"), sem("share_loaded")
        h_done = sem("h_done")
        of_h_done, rz_sum, rz_done, keep_done, rh_done = [
            sem(n) for n in ("of_h_done", "rz_sum", "rz_done", "keep_done", "rh_done")]
        of_rh_done, c_sum, cand_done, parts_done = [sem(n) for n in ("of_rh_done", "c_sum", "cand_done", "parts_done")]
        state_kept, y_done, y_turn_done, y_kept, y_stored = [
            sem(n) for n in ("state_kept", "y_done", "y_turn_done", "y_kept", "y_stored")]

        def where_unsettled(eng, run):
            settled = eng.value_load(g.settled[0:1, 0:1], min_val=0, max_val=1)
            with eng.If(settled == 0):
                run()
            with eng.Else():
                eng.nop()

        with nc.Block() as block:
            @block.sync
            def _(sp):
                def run():
                    sp.sem_inc(y_stored, 16 * B)
                    for c in range(3):
                        sp.dma_start(u[c][:], steps[c].rearrange("(k p) n -> p k n", p=P)).then_inc(u_loaded, 16)
                    with sp.Fori(0, CHUNKS // PER_TILE) as i, sp.Fori(0, PER_TILE) as q:
                        c = i * PER_TILE + q
                        for b in range(B):
                            sp.dma_start(share[:, :, b], shares[b * CHUNKS + c]).then_inc(share_loaded, 16)
                            sp.dma_start(x_in[:, b], g.x1_t[b * (TILES // B) + i]
                                         [:, :, bass.ds(q * CH, CH)]).then_inc(x_loaded, 16)
                        for b in range(B):
                            sp.wait_ge(y_kept, B * c + b + 1)
                            sp.dma_start(out[b, bass.ds(c * CH, CH), :], y_rows[:, b]).then_inc(y_stored, 16)
                    sp.wait_ge(y_stored, 16 * B * (CHUNKS + 1))
                where_unsettled(sp, run)

            @block.tensor
            def _(pe):
                def add(to, weights, columns):
                    for m in range(KD):
                        for k in range(KD):
                            ins = nc.tensor.matmul(to[:, :, m], weights[:, k, m * P:(m + 1) * P], columns[:, :, k],
                                                   start=k == 0, stop=k == KD - 1)
                    return ins

                def run():
                    pe.wait_ge(u_loaded, 3 * 16)
                    with pe.Fori(0, CHUNKS) as c:
                        with pe.Fori(0, CH) as t:
                            n = c * CH + t + 1
                            pe.wait_ge(h_done, n)
                            for gate in (R, Z):
                                ins = add(of_h[:, gate], u[gate], h)
                            ins.then_inc(of_h_done, 1)
                            pe.wait_ge(rh_done, n)
                            add(of_rh, u[C], rh).then_inc(of_rh_done, 1)
                        pe.wait_ge(y_done, c + 1)
                        for b in range(B):
                            if b == 1:
                                pe.wait_ge(y_kept, B * c + 1)
                            for k in range(KD):
                                ins = nc.tensor.transpose(y_turned[:, k * P:(k + 1) * P], y[:, b, k, :], g.ident[:])
                            ins.then_inc(y_turn_done, 1)
                where_unsettled(pe, run)

            @block.scalar
            def _(act):
                def run():
                    with act.Fori(0, CHUNKS) as c:
                        with act.Fori(0, CH) as t:
                            n = c * CH + t + 1
                            act.wait_ge(rz_sum, n)
                            nc.scalar.activation(gates[:], sums[:, 0:2], ACT.Sigmoid).then_inc(rz_done, 1)
                            nc.scalar.activation(keep[:], sums[:, Z], ACT.Sigmoid, scale=-1.0).then_inc(keep_done, 1)
                            act.wait_ge(c_sum, n)
                            nc.scalar.activation(cand[:], sums[:, C], ACT.Tanh).then_inc(cand_done, 1)
                        for b in range(B):
                            act.wait_ge(y_turn_done, B * c + b + 1)
                            act.wait_ge(y_stored, 16 * B * (c + 1))
                            nc.scalar.activation(y_rows[:, b], y_turned[:], ACT.Copy).then_inc(y_kept, 1)
                where_unsettled(act, run)

            @block.gpsimd
            def _(pool):
                pool.nop()

            @block.vector
            def _(dve):
                def run():
                    nc.vector.memset(h[:], 0.0).then_inc(h_done, 1)
                    with dve.Fori(0, CHUNKS) as c:
                        with dve.Fori(0, CH) as t:
                            n = c * CH + t + 1
                            at = bass.ds(t, 1)
                            dve.wait_ge(share_loaded, 16 * B * (c + 1))
                            dve.wait_ge(of_h_done, n)
                            for gate in (R, Z):
                                ins = nc.vector.tensor_tensor(sums[:, gate], of_h[:, gate],
                                                              share[:, gate, :, :, at].rearrange("p b k t -> p b (k t)"),
                                                              ALU.add)
                            ins.then_inc(rz_sum, 1)
                            dve.wait_ge(rz_done, n)
                            nc.vector.tensor_tensor(rh[:], gates[:, R], h[:], ALU.mult).then_inc(rh_done, 1)
                            dve.wait_ge(keep_done, n)
                            nc.vector.tensor_tensor(kept[:], keep[:], h[:], ALU.mult).then_inc(parts_done, 1)
                            dve.wait_ge(of_rh_done, n)
                            nc.vector.tensor_tensor(sums[:, C], of_rh[:],
                                                    share[:, C, :, :, at].rearrange("p b k t -> p b (k t)"), ALU.add
                                                    ).then_inc(c_sum, 1)
                            dve.wait_ge(cand_done, n)
                            nc.vector.tensor_tensor(gain[:], gates[:, Z], cand[:], ALU.mult).then_inc(parts_done, 1)
                            dve.wait_ge(parts_done, 2 * n)
                            nc.vector.tensor_tensor(h[:], kept[:], gain[:], ALU.add).then_inc(h_done, 1)
                            dve.wait_ge(h_done, n + 1)
                            nc.vector.tensor_copy(states[:, :, :, at].rearrange("p b k t -> p b (k t)"), h[:]
                                                  ).then_inc(state_kept, 1)
                        dve.wait_ge(state_kept, CH * (c + 1))
                        dve.wait_ge(x_loaded, 16 * B * (c + 1))
                        nc.vector.tensor_tensor(y[:], x_in[:], states[:], ALU.add).then_inc(y_done, 1)
                where_unsettled(dve, run)


def build(nc, x, cond, router_w, router_t_w, router_bias, sw1, sw3, sw2, rw1, rw2,
          w_z, u_z, c_z, b_z, w_r, u_r, c_r, b_r, w_c, u_c, c_c, b_c, out):
    g = Shared()
    dram = lambda n, s, d=F32: nc.dram_tensor(n, s, d, kind="Internal").ap()
    g.x_t, g.shared, g.x1_t = [dram(n, [TILES, P, KD, TILE]) for n in ("x_t", "shared_t", "x1_t")]
    g.shares = dram("input_shares", [TILES, PER_TILE, P, 3, KD, CH])
    g.guess = dram("first_guess", [TILES, PER_TILE, P, 2, KD, CH + 1], F16)
    rows4 = lambda w, j: w[j * P:(j + 1) * P, :].rearrange("p (k q) -> p k q", q=P)
    cols4 = lambda w, j: w[:, j * P:(j + 1) * P].rearrange("(k p) q -> p k q", p=P)
    n_s, n_r, per = HS // P, E * HR // P, HR // P
    up = rw1.rearrange("e h d -> (e h) d")
    down = rw2.rearrange("e (k p) (j q) -> e j p k q", p=P, q=P)
    shared_units = ([rows4(sw1, j) for j in range(n_s)] + [rows4(sw3, j) for j in range(n_s)]
                    + [cols4(sw2, j) for j in range(n_s)])
    routed_units = [rows4(up, j) for j in range(n_r)] + [down[j // per, j % per] for j in range(n_r)]
    with ExitStack() as ctx:
        sb = lambda n, s, d, to=ctx: to.enter_context(nc.sbuf_tensor(n, s, d))
        loaded_s, loaded_r = [[ctx.enter_context(nc.semaphore(f"units_{t}{i}")) for i in range(len(u) // GROUP)]
                              for t, u in (("s", shared_units), ("r", routed_units))]
        constants(nc, ctx, g)
        with ExitStack() as raw_space:
            raw = sb("raw_units", [P, RAW, KD, P], F32, raw_space)
            tokens(nc, g, x, cond, router_w, router_t_w, router_bias,
                   lambda eng: load_units(eng, raw, shared_units[:RAW], 0, loaded_s))
            with ExitStack() as weights:
                hi, lo = [sb(f"shared_{s}", [P, len(shared_units), D], F32R, weights) for s in ("hi", "lo")]
                plain = sb("plain", [P, PLAIN, TILE], F32, weights)
                turned_weights(nc, g, raw, shared_units, loaded_s, hi, lo, "_s")
                experts(nc, g, hi, lo, plain, n_s, True,
                        lambda eng: load_units(eng, raw, routed_units[:RAW], 0, loaded_r), "_s")
            with ExitStack() as weights:
                hi, lo = [sb(f"routed_{s}", [P, len(routed_units), D], F32R, weights) for s in ("hi", "lo")]
                turned_weights(nc, g, raw, routed_units, loaded_r, hi, lo, "_r")
                plain = raw[:].rearrange("p u k q -> p u (k q)")
                experts(nc, g, hi, lo, plain, n_r, False, lambda eng: None, "_r")
        g.gate_bias = sb("gate_bias", [P, 3, KD, B], F32)
        g.u_hi, g.u_lo = [sb(f"u_{s}", [P, 3, KD, D], F16) for s in ("hi", "lo")]
        g.left = sb("left", [P, CHECKS, B, CHUNKS], F32)
        g.settled = sb("settled", [1, 1], I32)
        with ExitStack() as weights:
            g.w_hi, g.w_lo = [sb(f"w_{s}", [P, 3, KD, D], F32R, weights) for s in ("hi", "lo")]
            input_shares(nc, g, (w_r, w_z, w_c), (u_r, u_z, u_c), (c_r, c_z, c_c), (b_r, b_z, b_c))
        gru(nc, g, out)
        all_settled(nc, g)
        step_by_step(nc, g, (u_r, u_z, u_c), out)


_INS = ['x', 'cond_1024', 'L0_cond_router_w', 'L0_cond_router_t_w', 'L0_cond_router_bias', 'L0_cond_sw1',
        'L0_cond_sw3', 'L0_cond_sw2', 'L0_cond_rw1', 'L0_cond_rw2', 'L1_cond_W_z', 'L1_cond_U_z', 'L1_cond_C_z',
        'L1_cond_b_z', 'L1_cond_W_r', 'L1_cond_U_r', 'L1_cond_C_r', 'L1_cond_b_r', 'L1_cond_W', 'L1_cond_U',
        'L1_cond_C', 'L1_cond_b']
_OUTS = [((2, 2048, 512), 'float32')]


def kernel(**inputs):
    import numpy as _np
    import concourse.bacc as _bacc
    from concourse import mybir as _mybir
    from concourse.bass_utils import run_bass_kernel_spmd as _run

    nc = _bacc.Bacc("TRN2", target_bir_lowering=False, num_devices=1)
    arrays, args = {}, []
    for name in _INS:
        a = _np.ascontiguousarray(inputs[name])
        arrays[f"in_{name}_dram"] = a
        args.append(nc.dram_tensor(f"in_{name}_dram", a.shape, _mybir.dt.from_np(a.dtype), kind="ExternalInput").ap())
    for i, (shape, dtype) in enumerate(_OUTS):
        dt = _mybir.dt.from_np(_np.dtype(dtype))
        args.append(nc.dram_tensor(f"out_{i}_dram", shape, dt, kind="ExternalOutput").ap())
    build(nc, *args)
    r = _run(nc, [arrays], core_ids=[0])
    return r.results[0]["out_0_dram"]
```

```python
from contextlib import ExitStack

import concourse.bass as bass
from concourse import mybir

ALU = mybir.AluOpType
ACT = mybir.ActivationFunctionType
AX = mybir.AxisListType
F32 = mybir.dt.float32
F32R = mybir.dt.float32r
F16 = mybir.dt.float16
BF16 = mybir.dt.bfloat16
I32 = mybir.dt.int32

P = 128
D = 512
KD = D // P
B = 2
T = 2048
TILE = 512
TILES = B * T // TILE
TT = TILE // P
BLOCKS = B * T // P
E = 8
HS = 1024
HR = 256
TOP_K = 2
EPS = 1e-9
SCALE = 1.0 / 3.0
PARTS = 3
NONE = -3.0e38

CH = 128
CHUNKS = T // CH
PER_TILE = TILE // CH
TURNS = 7
COARSE = 3
FINE_H, FINE_RH = 2, 3
LATE_H, LATE_RH = TURNS - 1 - FINE_H, TURNS - 1 - FINE_RH
LOW = 2048.0
R, Z, C = range(3)
ROW = CH + 2
CHECKS = LATE_H + LATE_RH + 1
BOUNDS = [KD * CH * x * x for x in [4e-3] * (LATE_H + LATE_RH) + [1e-6]]


class Shared:
    pass


def constants(nc, ctx, g):
    sb = lambda n, s, d: ctx.enter_context(nc.sbuf_tensor(n, s, d))
    g.ident = sb("ident", [P, P], F32)
    g.ident_b = sb("ident_b", [P, P], BF16)
    g.ones = sb("ones", [P, P], F32)
    g.select = sb("select", [PARTS * E, E, P], BF16)
    g.gates_t = sb("gates_t", [PARTS * E, B * T], BF16)
    g.cond_t = sb("cond_t", [P, KD, B], F32)
    g.made = ctx.enter_context(nc.semaphore("constants_made"))


MADE = 4 + 2 + PARTS


def make_constants(nc, pool, g):
    nc.gpsimd.memset(g.ident[:], 0.0).then_inc(g.made, 1)
    nc.gpsimd.memset(g.ident_b[:], 0.0).then_inc(g.made, 1)
    nc.gpsimd.memset(g.select[:], 0.0).then_inc(g.made, 1)
    nc.gpsimd.memset(g.ones[:], 1.0).then_inc(g.made, 1)
    pool.wait_ge(g.made, 4)
    for t in (g.ident, g.ident_b):
        nc.gpsimd.affine_select(out=t[:], in_=t[:], compare_op=ALU.not_equal, fill=1.0, base=0,
                                pattern=[[-1, P]], channel_multiplier=1).then_inc(g.made, 1)
    for q in range(PARTS):
        nc.gpsimd.affine_select(out=g.select[:], in_=g.select[:], compare_op=ALU.not_equal, fill=1.0,
                                base=-q * E, pattern=[[-1, E], [0, P]], channel_multiplier=1
                                ).then_inc(g.made, 1)
        pool.wait_ge(g.made, 7 + q)


def tokens(nc, g, x, cond, router_w, router_t_w, router_bias, conds, biases, ahead):
    with ExitStack() as ctx:
        sb = lambda n, s, d=F32: ctx.enter_context(nc.sbuf_tensor(n, s, d))
        ps = lambda n, s, d=F32: ctx.enter_context(nc.psum_tensor(n, s, d))
        sem = lambda n: ctx.enter_context(nc.semaphore(n))
        x_rows = [sb(f"x_rows{q}", [P, TT, D]) for q in range(2)]
        x_cols = [sb(f"x_cols{q}", [P, KD, TILE]) for q in range(2)]
        small = sb("small_rows", [E, 3, D])
        router_t = sb("router_t", [P, KD, 2, E])
        t_bias = sb("t_bias", [E, B])
        logits = sb("logits", [E, B * T])
        bias = sb("bias_all", [P, 1, E])
        score, chosen, replaced, mask, kept, gate, rest, top, find = [sb(n, [P, BLOCKS, E]) for n in (
            "score", "chosen", "replaced", "mask", "kept", "gate", "rest", "top", "find")]
        total, good, inverse, half = [sb(n, [P, BLOCKS, 1]) for n in ("total", "good", "inverse", "half")]
        parts = sb("parts", [P, BLOCKS, PARTS, E], BF16)
        c_raw, c_bias, rows = sb("c_raw", [P, 3, KD, D]), sb("c_bias", [1, 3, D]), sb("rows", [B, 3, D])
        turned = [ps(f"turned{a}", [P, KD, P]) for a in range(TT)]
        logits_p = [ps(f"logits_p{q}", [E, TILE]) for q in range(2)]
        small_t = ps("small_t", [P, 3, KD, E])
        gates_p = ps("gates_p", [PARTS * E, 8 * P], BF16)

        x_loaded = [sem(f"x_loaded{q}") for q in range(2)]
        x_stored = [sem(f"x_stored{q}") for q in range(2)]
        small_loaded, x_turned = sem("small_loaded"), sem("x_turned")
        cols_v, cols_a = sem("cols_v"), sem("cols_a")
        small_turned, small_kept = sem("small_turned"), sem("small_kept")
        logits_done, logits_kept = sem("logits_done"), sem("logits_kept")
        logits_turned, scored, routed = sem("logits_turned"), sem("scored"), sem("routed")
        c_loaded = sem("c_loaded")
        rows_done, rows_kept = sem("rows_done"), sem("rows_kept")
        gates_turned, gates_kept, step = sem("gates_turned"), sem("gates_kept"), sem("route_step")
        x_v = x.rearrange("b (i a p) d -> (b i) p a d", a=TT, p=P)
        half_tiles = TILES // 2
        scores_p = small_t[:, :, :, :].rearrange("p a b c -> p (a b c)")

        with nc.Block() as block:
            @block.sync
            def _(sp):
                sp.dma_start(small[0:E, 0, :], router_w).then_inc(small_loaded, 16)
                sp.dma_start(small[0:E, 1, :], router_t_w).then_inc(small_loaded, 16)
                sp.dma_start(small[0:B, 2, :], cond).then_inc(small_loaded, 16)
                sp.dma_start(bias[:, 0, :], router_bias.partition_broadcast(P)).then_inc(small_loaded, 16)
                for q in range(2):
                    sp.dma_start(x_rows[q][:], x_v[q]).then_inc(x_loaded[q], 16)
                    sp.sem_inc(x_stored[q], 16)
                for c in range(3):
                    sp.dma_start(c_raw[:, c], conds[c].rearrange("(k p) n -> p k n", p=P)).then_inc(c_loaded, 16)
                    sp.dma_start(c_bias[0:1, c, :], biases[c].rearrange("(a n) -> a n", a=1)).then_inc(c_loaded, 16)
                with sp.Fori(0, half_tiles) as pair:
                    for q in range(2):
                        sp.wait_ge(cols_v, 2 * (2 * pair + q) + 4)
                        sp.wait_ge(cols_a, 2 * (2 * pair + q) + 4)
                        sp.dma_start(x_rows[q][:], x_v[(2 * pair + (2 + q)) % TILES]).then_inc(x_loaded[q], 16)
                        sp.dma_start(g.x_t[2 * pair + q], x_cols[q][:]).then_inc(x_stored[q], 16)
                ahead(sp)
                for q in range(2):
                    sp.wait_ge(x_stored[q], 16 * (half_tiles + 1))
                    sp.wait_ge(x_loaded[q], 16 * (half_tiles + 1))

            @block.gpsimd
            def _(pool):
                make_constants(nc, pool, g)

            @block.tensor
            def _(pe):
                pe.wait_ge(g.made, MADE)
                pe.wait_ge(small_loaded, 64)
                for w, n in ((0, E), (1, E), (2, B)):
                    for k in range(KD):
                        last = nc.tensor.transpose(small_t[:, w, k, 0:n], small[0:n, w, k * P:(k + 1) * P],
                                                   g.ident[0:n, 0:n])
                last.then_inc(small_turned, 1)
                pe.wait_ge(small_kept, 3)
                for k in range(KD):
                    last = nc.tensor.matmul(logits_p[0][:, 0:B], router_t[:, k, 1, :], g.cond_t[:, k, :],
                                            start=k == 0, stop=k == KD - 1)
                last.then_inc(small_turned, 1)
                pe.wait_ge(small_kept, 4)
                with pe.Fori(0, half_tiles) as pair:
                    for q in range(2):
                        tile = 2 * pair + q
                        pe.wait_ge(x_loaded[q], 16 * (pair + 1))
                        for a in range(TT):
                            if a == 0:
                                pe.wait_ge(cols_v, 2 * tile + 2)
                            if a == 2:
                                pe.wait_ge(cols_a, 2 * tile + 2)
                            for k in range(KD):
                                last = nc.tensor.transpose(turned[a][:, k, :], x_rows[q][:, a, k * P:(k + 1) * P],
                                                           g.ident[:])
                            last.then_inc(x_turned, 1)
                        pe.wait_ge(cols_v, 2 * tile + 4)
                        pe.wait_ge(cols_a, 2 * tile + 4)
                        pe.wait_ge(logits_kept, tile + 1)
                        for k in range(KD):
                            last = nc.tensor.matmul(logits_p[q][:], router_t[:, k, 0, :], x_cols[q][:, k, :],
                                                    start=k == 0, stop=k == KD - 1)
                        last.then_inc(logits_done, 1)
                pe.wait_ge(logits_kept, TILES + 2)
                for i in range(BLOCKS):
                    last = nc.tensor.transpose(turned[0][:, :, :].rearrange("p k q -> p (k q)")[:, i * E:(i + 1) * E],
                                               logits[:, i * P:(i + 1) * P], g.ident[0:E, 0:E])
                last.then_inc(logits_turned, 1)
                pe.wait_ge(c_loaded, 6 * 16)
                for c in range(3):
                    to = turned[1 + c][0:B, :, :].rearrange("b k q -> b (k q)")
                    for k in range(KD):
                        nc.tensor.matmul(to, g.cond_t[:, k, :], c_raw[:, c, k, :], start=k == 0, stop=False)
                    nc.tensor.matmul(to, g.ones[0:1, 0:B], c_bias[0:1, c, :], start=False, stop=True
                                     ).then_inc(rows_done, 1)
                pe.wait_ge(rows_kept, 3)
                for c in range(3):
                    for m in range(KD):
                        at = (c * KD + m) * B
                        last = nc.tensor.transpose(turned[1][:, 0, at:at + B], rows[:, c, m * P:(m + 1) * P],
                                                   g.ident[0:B, 0:B])
                last.then_inc(rows_done, 1)
                pe.wait_ge(routed, 1)
                for i in range(BLOCKS // 8):
                    if i >= 1:
                        pe.wait_ge(gates_kept, i)
                    for a in range(8):
                        last = nc.tensor.transpose(
                            gates_p[:, a * P:(a + 1) * P],
                            parts[:, 8 * i + a, :, :].rearrange("p q e -> p (q e)"), g.ident_b[:])
                    last.then_inc(gates_turned, 1)

            @block.scalar
            def _(act):
                act.sem_inc(cols_a, 2)
                act.wait_ge(g.made, MADE)
                nc.scalar.activation(score[:, 0, 0:1], g.ones[:, 0:1], ACT.Sigmoid)
                with act.Fori(0, half_tiles) as pair:
                    for q in range(2):
                        act.wait_ge(x_stored[q], 16 * (pair + 1))
                        for a in (2, 3):
                            act.wait_ge(x_turned, TT * (2 * pair + q) + a + 1)
                            nc.scalar.activation(x_cols[q][:, :, a * P:(a + 1) * P], turned[a][:], ACT.Copy
                                                 ).then_inc(cols_a, 1)
                act.wait_ge(logits_turned, 1)
                nc.scalar.activation(score[:].rearrange("p i e -> p (i e)"),
                                     turned[0][:, :, :].rearrange("p k q -> p (k q)")[:, 0:BLOCKS * E], ACT.Sigmoid
                                     ).then_inc(scored, 1)
                for c in range(3):
                    act.wait_ge(rows_done, c + 1)
                    nc.scalar.activation(rows[:, c, :], turned[1 + c][0:B, :, :].rearrange("b k q -> b (k q)"),
                                         ACT.Copy).then_inc(rows_kept, 1)
                act.wait_ge(rows_done, 4)
                nc.scalar.activation(g.gate_bias[:].rearrange("p c m b -> p (c m b)"), turned[1][:, 0, 0:3 * KD * B],
                                     ACT.Copy)

            @block.vector
            def _(dve):
                dve.sem_inc(cols_v, 2)
                dve.sem_inc(logits_kept, 2)
                dve.wait_ge(small_turned, 1)
                for w in range(2):
                    nc.vector.tensor_copy(router_t[:, :, w, :], small_t[:, w, :, :]).then_inc(small_kept, 1)
                nc.vector.tensor_copy(g.cond_t[:], small_t[:, 2, :, 0:B]).then_inc(small_kept, 1)
                dve.wait_ge(small_turned, 2)
                nc.vector.tensor_copy(t_bias[:], logits_p[0][:, 0:B]).then_inc(small_kept, 1)
                dve.wait_ge(small_kept, 4)
                for b in range(B):
                    with dve.Fori(b * half_tiles // B, (b + 1) * half_tiles // B) as pair:
                        for q in range(2):
                            dve.wait_ge(x_stored[q], 16 * (pair + 1))
                            for a in (0, 1):
                                dve.wait_ge(x_turned, TT * (2 * pair + q) + a + 1)
                                nc.vector.tensor_copy(x_cols[q][:, :, a * P:(a + 1) * P], turned[a][:]
                                                      ).then_inc(cols_v, 1)
                            dve.wait_ge(logits_done, 2 * pair + q + 1)
                            nc.vector.tensor_scalar(logits[:, bass.ds((2 * pair + q) * TILE, TILE)], logits_p[q][:],
                                                    t_bias[:, b:b + 1], None, ALU.add).then_inc(logits_kept, 1)

                count = [0]

                def in_turn(ins):
                    count[0] += 1
                    ins.then_inc(step, 1)
                    dve.wait_ge(step, count[0])

                wide = lambda t: t[:, :, :].to_broadcast([P, BLOCKS, E])
                in_turn(nc.vector.memset(find[:], NONE))
                dve.wait_ge(scored, 1)
                in_turn(nc.vector.tensor_tensor(chosen[:], score[:], bias[:].to_broadcast([P, BLOCKS, E]), ALU.add))
                for i in range(BLOCKS - 1):
                    nc.vector.max(top[:, i, :], chosen[:, i, :])
                in_turn(nc.vector.max(top[:, BLOCKS - 1, :], chosen[:, BLOCKS - 1, :]))
                in_turn(nc.vector.tensor_copy(find[:, :, 0:TOP_K], top[:, :, 0:TOP_K]))
                for i in range(BLOCKS - 1):
                    nc.vector.match_replace(replaced[:, i, :], find[:, i, :], chosen[:, i, :], NONE)
                in_turn(nc.vector.match_replace(replaced[:, BLOCKS - 1, :], find[:, BLOCKS - 1, :],
                                                chosen[:, BLOCKS - 1, :], NONE))
                in_turn(nc.vector.tensor_tensor(mask[:], replaced[:], chosen[:], ALU.not_equal))
                in_turn(nc.vector.tensor_tensor(kept[:], mask[:], score[:], ALU.mult))
                in_turn(nc.vector.tensor_reduce(total[:, :, 0], kept[:], AX.X, ALU.add))
                in_turn(nc.vector.tensor_scalar(good[:], total[:], EPS, None, ALU.is_gt))
                in_turn(nc.vector.tensor_scalar(half[:], good[:], -1.0 / TOP_K, 1.0 / TOP_K, ALU.mult, ALU.add))
                in_turn(nc.vector.tensor_scalar(total[:], total[:], EPS, None, ALU.add))
                in_turn(nc.vector.reciprocal(inverse[:], total[:]))
                in_turn(nc.vector.tensor_tensor(inverse[:], inverse[:], good[:], ALU.mult))
                in_turn(nc.vector.tensor_tensor(kept[:], kept[:], wide(inverse), ALU.mult))
                in_turn(nc.vector.tensor_tensor(mask[:], mask[:], wide(half), ALU.mult))
                in_turn(nc.vector.tensor_tensor(gate[:], kept[:], mask[:], ALU.add))
                left = [gate, rest, gate]
                for q in range(PARTS):
                    last = nc.vector.tensor_copy(parts[:, :, q, :], left[q][:])
                    if q < PARTS - 1:
                        in_turn(last)
                        in_turn(nc.vector.tensor_tensor(left[q + 1][:], left[q][:], parts[:, :, q, :], ALU.subtract))
                last.then_inc(routed, 1)
                for i in range(BLOCKS // 8):
                    dve.wait_ge(gates_turned, i + 1)
                    nc.vector.tensor_copy(g.gates_t[:, i * 8 * P:(i + 1) * 8 * P], gates_p[:]
                                          ).then_inc(gates_kept, 1)


GROUP = 8
RAW = 16


def load_units(eng, raw, views, first, loaded):
    for u, view in enumerate(views, first):
        eng.dma_start(raw[:, u % RAW], view).then_inc(loaded[u // GROUP], 16)


def first_tile(nc, ctx, plain, tag):
    first = Shared()
    first.x_cols = plain[:, 0:KD]
    first.x_hi, first.x_lo = [ctx.enter_context(nc.sbuf_tensor(n + tag, [P, KD, TILE], F32R)) for n in ("x_hi", "x_lo")]
    first.loaded, first.hi_done, first.split = [ctx.enter_context(nc.semaphore(n + tag)) for n in (
        "x_loaded", "x_hi_done", "x_split")]
    return first


def tile_high(nc, act, first, i):
    act.wait_ge(first.loaded, 16 * (i + 1))
    for k in range(KD):
        nc.scalar.activation(first.x_hi[:, k, :], first.x_cols[:, k, :], ACT.Copy).then_inc(first.hi_done, 1)


def tile_low(nc, dve, first, i):
    for k in range(KD):
        dve.wait_ge(first.hi_done, KD * i + k + 1)
        ins = nc.vector.tensor_tensor(first.x_lo[:, k, :], first.x_cols[:, k, :], first.x_hi[:, k, :].bitcast(F32),
                                      ALU.subtract)
    ins.then_inc(first.split, 1)


def turned_weights(nc, g, raw, views, loaded, hi, lo, first, base_stored, tag):
    with ExitStack() as ctx:
        sem = lambda n: ctx.enter_context(nc.semaphore(n + tag))
        banks = 8
        blocks = [ctx.enter_context(nc.psum_tensor(f"blocks{q}{tag}", [P, 4 * P], F32)) for q in range(banks)]
        turned, hi_done, lo_done = sem("raw_turned"), sem("hi_done"), sem("lo_done")
        units = range(len(views))

        with nc.Block() as block:
            @block.sync
            def _(sp):
                if base_stored is None:
                    sp.dma_start(first.x_cols, g.x_t[0]).then_inc(first.loaded, 16)
                for u in units[RAW:]:
                    sp.wait_ge(turned, u - RAW + 1)
                    load_units(sp, raw, [views[u]], u, loaded)
                if base_stored is not None:
                    sp.wait_ge(turned, RAW + KD)
                    sp.dma_start(first.x_cols, g.x_t[0]).then_inc(first.loaded, 16)
                    sp.wait_ge(base_stored, 16 * (TILES + 1))

            @block.tensor
            def _(pe):
                for u in units:
                    if u % GROUP == 0:
                        pe.wait_ge(loaded[u // GROUP], 16 * GROUP)
                    if u >= banks:
                        pe.wait_ge(lo_done, u - banks + 1)
                    for k in range(4):
                        last = nc.tensor.transpose(blocks[u % banks][:, k * P:(k + 1) * P], raw[:, u % RAW, k, :],
                                                   g.ident[:])
                    last.then_inc(turned, 1)

            @block.scalar
            def _(act):
                for u in units:
                    if u == banks and base_stored is not None:
                        act.wait_ge(base_stored, 16 * (TILES + 1))
                    act.wait_ge(turned, u + 1)
                    nc.scalar.activation(hi[:, u, :], blocks[u % banks][:], ACT.Copy).then_inc(hi_done, 1)
                tile_high(nc, act, first, 0)

            @block.vector
            def _(dve):
                for u in units:
                    dve.wait_ge(hi_done, u + 1)
                    nc.vector.tensor_tensor(lo[:, u, :], blocks[u % banks][:], hi[:, u, :].bitcast(F32),
                                            ALU.subtract).then_inc(lo_done, 1)
                tile_low(nc, dve, first, 0)


PLAIN = 2 * KD + 4


def experts(nc, g, hi, lo, plain, first, blocks, gated, base_stored, ahead, tag):
    with ExitStack() as ctx:
        sb = lambda n, s, d=F32: ctx.enter_context(nc.sbuf_tensor(n + tag, s, d))
        ps = lambda n, s, d=F32: ctx.enter_context(nc.psum_tensor(n + tag, s, d))
        sem = lambda n: ctx.enter_context(nc.semaphore(n + tag))
        x_cols, base, x_hi, x_lo = first.x_cols, plain[:, KD:2 * KD], first.x_hi, first.x_lo
        bent, hidden = [[plain[:, 2 * KD + 2 * t + q] for q in range(2)] for t in range(2)]
        table_in = sb("table_in", [P, 1])
        hid_hi = [sb(f"hid_hi{q}", [P, TILE], F32R) for q in range(2)]
        hid_lo = [sb(f"hid_lo{q}", [P, TILE], F32R) for q in range(2)]
        up = [ps(f"up{q}", [P, TILE]) for q in range(2)]
        factor = [ps(f"factor{q}", [P, TILE]) for q in range(2)]
        out = [ps(f"out{m}", [P, TILE]) for m in range(KD)]

        x_loaded, x_split = first.loaded, first.split
        up_done, factor_done = sem("up_done"), sem("factor_done")
        bent_done = sem("bent_done")
        hid_step, hid_split = sem("hid_step"), sem("hid_split")
        hid_used = sem("hid_used")
        out_done = sem("out_done")
        out_kept = sem("out_kept")
        base_loaded = sem("base_loaded")
        per = 1 if gated else HR // P

        down0 = 2 * blocks if gated else blocks

        with nc.Block() as block:
            @block.sync
            def _(sp):
                sp.sem_inc(base_stored, 16)
                ahead(sp)
                with sp.Fori(0, TILES) as i:
                    sp.wait_ge(base_stored, 16 * (i + 1))
                    sp.dma_start(base, (g.x_t if gated else g.shared)[i]).then_inc(base_loaded, 16)
                    sp.wait_ge(x_split, i + 1)
                    sp.dma_start(x_cols, g.x_t[(i + 1) % TILES]).then_inc(x_loaded, 16)
                    sp.wait_ge(out_kept, KD * (i + 2))
                    sp.dma_start((g.shared if gated else g.x1_t)[i], base).then_inc(base_stored, 16)
                sp.wait_ge(x_loaded, 16 * (TILES + 1))

            @block.tensor
            def _(pe):
                pe.sem_inc(hid_used, 2)

                def product(to, slots, columns, first=True, last=True):
                    for k, (slot, col) in enumerate(slots):
                        a_hi, a_lo = hi[:, slot, col:col + P], lo[:, slot, col:col + P]
                        b_hi, b_lo = columns(k)
                        nc.tensor.matmul(to, a_hi, b_hi, start=first and k == 0, stop=False)
                        nc.tensor.matmul(to, a_hi, b_lo, start=False, stop=False)
                        ins = nc.tensor.matmul(to, a_lo, b_hi, start=False, stop=last and k == len(slots) - 1)
                    return ins

                x_at = lambda k: (x_hi[:, k, :], x_lo[:, k, :])

                def down(i, j):
                    pe.wait_ge(hid_split, blocks * i + j + 1)
                    if j == 0:
                        pe.wait_ge(out_kept, KD * (i + 1))
                    for m in range(KD):
                        ins = product(out[m][:], [(down0 + j, m * P)],
                                      lambda k: (hid_hi[j % 2][:], hid_lo[j % 2][:]), j == 0, j == blocks - 1)
                        if j == blocks - 1 and m < KD - 1:
                            ins.then_inc(out_done, 1)
                    ins.then_inc(hid_used, 1)

                with pe.Fori(0, TILES) as i:
                    pe.wait_ge(x_split, i + 1)
                    for j in range(blocks):
                        product(up[j % 2][:], [(j, k * P) for k in range(KD)], x_at).then_inc(up_done, 1)
                        if gated:
                            product(factor[j % 2][:], [(blocks + j, k * P) for k in range(KD)], x_at
                                    ).then_inc(factor_done, 1)
                        elif j % per == 0:
                            e = j // per
                            nc.tensor.matmul(factor[e % 2][:], g.select[:, e, :],
                                             g.gates_t[:, bass.ds(i * TILE, TILE)], start=True, stop=True
                                             ).then_inc(factor_done, 1)
                        if j >= 1:
                            down(i, j - 1)
                    down(i, blocks - 1)

            @block.scalar
            def _(act):
                nc.scalar.activation(table_in[:], g.ones[:, 0:1], ACT.Silu if gated else ACT.Gelu)
                with act.Fori(0, TILES) as i:
                    for j in range(blocks):
                        act.wait_ge(up_done, blocks * i + j + 1)
                        nc.scalar.activation(bent[j % 2], up[j % 2][:], ACT.Silu if gated else ACT.Gelu
                                             ).then_inc(bent_done, 1)
                    act.wait_ge(factor_done if gated else up_done, blocks * (i + 1))
                    tile_high(nc, act, first, i + 1)

            @block.vector
            def _(dve):
                dve.sem_inc(out_kept, KD)

                with dve.Fori(0, TILES) as i:
                    for j in range(blocks):
                        n = blocks * i + j + 1
                        dve.wait_ge(bent_done, n)
                        if j % per == 0:
                            dve.wait_ge(factor_done, (blocks // per) * i + j // per + 1)
                        dve.wait_ge(hid_used, n)
                        nc.vector.tensor_tensor(hidden[j % 2], bent[j % 2], factor[j // per % 2][:], ALU.mult
                                                ).then_inc(hid_step, 1)
                        dve.wait_ge(hid_step, 2 * n - 1)
                        nc.vector.tensor_copy(hid_hi[j % 2][:], hidden[j % 2]).then_inc(hid_step, 1)
                        dve.wait_ge(hid_step, 2 * n)
                        nc.vector.tensor_tensor(hid_lo[j % 2][:], hidden[j % 2], hid_hi[j % 2][:].bitcast(F32),
                                                ALU.subtract).then_inc(hid_split, 1)
                    tile_low(nc, dve, first, i + 1)
                    dve.wait_ge(base_loaded, 16 * (i + 1))
                    for m in range(KD):
                        if m < KD - 1:
                            dve.wait_ge(out_done, (KD - 1) * i + m + 1)
                        else:
                            dve.wait_ge(hid_used, blocks * (i + 1) + 2)
                        nc.vector.scalar_tensor_tensor(base[:, m, :], out[m][:], SCALE, base[:, m, :],
                                                       ALU.mult, ALU.add).then_inc(out_kept, 1)


def input_shares(nc, g, w_first, w_first_loaded, weights, steps, x1_stored):
    with ExitStack() as ctx:
        sem = lambda n: ctx.enter_context(nc.semaphore("in_" + n))
        sb = lambda n, s, d=F32: ctx.enter_context(nc.sbuf_tensor("in_" + n, s, d))
        ps = lambda n, s: ctx.enter_context(nc.psum_tensor("in_" + n, s, F32))
        w_raw = [w_first] + [sb(f"w{c}", [P, KD, D]) for c in range(1, 3)]
        u_raw = w_raw
        x1, table_in = sb("x1", [P, KD, TILE]), sb("table_in", [P, 1])
        x_hi, x_lo = [[sb(f"x_{n}{q}", [P, KD, TILE], F32R) for q in range(2)] for n in ("hi", "lo")]
        shares = sb("shares", [P, PER_TILE, 3, KD, CH])
        z0, cand0 = [sb(n, [P, PER_TILE, KD, CH], F16) for n in ("z0", "cand0")]
        guess = sb("guess", [P, PER_TILE, 2, KD, ROW], F16)
        banks = 6
        bank = [ps(f"bank{q}", [P, PER_TILE, CH]) for q in range(banks)]
        u_loaded = sem("u_loaded")
        w_loaded = [w_first_loaded] + [sem(f"w{c}_loaded") for c in range(1, 3)]
        hi_done, rest_done = sem("hi_done"), sem("rest_done")
        x1_loaded, x_hi_done, x_split = sem("x1_loaded"), sem("x_hi_done"), sem("x_split")
        sum_done = sem("sum_done")
        kept_a, kept_v = sem("kept_a"), sem("kept_v")
        stored = sem("stored")
        gates_done = sem("gates_done")
        cleared, gain_done = sem("cleared"), sem("gain_done")
        guess_stored = sem("guess_stored")
        by_block = lambda w: w.rearrange("(k p) n -> p k n", p=P)
        blocks = [(c, m) for c in range(3) for m in range(KD)]
        each = len(blocks) // 2

        with nc.Block() as block:
            @block.sync
            def _(sp):
                sp.wait_ge(x1_stored, 16 * TILES)
                sp.dma_start(x1[:], g.x1_t[0]).then_inc(x1_loaded, 16)
                for c in range(1, 3):
                    sp.dma_start(w_raw[c][:], by_block(weights[c])).then_inc(w_loaded[c], 16)
                sp.sem_inc(stored, 3 * 16)
                sp.sem_inc(guess_stored, 16)
                sp.wait_ge(x1_stored, 16 * (TILES + 1))
                sp.wait_ge(rest_done, 3)
                for c in range(3):
                    sp.dma_start(u_raw[c][:], by_block(steps[c])).then_inc(u_loaded, 16)
                with sp.Fori(0, TILES) as i:
                    sp.wait_ge(x_split, i + 1)
                    sp.dma_start(x1[:], g.x1_t[(i + 1) % TILES]).then_inc(x1_loaded, 16)
                    for c in range(3):
                        sp.wait_ge(kept_a, each * i + 2 * c + 5)
                        sp.wait_ge(kept_v, each * i + 2 * c + 5)
                        sp.dma_start(g.shares[i].rearrange("q p c k t -> c p q k t")[c], shares[:, :, c]
                                     ).then_inc(stored, 16)
                    sp.wait_ge(gain_done, i + 1)
                    sp.dma_start(g.guess[i].rearrange("q p a k t -> p q (a k t)"), guess[:].rearrange("p q a k t -> p q (a k t)")
                                 ).then_inc(guess_stored, 16)
                sp.wait_ge(stored, 3 * 16 * (TILES + 1))
                sp.wait_ge(guess_stored, 16 * (TILES + 1))
                sp.wait_ge(x1_loaded, 16 * (TILES + 1))

            @block.tensor
            def _(pe):
                with pe.Fori(0, TILES // 2) as pair:
                    for q in range(2):
                        i = 2 * pair + q
                        pe.wait_ge(x_split, i + 1)
                        for n, (c, m) in enumerate(blocks):
                            if m == 0:
                                pe.wait_ge(rest_done, c + 1)
                            pe.wait_ge(kept_a if n % 2 == 0 else kept_v, each * i + n // 2 + 1)
                            to, cut = bank[n % banks][:], slice(m * P, (m + 1) * P)
                            for k in range(KD):
                                nc.tensor.matmul(to, g.w_hi[:, c, k, cut], x_hi[q][:, k, :], start=k == 0, stop=False)
                                nc.tensor.matmul(to, g.w_hi[:, c, k, cut], x_lo[q][:, k, :], start=False, stop=False)
                                last = nc.tensor.matmul(to, g.w_lo[:, c, k, cut], x_hi[q][:, k, :], start=False,
                                                        stop=k == KD - 1)
                            last.then_inc(sum_done, 1)

            @block.scalar
            def _(act):
                act.sem_inc(kept_a, 3)
                act.sem_inc(gates_done, 3)
                nc.scalar.activation(table_in[:], g.ones[:, 0:1], ACT.Sigmoid)

                def split_w(c):
                    act.wait_ge(w_loaded[c], 16)
                    nc.scalar.activation(g.w_hi[:, c, :, :], w_raw[c][:], ACT.Copy).then_inc(hi_done, 1)

                def split(i, q):
                    act.wait_ge(x1_loaded, 16 * (i + 1))
                    for k in range(KD):
                        nc.scalar.activation(x_hi[q][:, k], x1[:, k], ACT.Copy).then_inc(x_hi_done, 1)

                split_w(0)
                split(0, 0)
                for c in range(1, 3):
                    split_w(c)
                for b in range(B):
                    with act.Fori(b * TILES // 4, (b + 1) * TILES // 4) as pair:
                        for q in range(2):
                            i = 2 * pair + q
                            for n, (c, m) in enumerate(blocks):
                                if n % 2:
                                    continue
                                act.wait_ge(sum_done, len(blocks) * i + n + 1)
                                act.wait_ge(stored, 3 * 16 * (i + 1))
                                if n in (KD, KD + 1):
                                    act.wait_ge(gates_done, 3 * (i + 1))
                                nc.scalar.activation(shares[:, :, c, m, :], bank[n % banks][:], ACT.Identity,
                                                     bias=g.gate_bias[:, c, m, b:b + 1]).then_inc(kept_a, 1)
                                if n == 0:
                                    split(i + 1, 1 - q)
                                if n == 2 * KD:
                                    act.wait_ge(kept_a, each * i + 7)
                                    act.wait_ge(kept_v, each * i + 7)
                                    act.wait_ge(guess_stored, 16 * (i + 1))
                                    nc.scalar.activation(z0[:], shares[:, :, Z], ACT.Sigmoid).then_inc(gates_done, 1)
                                    nc.scalar.activation(guess[:, :, 0, :, 1:CH + 1], shares[:, :, Z], ACT.Sigmoid,
                                                         scale=-1.0).then_inc(gates_done, 1)
                            act.wait_ge(kept_a, each * i + 9)
                            act.wait_ge(kept_v, each * i + 9)
                            nc.scalar.activation(cand0[:], shares[:, :, C], ACT.Tanh).then_inc(gates_done, 1)
                    if b == 0:
                        act.wait_ge(u_loaded, 3 * 16)
                        for c in range(3):
                            nc.scalar.activation(g.u_hi[:, c, :, :], u_raw[c][:], ACT.Copy).then_inc(hi_done, 1)
                for c in range(3):
                    act.wait_ge(rest_done, c + 4)
                    nc.scalar.activation(g.u_lo[:, c, :, :], u_raw[c][:], ACT.Copy, scale=LOW)

            @block.vector
            def _(dve):
                dve.sem_inc(kept_v, 3)
                for column in (0, CH + 1):
                    nc.vector.memset(guess[:, :, :, :, column:column + 1], 0.0).then_inc(cleared, 1)
                def split_w(c):
                    dve.wait_ge(hi_done, c + 1)
                    nc.vector.tensor_tensor(g.w_lo[:, c, :, :], w_raw[c][:], g.w_hi[:, c, :, :].bitcast(F32),
                                            ALU.subtract).then_inc(rest_done, 1)

                def split(i, q):
                    for k in range(KD):
                        dve.wait_ge(x_hi_done, KD * i + k + 1)
                        ins = nc.vector.tensor_tensor(x_lo[q][:, k], x1[:, k], x_hi[q][:, k].bitcast(F32),
                                                      ALU.subtract)
                    ins.then_inc(x_split, 1)

                split_w(0)
                split(0, 0)
                for c in range(1, 3):
                    split_w(c)
                for b in range(B):
                    with dve.Fori(b * TILES // 4, (b + 1) * TILES // 4) as pair:
                        for q in range(2):
                            i = 2 * pair + q
                            for n, (c, m) in enumerate(blocks):
                                if n % 2 == 0:
                                    continue
                                dve.wait_ge(sum_done, len(blocks) * i + n + 1)
                                dve.wait_ge(stored, 3 * 16 * (i + 1))
                                if n in (KD, KD + 1):
                                    dve.wait_ge(gates_done, 3 * (i + 1))
                                nc.vector.tensor_scalar(shares[:, :, c, m, :], bank[n % banks][:],
                                                        g.gate_bias[:, c, m, b:b + 1], None, ALU.add
                                                        ).then_inc(kept_v, 1)
                                if n == 1:
                                    split(i + 1, 1 - q)
                            dve.wait_ge(gates_done, 3 * (i + 2))
                            nc.vector.tensor_tensor(guess[:, :, 1, :, 1:CH + 1], z0[:], cand0[:], ALU.mult
                                                    ).then_inc(gain_done, 1)
                    if b == 0:
                        for c in range(3):
                            dve.wait_ge(hi_done, c + 4)
                            nc.vector.tensor_tensor(u_raw[c][:], u_raw[c][:], g.u_hi[:, c, :, :], ALU.subtract
                                                    ).then_inc(rest_done, 1)


def gru(nc, g, out):
    with ExitStack() as ctx:
        sb = lambda n, s, d=F32: [ctx.enter_context(nc.sbuf_tensor(f"{n}_b{b}", s, d)) for b in range(B)]
        sem = lambda n: [ctx.enter_context(nc.semaphore(f"{n}_b{b}")) for b in range(B)]
        flat = [P, KD, CH]
        long = [P, KD, ROW]
        share_in, guess, x_add = sb("share_in", [P, 3, KD, CH]), sb("guess_in", [P, 2, KD, ROW], F16), sb("x_add", flat)
        h, keep, gain = sb("h", long), sb("keep", long), sb("gain", long)
        r, z, cand, rh = sb("r", flat), sb("z", flat), sb("cand", flat), sb("rh", flat)
        h_sent, rh_sent = sb("h_sent", flat), sb("rh_sent", flat)
        r16, z16, cand16, rh16 = [sb(n, flat, F16) for n in ("r16", "z16", "cand16", "rh16")]
        h16, gain16 = sb("h16", long, F16), sb("gain16", long, F16)
        h_head, rh_head = sb("h_head", long, F16), sb("rh_head", flat, F16)
        h_step, rh_step = sb("h_step", flat, F16), sb("rh_step", flat, F16)
        h_fine, rh_fine = sb("h_fine", flat, F16), sb("rh_fine", flat, F16)
        change, square = sb("change", flat), sb("square", [P, CHECKS, KD, CH])
        y, y_rows = sb("y", flat), sb("y_rows", [P, D])
        bank = [[ctx.enter_context(nc.psum_tensor(f"gate{c}_b{b}", flat, F32)) for c in range(3)] for b in range(B)]
        y_turned = [ctx.enter_context(nc.psum_tensor(f"y_turned_b{b}", [P, D], F32)) for b in range(B)]

        share_loaded, guess_loaded, x_add_loaded = sem("share_loaded"), sem("guess_loaded"), sem("x_add_loaded")
        seeded = sem("seeded")
        start_done = sem("start_done")
        h_step_done, rh_step_done = sem("h_step_done"), sem("rh_step_done")
        r_sum, z_sum, c_sum = sem("r_sum"), sem("z_sum"), sem("c_sum")
        r_done, cand_done = sem("r_done"), sem("cand_done")
        gain_done, h_done = sem("gain_done"), sem("h_done")
        rh_done, h_sent_done = sem("rh_done"), sem("h_sent_done")
        rh_sent_done = sem("rh_sent_done")
        h_fine_done, rh_fine_done = sem("h_fine_done"), sem("rh_fine_done")
        h_squared, rh_squared = sem("h_squared"), sem("rh_squared")
        change_done, change_squared = sem("change_done"), sem("change_squared")
        y_done, y_turn_done, y_kept = sem("y_done"), sem("y_turn_done"), sem("y_kept")
        y_stored = sem("y_stored")
        table_in = ctx.enter_context(nc.sbuf_tensor("table_warmed", [P, 1], F32))
        banks_taken, cleared = [ctx.enter_context(nc.semaphore(n)) for n in ("banks_taken", "cleared")]

        shares, guesses = [t.rearrange("i q p c k t -> (i q) p c k t") for t in (g.shares, g.guess)]
        streams = range(B)
        before = lambda t: t[:, :, 0:CH]
        after = lambda t: t[:, :, 1:CH + 1]

        def all_turns(eng, turn):
            turn(0, 0, None)
            with eng.Fori(0, CHUNKS) as c:
                for k in range(1, TURNS):
                    turn(c, k, None)
                turn(c + 1, 0, c)

        with nc.Block() as block:
            @block.sync
            def _(sp):
                for b in streams:
                    sp.sem_inc(y_stored[b], 16)
                    sp.dma_start(share_in[b][:], shares[b * CHUNKS]).then_inc(share_loaded[b], 16)
                    sp.dma_start(guess[b][:], guesses[b * CHUNKS]).then_inc(guess_loaded[b], 16)
                with sp.Fori(0, CHUNKS // PER_TILE) as i, sp.Fori(0, PER_TILE) as q:
                    c = i * PER_TILE + q
                    after_c = (c + 1) % CHUNKS
                    for b in streams:
                        sp.wait_ge(seeded[b], 3 * (c + 1))
                        sp.dma_start(share_in[b][:], shares[b * CHUNKS + after_c]).then_inc(share_loaded[b], 16)
                        sp.wait_ge(h_step_done[b], TURNS * c + 1)
                        sp.dma_start(guess[b][:], guesses[b * CHUNKS + after_c]).then_inc(guess_loaded[b], 16)
                        sp.wait_ge(y_done[b], c + 1)
                        sp.dma_start(x_add[b][:], g.x1_t[b * (TILES // B) + i]
                                     [:, :, bass.ds(q * CH, CH)]).then_inc(x_add_loaded[b], 16)
                    for b in streams:
                        sp.wait_ge(y_kept[b], c + 2)
                        sp.dma_start(out[b, bass.ds(c * CH, CH), :], y_rows[b][:]).then_inc(y_stored[b], 16)
                for b in streams:
                    sp.wait_ge(y_stored[b], 16 * (CHUNKS + 1))
                    sp.wait_ge(share_loaded[b], 16 * (CHUNKS + 1))
                    sp.wait_ge(guess_loaded[b], 16 * (CHUNKS + 1))

            @block.tensor
            def _(pe):
                for b in streams:
                    pe.sem_inc(y_turn_done[b], 1)
                    for c in range(3):
                        for k in range(KD):
                            ins = nc.tensor.matmul(bank[b][c][:, k, :], g.ident[:], g.ones[:], start=k == 0,
                                                   stop=k == KD - 1, skip_group_check=True)
                ins.then_inc(banks_taken, 1)

                def add(to, weights, columns):
                    for m in range(KD):
                        for k in range(KD):
                            ins = nc.tensor.matmul(to[:, m, :], weights[:, k, m * P:(m + 1) * P], columns[:, k, :],
                                                   start=False, stop=m == KD - 1 and k == KD - 1,
                                                   skip_group_check=True)
                    return ins

                def turn(c, k, before_c):
                    n = c * TURNS + k

                    def total(b, gate, done):
                        if k == 0:
                            pe.wait_ge(seeded[b], 3 * c + gate + 1)
                        if gate == C:
                            pe.wait_ge(rh_step_done[b], n + 1)
                            step = rh_head[b][:] if k == 0 else rh_step[b][:]
                        else:
                            pe.wait_ge(h_step_done[b], n + 1)
                            step = before(h_head[b]) if k == 0 else h_step[b][:]
                        add(bank[b][gate], g.u_hi[:, gate], step).then_inc(done[b], 1)

                    def low(b, gate, turns):
                        pe.wait_ge((r_done if gate == R else cand_done)[b], turns)
                        if gate == C:
                            pe.wait_ge(rh_fine_done[b], c + 1)
                        else:
                            pe.wait_ge(h_fine_done[b], c + 1)
                        add(bank[b][gate], g.u_lo[:, gate], (rh_fine if gate == C else h_fine)[b][:])

                    total(0, R, r_sum)
                    total(0, Z, z_sum)
                    total(1, R, r_sum)
                    if k == FINE_H + 1:
                        low(1, Z, n)
                    if k == FINE_RH + 1:
                        low(1, C, n)
                    total(0, C, c_sum)
                    total(1, Z, z_sum)
                    total(1, C, c_sum)
                    if k == FINE_H:
                        low(0, Z, n + 1)
                    if k == FINE_RH:
                        low(0, C, n + 1)
                    if k == FINE_RH + 1:
                        for b in streams:
                            low(b, R, n + 1)
                    if before_c is not None:
                        for b in streams:
                            pe.wait_ge(y_done[b], before_c + 2)
                            pe.wait_ge(y_kept[b], before_c + 1)
                            for k in range(KD):
                                ins = nc.tensor.transpose(y_turned[b][:, k * P:(k + 1) * P], y[b][:, k, :], g.ident[:])
                            ins.then_inc(y_turn_done[b], 1)

                all_turns(pe, turn)

            @block.scalar
            def _(act):
                for b in streams:
                    act.sem_inc(h_squared[b], LATE_H)
                    act.sem_inc(rh_squared[b], LATE_RH)
                    act.sem_inc(change_squared[b], 1)
                    act.sem_inc(y_kept[b], 1)
                nc.scalar.activation(table_in[:], g.ones[:, 0:1], ACT.Sigmoid)

                def seed(b, gate, c):
                    act.wait_ge(share_loaded[b], 16 * (c + 1))
                    nc.scalar.activation(bank[b][gate][:], share_in[b][:, gate], ACT.Copy).then_inc(seeded[b], 1)

                def sum_squares(b, what, kind, c):
                    return nc.scalar.activation(square[b][:, kind], what, ACT.Square,
                                                accum_out=g.left[:, kind, b, bass.ds(c, 1)])

                def turn(c, k, before_c):
                    n = c * TURNS + k
                    last, late = k == TURNS - 1, k - FINE_RH - 1

                    coarse = k < COARSE

                    def fine_h(b):
                        act.wait_ge(h_done[b], n)
                        nc.scalar.activation(h_fine[b][:], before(h16[b]), ACT.Copy, scale=1 / LOW
                                             ).then_inc(h_fine_done[b], 1)

                    def fine_rh(b):
                        act.wait_ge(rh_done[b], c * (TURNS - 1) + k)
                        nc.scalar.activation(rh_fine[b][:], rh[b][:], ACT.Copy, scale=1 / LOW
                                             ).then_inc(rh_fine_done[b], 1)

                    def reset_gate(b):
                        act.wait_ge(r_sum[b], n + 1)
                        nc.scalar.activation((r16 if coarse else r)[b][:], bank[b][R][:], ACT.Sigmoid
                                             ).then_inc(r_done[b], 1)

                    def update_gate(b):
                        act.wait_ge(z_sum[b], n + 1)
                        nc.scalar.activation((z16 if coarse else z)[b][:], bank[b][Z][:], ACT.Sigmoid)
                        nc.scalar.activation(after(keep[b]), bank[b][Z][:], ACT.Sigmoid, scale=-1.0)

                    def candidate(b):
                        act.wait_ge(c_sum[b], n + 1)
                        nc.scalar.activation((cand16 if coarse else cand)[b][:], bank[b][C][:], ACT.Tanh
                                             ).then_inc(cand_done[b], 1)

                    def late_h(b):
                        act.wait_ge(h_step_done[b], n + 1)
                        sum_squares(b, h_step[b][:], k - FINE_H - 1, c).then_inc(h_squared[b], 1)

                    def late_rh(b, late, chunk, n):
                        act.wait_ge(rh_step_done[b], n + 1)
                        sum_squares(b, rh_step[b][:], LATE_H + late, chunk).then_inc(rh_squared[b], 1)

                    if k == FINE_H:
                        fine_h(0)
                    if k > FINE_H:
                        late_h(0)
                    reset_gate(0)
                    update_gate(0)
                    reset_gate(1)
                    if last:
                        act.wait_ge(r_done[0], n + 1)
                        seed(0, R, c + 1)
                    if k == FINE_H:
                        fine_h(1)
                    if k > FINE_H:
                        late_h(1)
                    if before_c is not None:
                        late_rh(1, LATE_RH - 1, before_c, n - 1)
                    candidate(0)
                    if k == FINE_RH:
                        fine_rh(0)
                    update_gate(1)
                    candidate(1)
                    if last:
                        act.wait_ge(cand_done[1], n + 1)
                        for b, gate in ((0, Z), (1, R), (0, C), (1, Z), (1, C)):
                            seed(b, gate, c + 1)
                    if k == FINE_RH:
                        fine_rh(1)
                    if late >= 0:
                        late_rh(0, late, c, n)
                        if not last:
                            late_rh(1, late, c, n)
                    if before_c is not None:
                        for b in streams:
                            act.wait_ge(change_done[b], before_c + 2)
                            sum_squares(b, change[b][:], CHECKS - 1, before_c).then_inc(change_squared[b], 1)
                        for b in streams:
                            act.wait_ge(y_turn_done[b], before_c + 2)
                            act.wait_ge(y_stored[b], 16 * (before_c + 1))
                            nc.scalar.activation(y_rows[b][:], y_turned[b][:], ACT.Copy).then_inc(y_kept[b], 1)

                act.wait_ge(banks_taken, 1)
                for gate in range(3):
                    for b in streams:
                        seed(b, gate, 0)
                all_turns(act, turn)

            @block.gpsimd
            def _(pool):
                for b in streams:
                    pool.sem_inc(y_done[b], 1)
                    pool.sem_inc(change_done[b], 1)

                def turn(c, k, before_c):
                    n = c * TURNS + k
                    if k >= 1:
                        for b in streams:
                            pool.wait_ge(h_step_done[b], n + 1)
                            if k == 1:
                                pool.wait_ge(change_done[b], c + 1)
                            else:
                                pool.wait_ge(h_sent_done[b], c * (TURNS - 1) + k - 1)
                            nc.gpsimd.tensor_tensor(h_sent[b][:], before(h_head[b]) if k == 1 else h_sent[b][:], h_step[b][:],
                                                    ALU.add).then_inc(h_sent_done[b], 1)
                        if k < TURNS - 1:
                            for b in streams:
                                pool.wait_ge(rh_step_done[b], n + 1)
                                if k > 1:
                                    pool.wait_ge(rh_sent_done[b], c * (TURNS - 2) + k - 1)
                                nc.gpsimd.tensor_tensor(rh_sent[b][:], (rh_head if k == 1 else rh_sent)[b][:],
                                                        rh_step[b][:], ALU.add).then_inc(rh_sent_done[b], 1)
                    if k == TURNS - 1:
                        for b in streams:
                            pool.wait_ge(h_done[b], n + 1)
                            pool.wait_ge(x_add_loaded[b], 16 * (c + 1))
                            pool.wait_ge(y_turn_done[b], c + 1)
                            nc.gpsimd.tensor_tensor(y[b][:], x_add[b][:], after(h[b]), ALU.add).then_inc(y_done[b], 1)
                            pool.wait_ge(h_sent_done[b], (TURNS - 1) * (c + 1))
                            pool.wait_ge(change_squared[b], c + 1)
                            nc.gpsimd.tensor_tensor(change[b][:], before(h[b]), h_sent[b][:], ALU.subtract
                                                    ).then_inc(change_done[b], 1)

                all_turns(pool, turn)

            @block.vector
            def _(dve):
                for b in streams:
                    nc.vector.memset(h[b][:], 0.0).then_inc(cleared, 1)
                    for t in (keep, gain, gain16):
                        nc.vector.memset(t[b][:], 0.0).then_inc(cleared, 1)
                dve.wait_ge(cleared, 4 * B)

                def scan(b, to, keep, gain):
                    flat = lambda t: t.rearrange("p k t -> p (k t)")
                    return nc.vector.tensor_tensor_scan(flat(to), flat(keep), flat(gain), 0.0, ALU.mult, ALU.add)

                def begin(b, c):
                    dve.wait_ge(guess_loaded[b], 16 * (c + 1))
                    for to in (guess[b][:, 1], gain16[b][:], gain[b][:]):
                        nc.vector.tensor_copy(to[:, :, 0:1], h[b][:, :, CH:CH + 1]).then_inc(start_done[b], 1)
                    dve.wait_ge(start_done[b], 3 * (c + 1))
                    scan(b, h_head[b][:], guess[b][:, 0], guess[b][:, 1]).then_inc(h_step_done[b], 1)

                def turn(c, k, before_c):
                    n = c * TURNS + k
                    states = h_head if k == 0 else h16 if k <= COARSE else h
                    if k < COARSE:
                        reset, update, candidate, product, gained, new = r16, z16, cand16, rh16, gain16, h16
                    else:
                        reset, update, candidate, product, gained, new = r, z, cand, rh, gain, h
                    for b in streams:
                        dve.wait_ge(r_done[b], n + 1)
                        if k == 0:
                            dve.wait_ge(h_step_done[b], n + 1)
                            nc.vector.tensor_tensor(rh_head[b][:], reset[b][:], before(states[b]), ALU.mult
                                                    ).then_inc(rh_step_done[b], 1)
                            continue
                        nc.vector.tensor_tensor(product[b][:], reset[b][:], before(states[b]), ALU.mult
                                                ).then_inc(rh_done[b], 1)
                        dve.wait_ge(rh_done[b], c * (TURNS - 1) + k)
                        if k > 1:
                            dve.wait_ge(rh_sent_done[b], c * (TURNS - 2) + k - 1)
                        if k == 1 or k > FINE_RH + 1:
                            dve.wait_ge(rh_squared[b], LATE_RH * (c + 1) + max(k - FINE_RH - 1, 0))
                        nc.vector.tensor_tensor(rh_step[b][:], product[b][:], (rh_head if k == 1 else rh_sent)[b][:],
                                                ALU.subtract).then_inc(rh_step_done[b], 1)
                    for b in streams:
                        dve.wait_ge(cand_done[b], n + 1)
                        nc.vector.tensor_tensor(after(gained[b]), update[b][:], candidate[b][:], ALU.mult
                                                ).then_inc(gain_done[b], 1)
                        dve.wait_ge(gain_done[b], n + 1)
                        if k == COARSE:
                            dve.wait_ge(change_done[b], c + 1)
                        scan(b, new[b][:], keep[b][:], gained[b][:]).then_inc(h_done[b], 1)
                        dve.wait_ge(h_done[b], n + 1)
                        if k == TURNS - 1:
                            begin(b, c + 1)
                            continue
                        if k > 0:
                            dve.wait_ge(h_sent_done[b], c * (TURNS - 1) + k)
                        else:
                            dve.wait_ge(y_done[b], c + 1)
                        if k == 0 or k > FINE_H:
                            dve.wait_ge(h_squared[b], LATE_H * (c + 1) + max(k - FINE_H, 0))
                        nc.vector.tensor_tensor(h_step[b][:], before(new[b]),
                                                before(h_head[b]) if k == 0 else h_sent[b][:],
                                                ALU.subtract).then_inc(h_step_done[b], 1)

                for b in streams:
                    begin(b, 0)
                all_turns(dve, turn)


def all_settled(nc, g):
    with ExitStack() as ctx:
        below = ctx.enter_context(nc.sbuf_tensor("below", [P, CHECKS, B, CHUNKS], F32))
        count = ctx.enter_context(nc.sbuf_tensor("count", [P, 1], F32))
        number = ctx.enter_context(nc.psum_tensor("number", [1, 1], F32))
        compared, counted, summed = [ctx.enter_context(nc.semaphore(n)) for n in ("compared", "counted", "summed")]
        with nc.Block() as block:
            @block.vector
            def _(dve):
                for kind in range(CHECKS):
                    nc.vector.tensor_scalar(below[:, kind], g.left[:, kind], BOUNDS[kind], None, ALU.is_le
                                            ).then_inc(compared, 1)
                dve.wait_ge(compared, CHECKS)
                nc.vector.tensor_reduce(count[:], below[:].rearrange("p a b c -> p (a b c)"), AX.X, ALU.add
                                        ).then_inc(counted, 1)
                dve.wait_ge(summed, 1)
                nc.vector.tensor_scalar(g.settled[:], number[:], float(P * CHECKS * B * CHUNKS), None, ALU.is_equal)

            @block.tensor
            def _(pe):
                pe.wait_ge(counted, 1)
                nc.tensor.matmul(number[:], count[:], g.ones[:, 0:1], start=True, stop=True).then_inc(summed, 1)


def step_by_step(nc, g, steps, out):
    with ExitStack() as ctx:
        sb = lambda n, s, d=F32: ctx.enter_context(nc.sbuf_tensor("st_" + n, s, d))
        ps = lambda n, s: ctx.enter_context(nc.psum_tensor("st_" + n, s, F32))
        sem = lambda n: ctx.enter_context(nc.semaphore("st_" + n))
        flat = [P, B, KD, CH]
        shares = g.shares.rearrange("i q p c k t -> (i q) p c k t")
        x_in = sb("x_in", flat)
        share = sb("share", [P, 3, B, KD, CH])
        states, y, y_rows = sb("states", flat), sb("y", flat), sb("y_rows", [P, B, D])
        u = [sb(f"u{c}", [P, KD, D]) for c in range(3)]
        h, rh, keep, cand = [sb(n, [P, B, KD]) for n in ("h", "rh", "keep", "cand")]
        sums, gates = sb("sums", [P, 3, B, KD]), sb("gates", [P, 2, B, KD])
        kept, gain = sb("kept", [P, B, KD]), sb("gain", [P, B, KD])
        of_h, of_rh, y_turned = ps("of_h", [P, 2, B, KD]), ps("of_rh", [P, B, KD]), ps("y_turned", [P, D])
        u_loaded, x_loaded, share_loaded = sem("u_loaded"), sem("x_loaded"), sem("share_loaded")
        h_done = sem("h_done")
        of_h_done, rz_sum, rz_done, keep_done, rh_done = [
            sem(n) for n in ("of_h_done", "rz_sum", "rz_done", "keep_done", "rh_done")]
        of_rh_done, c_sum, cand_done, parts_done = [sem(n) for n in ("of_rh_done", "c_sum", "cand_done", "parts_done")]
        state_kept, y_done, y_turn_done, y_kept, y_stored = [
            sem(n) for n in ("state_kept", "y_done", "y_turn_done", "y_kept", "y_stored")]

        def where_unsettled(eng, run):
            settled = eng.value_load(g.settled[0:1, 0:1], min_val=0, max_val=1)
            with eng.If(settled == 0):
                run()
            with eng.Else():
                eng.nop()

        with nc.Block() as block:
            @block.sync
            def _(sp):
                def run():
                    sp.sem_inc(y_stored, 16 * B)
                    for c in range(3):
                        sp.dma_start(u[c][:], steps[c].rearrange("(k p) n -> p k n", p=P)).then_inc(u_loaded, 16)
                    with sp.Fori(0, CHUNKS // PER_TILE) as i, sp.Fori(0, PER_TILE) as q:
                        c = i * PER_TILE + q
                        for b in range(B):
                            sp.dma_start(share[:, :, b], shares[b * CHUNKS + c]).then_inc(share_loaded, 16)
                            sp.dma_start(x_in[:, b], g.x1_t[b * (TILES // B) + i]
                                         [:, :, bass.ds(q * CH, CH)]).then_inc(x_loaded, 16)
                        for b in range(B):
                            sp.wait_ge(y_kept, B * c + b + 1)
                            sp.dma_start(out[b, bass.ds(c * CH, CH), :], y_rows[:, b]).then_inc(y_stored, 16)
                    sp.wait_ge(y_stored, 16 * B * (CHUNKS + 1))
                where_unsettled(sp, run)

            @block.tensor
            def _(pe):
                def add(to, weights, columns):
                    for m in range(KD):
                        for k in range(KD):
                            ins = nc.tensor.matmul(to[:, :, m], weights[:, k, m * P:(m + 1) * P], columns[:, :, k],
                                                   start=k == 0, stop=k == KD - 1)
                    return ins

                def run():
                    pe.wait_ge(u_loaded, 3 * 16)
                    with pe.Fori(0, CHUNKS) as c:
                        with pe.Fori(0, CH) as t:
                            n = c * CH + t + 1
                            pe.wait_ge(h_done, n)
                            for gate in (R, Z):
                                ins = add(of_h[:, gate], u[gate], h)
                            ins.then_inc(of_h_done, 1)
                            pe.wait_ge(rh_done, n)
                            add(of_rh, u[C], rh).then_inc(of_rh_done, 1)
                        pe.wait_ge(y_done, c + 1)
                        for b in range(B):
                            if b == 1:
                                pe.wait_ge(y_kept, B * c + 1)
                            for k in range(KD):
                                ins = nc.tensor.transpose(y_turned[:, k * P:(k + 1) * P], y[:, b, k, :], g.ident[:])
                            ins.then_inc(y_turn_done, 1)
                where_unsettled(pe, run)

            @block.scalar
            def _(act):
                def run():
                    with act.Fori(0, CHUNKS) as c:
                        with act.Fori(0, CH) as t:
                            n = c * CH + t + 1
                            act.wait_ge(rz_sum, n)
                            nc.scalar.activation(gates[:], sums[:, 0:2], ACT.Sigmoid).then_inc(rz_done, 1)
                            nc.scalar.activation(keep[:], sums[:, Z], ACT.Sigmoid, scale=-1.0).then_inc(keep_done, 1)
                            act.wait_ge(c_sum, n)
                            nc.scalar.activation(cand[:], sums[:, C], ACT.Tanh).then_inc(cand_done, 1)
                        for b in range(B):
                            act.wait_ge(y_turn_done, B * c + b + 1)
                            act.wait_ge(y_stored, 16 * B * (c + 1))
                            nc.scalar.activation(y_rows[:, b], y_turned[:], ACT.Copy).then_inc(y_kept, 1)
                where_unsettled(act, run)

            @block.gpsimd
            def _(pool):
                pool.nop()

            @block.vector
            def _(dve):
                def run():
                    nc.vector.memset(h[:], 0.0).then_inc(h_done, 1)
                    with dve.Fori(0, CHUNKS) as c:
                        with dve.Fori(0, CH) as t:
                            n = c * CH + t + 1
                            at = bass.ds(t, 1)
                            dve.wait_ge(share_loaded, 16 * B * (c + 1))
                            dve.wait_ge(of_h_done, n)
                            for gate in (R, Z):
                                ins = nc.vector.tensor_tensor(sums[:, gate], of_h[:, gate],
                                                              share[:, gate, :, :, at].rearrange("p b k t -> p b (k t)"),
                                                              ALU.add)
                            ins.then_inc(rz_sum, 1)
                            dve.wait_ge(rz_done, n)
                            nc.vector.tensor_tensor(rh[:], gates[:, R], h[:], ALU.mult).then_inc(rh_done, 1)
                            dve.wait_ge(keep_done, n)
                            nc.vector.tensor_tensor(kept[:], keep[:], h[:], ALU.mult).then_inc(parts_done, 1)
                            dve.wait_ge(of_rh_done, n)
                            nc.vector.tensor_tensor(sums[:, C], of_rh[:],
                                                    share[:, C, :, :, at].rearrange("p b k t -> p b (k t)"), ALU.add
                                                    ).then_inc(c_sum, 1)
                            dve.wait_ge(cand_done, n)
                            nc.vector.tensor_tensor(gain[:], gates[:, Z], cand[:], ALU.mult).then_inc(parts_done, 1)
                            dve.wait_ge(parts_done, 2 * n)
                            nc.vector.tensor_tensor(h[:], kept[:], gain[:], ALU.add).then_inc(h_done, 1)
                            dve.wait_ge(h_done, n + 1)
                            nc.vector.tensor_copy(states[:, :, :, at].rearrange("p b k t -> p b (k t)"), h[:]
                                                  ).then_inc(state_kept, 1)
                        dve.wait_ge(state_kept, CH * (c + 1))
                        dve.wait_ge(x_loaded, 16 * B * (c + 1))
                        nc.vector.tensor_tensor(y[:], x_in[:], states[:], ALU.add).then_inc(y_done, 1)
                where_unsettled(dve, run)


def build(nc, x, cond, router_w, router_t_w, router_bias, sw1, sw3, sw2, rw1, rw2,
          w_z, u_z, c_z, b_z, w_r, u_r, c_r, b_r, w_c, u_c, c_c, b_c, out):
    g = Shared()
    dram = lambda n, s, d=F32: nc.dram_tensor(n, s, d, kind="Internal").ap()
    g.x_t, g.shared, g.x1_t = [dram(n, [TILES, P, KD, TILE]) for n in ("x_t", "shared_t", "x1_t")]
    g.shares = dram("input_shares", [TILES, PER_TILE, P, 3, KD, CH])
    g.guess = dram("first_guess", [TILES, PER_TILE, P, 2, KD, ROW], F16)
    rows4 = lambda w, j: w[j * P:(j + 1) * P, :].rearrange("p (k q) -> p k q", q=P)
    cols4 = lambda w, j: w[:, j * P:(j + 1) * P].rearrange("(k p) q -> p k q", p=P)
    n_s, n_r, per = HS // P, E * HR // P, HR // P
    up = rw1.rearrange("e h d -> (e h) d")
    down = rw2.rearrange("e (k p) (j q) -> e j p k q", p=P, q=P)
    shared_units = ([rows4(sw1, j) for j in range(n_s)] + [rows4(sw3, j) for j in range(n_s)]
                    + [cols4(sw2, j) for j in range(n_s)])
    routed_units = [rows4(up, j) for j in range(n_r)] + [down[j // per, j % per] for j in range(n_r)]
    with ExitStack() as ctx:
        sb = lambda n, s, d, to=ctx: to.enter_context(nc.sbuf_tensor(n, s, d))
        loaded_s, loaded_r = [[ctx.enter_context(nc.semaphore(f"units_{t}{i}")) for i in range(len(u) // GROUP)]
                              for t, u in (("s", shared_units), ("r", routed_units))]
        shared_stored, x1_stored = [ctx.enter_context(nc.semaphore(n)) for n in ("shared_stored", "x1_stored")]
        constants(nc, ctx, g)
        g.gate_bias = sb("gate_bias", [P, 3, KD, B], F32)
        w_first = sb("w_first", [P, KD, D], F32)
        w_first_loaded = ctx.enter_context(nc.semaphore("w_first_loaded"))
        with ExitStack() as raw_space:
            raw = sb("raw_units", [P, RAW, KD, P], F32, raw_space)
            tokens(nc, g, x, cond, router_w, router_t_w, router_bias, (c_r, c_z, c_c), (b_r, b_z, b_c),
                   lambda eng: load_units(eng, raw, shared_units[:RAW], 0, loaded_s))
            with ExitStack() as weights:
                hi, lo = [sb(f"shared_{s}", [P, len(shared_units), D], F32R, weights) for s in ("hi", "lo")]
                plain = sb("plain", [P, PLAIN, TILE], F32, weights)
                first = first_tile(nc, weights, plain, "_s")
                turned_weights(nc, g, raw, shared_units, loaded_s, hi, lo, first, None, "_s")
                experts(nc, g, hi, lo, plain, first, n_s, True, shared_stored,
                        lambda eng: load_units(eng, raw, routed_units[:RAW], 0, loaded_r), "_s")
            with ExitStack() as weights:
                hi, lo = [sb(f"routed_{s}", [P, len(routed_units), D], F32R, weights) for s in ("hi", "lo")]
                plain = raw[:].rearrange("p u k q -> p u (k q)")
                first = first_tile(nc, weights, plain, "_r")
                turned_weights(nc, g, raw, routed_units, loaded_r, hi, lo, first, shared_stored, "_r")
                experts(nc, g, hi, lo, plain, first, n_r, False, x1_stored,
                        lambda eng: eng.dma_start(w_first[:], w_r.rearrange("(k p) n -> p k n", p=P)
                                                  ).then_inc(w_first_loaded, 16), "_r")
        g.u_hi, g.u_lo = [sb(f"u_{s}", [P, 3, KD, D], F16) for s in ("hi", "lo")]
        g.left = sb("left", [P, CHECKS, B, CHUNKS], F32)
        g.settled = sb("settled", [1, 1], I32)
        with ExitStack() as weights:
            g.w_hi, g.w_lo = [sb(f"w_{s}", [P, 3, KD, D], F32R, weights) for s in ("hi", "lo")]
            input_shares(nc, g, w_first, w_first_loaded, (w_r, w_z, w_c), (u_r, u_z, u_c), x1_stored)
        gru(nc, g, out)
        all_settled(nc, g)
        step_by_step(nc, g, (u_r, u_z, u_c), out)


_INS = ['x', 'cond_1024', 'L0_cond_router_w', 'L0_cond_router_t_w', 'L0_cond_router_bias', 'L0_cond_sw1',
        'L0_cond_sw3', 'L0_cond_sw2', 'L0_cond_rw1', 'L0_cond_rw2', 'L1_cond_W_z', 'L1_cond_U_z', 'L1_cond_C_z',
        'L1_cond_b_z', 'L1_cond_W_r', 'L1_cond_U_r', 'L1_cond_C_r', 'L1_cond_b_r', 'L1_cond_W', 'L1_cond_U',
        'L1_cond_C', 'L1_cond_b']
_OUTS = [((2, 2048, 512), 'float32')]


def kernel(**inputs):
    import numpy as _np
    import concourse.bacc as _bacc
    from concourse import mybir as _mybir
    from concourse.bass_utils import run_bass_kernel_spmd as _run

    nc = _bacc.Bacc("TRN2", target_bir_lowering=False, num_devices=1)
    arrays, args = {}, []
    for name in _INS:
        a = _np.ascontiguousarray(inputs[name])
        arrays[f"in_{name}_dram"] = a
        args.append(nc.dram_tensor(f"in_{name}_dram", a.shape, _mybir.dt.from_np(a.dtype), kind="ExternalInput").ap())
    for i, (shape, dtype) in enumerate(_OUTS):
        dt = _mybir.dt.from_np(_np.dtype(dtype))
        args.append(nc.dram_tensor(f"out_{i}_dram", shape, dt, kind="ExternalOutput").ap())
    build(nc, *args)
    r = _run(nc, [arrays], core_ids=[0])
    return r.results[0]["out_0_dram"]
```
